# Optimizing a Trainium2 kernel written in Bass

```python
import numpy as np
import jax
import jax.numpy as jnp

def _softmax(x, axis=-1):
    return jax.nn.softmax(x, axis=axis)

def _gelu(x):
    return jax.nn.gelu(x, approximate=True)

def _silu(x):
    return jax.nn.silu(x)

def _sigmoid(x):
    return jax.nn.sigmoid(x)

def _layernorm(x, axis=-1, eps=1e-05):
    m = jnp.mean(x, axis=axis, keepdims=True)
    v = jnp.var(x, axis=axis, keepdims=True)
    return (x - m) / jnp.sqrt(v + eps)

def _scatter_add(tgt, idx, src, axis=0):
    return tgt.at[idx].add(src)

def _segment_sum(src, seg, n):
    return jax.ops.segment_sum(src, seg, n)
kernel_name = 'mk_adj_seq_d4_adj_r2_f11c2a'

def setup_inputs(seed: int=0):
    np.random.seed(seed)
    _w = jnp.asarray

    def _rec_inputs():
        import jax
        import jax.numpy as jnp
        _gk = jax.random.key(seed)
        x = -0.0002928 + 1 * jax.random.normal(jax.random.fold_in(_gk, 1), (128, 128, 256), jnp.float32)
        _w = (1.0 + jnp.arange(128, dtype=jnp.float32)) ** (-0.5)
        _w = _w / _w.mean()
        _pij = jnp.clip(0.125 * _w[:, None] * _w[None, :], 0.0, 1.0)
        _a = jax.random.uniform(jax.random.fold_in(_gk, 2), (128, 128, 128)) < _pij
        _a = jnp.logical_or(_a, jnp.swapaxes(_a, -1, -2))
        _a = jnp.logical_or(_a, jnp.eye(128, dtype=bool))
        _af = _a.astype(jnp.float32)
        _af = _af / jnp.maximum(_af.sum(-1, keepdims=True), 1.0)
        adj = _af
        return (x, adj)
    x, adj = _rec_inputs()

    def _L0_gnn_setup():
        import jax, jax.numpy as jnp
        import numpy as np
        B, N, D, H = (8, 512, 256, 8)
        DK = D // H
        LN_EPS = 1e-05
        ADJ_MIN = 1e-08

        def _layer_norm(x, gamma, beta):
            mu = jnp.mean(x, axis=-1, keepdims=True)
            var = jnp.mean(jnp.square(x - mu), axis=-1, keepdims=True)
            return (x - mu) * jax.lax.rsqrt(var + LN_EPS) * gamma + beta
        key = jax.random.key(seed)
        ks = jax.random.split(key, 12)
        x = jax.random.normal(ks[0], (B, N, D), dtype=jnp.float32)
        adj = jax.random.uniform(ks[1], (B, N, N), dtype=jnp.float32)
        adj = adj / jnp.sum(adj, axis=-1, keepdims=True)
        s = 1.0 / np.sqrt(D)
        Wq = jax.random.normal(ks[2], (D, D), dtype=jnp.float32) * s
        bq = jnp.zeros((D,), dtype=jnp.float32)
        Wk = jax.random.normal(ks[3], (D, D), dtype=jnp.float32) * s
        bk = jnp.zeros((D,), dtype=jnp.float32)
        Wv = jax.random.normal(ks[4], (D, D), dtype=jnp.float32) * s
        bv = jnp.zeros((D,), dtype=jnp.float32)
        Wo = jax.random.normal(ks[5], (D, D), dtype=jnp.float32) * s
        bo = jnp.zeros((D,), dtype=jnp.float32)
        gamma = jnp.ones((D,), dtype=jnp.float32)
        beta = jnp.zeros((D,), dtype=jnp.float32)
        return {'x': x, 'adj': adj, 'Wq': Wq, 'bq': bq, 'Wk': Wk, 'bk': bk, 'Wv': Wv, 'bv': bv, 'Wo': Wo, 'bo': bo, 'gamma': gamma, 'beta': beta}
    _L0_gnn_all = _L0_gnn_setup()
    _L0_gnn_in = {k: v for k, v in _L0_gnn_all.items() if k in ('Wq', 'bq', 'Wk', 'bk', 'Wv', 'bv', 'Wo', 'bo', 'gamma', 'beta')}
    del _L0_gnn_all

    def _L1_gnn_setup():
        import jax, jax.numpy as jnp
        import numpy as np
        import math
        EMBED = 256
        DFF = 256
        B, N = (8, 1024)
        key = jax.random.key(seed)
        ks = jax.random.split(key, 8)
        node_fts = jax.random.normal(ks[0], (B, N, EMBED), dtype=jnp.float32)
        rel_edges = jax.random.randint(ks[1], (B, N, N), 0, 2).astype(jnp.float32)
        s = 1.0 / math.sqrt(EMBED)
        Wq = jax.random.normal(ks[2], (EMBED, DFF), dtype=jnp.float32) * s
        bq = jnp.zeros((DFF,), dtype=jnp.float32)
        Wk = jax.random.normal(ks[3], (EMBED, DFF), dtype=jnp.float32) * s
        bk = jnp.zeros((DFF,), dtype=jnp.float32)
        Wc = jax.random.normal(ks[4], (EMBED, EMBED), dtype=jnp.float32) * s
        gamma = jnp.ones((EMBED,), dtype=jnp.float32)
        beta = jnp.zeros((EMBED,), dtype=jnp.float32)
        return {'node_fts': node_fts, 'rel_edges': rel_edges, 'Wq': Wq, 'bq': bq, 'Wk': Wk, 'bk': bk, 'Wc': Wc, 'gamma': gamma, 'beta': beta}
    _L1_gnn_all = _L1_gnn_setup()
    _L1_gnn_in = {k: v for k, v in _L1_gnn_all.items() if k in ('Wq', 'bq', 'Wk', 'bk', 'Wc', 'gamma', 'beta')}
    del _L1_gnn_all

    def _L2_gnn_setup():
        import jax, jax.numpy as jnp
        import numpy as np
        NUM_HEADS = 8
        EPS = 1e-09
        key = jax.random.key(seed)
        ks = jax.random.split(key, 8)
        B, N, D = (2, 1024, 256)
        s = 1.0 / np.sqrt(D)
        x = jax.random.normal(ks[0], (B, N, D), dtype=jnp.float32)
        adjacency = jax.random.uniform(ks[1], (B, N, N), dtype=jnp.float32)
        W_q = jax.random.normal(ks[2], (D, D), dtype=jnp.float32) * s
        W_k = jax.random.normal(ks[3], (D, D), dtype=jnp.float32) * s
        W_v = jax.random.normal(ks[4], (D, D), dtype=jnp.float32) * s
        b_q = jnp.zeros((D,), jnp.float32)
        b_k = jnp.zeros((D,), jnp.float32)
        b_v = jnp.zeros((D,), jnp.float32)
        w_g = jax.random.normal(ks[5], (2 * D,), dtype=jnp.float32) * (1.0 / np.sqrt(2 * D))
        b_g = jnp.zeros((), jnp.float32)
        return {'x': x, 'adjacency': adjacency, 'W_q': W_q, 'b_q': b_q, 'W_k': W_k, 'b_k': b_k, 'W_v': W_v, 'b_v': b_v, 'w_g': w_g, 'b_g': b_g}
    _L2_gnn_all = _L2_gnn_setup()
    _L2_gnn_in = {k: v for k, v in _L2_gnn_all.items() if k in ('W_q', 'b_q', 'W_k', 'b_k', 'W_v', 'b_v', 'w_g', 'b_g')}
    del _L2_gnn_all

    def _L3_gnn_setup():
        import jax, jax.numpy as jnp
        import numpy as np
        BS, N, H = (8, 1024, 256)
        NEG_INF = -1000000000.0
        LEAKY_SLOPE = 0.01
        key = jax.random.key(seed)
        ks = jax.random.split(key, 8)
        feats = jax.random.normal(ks[0], (BS, N, H), dtype=jnp.float32)
        adj = jax.random.randint(ks[1], (BS, N, N), 0, 2).astype(jnp.float32)
        adj = jnp.maximum(adj, jnp.eye(N, dtype=jnp.float32)[None])
        s = 1.0 / np.sqrt(H)
        return {'feats': feats, 'adj_mat': adj, 'fc_w': jax.random.normal(ks[2], (H, H), dtype=jnp.float32) * s, 'fc_b': jax.random.normal(ks[3], (H,), dtype=jnp.float32) * s, 'q_w': jax.random.normal(ks[4], (1, H), dtype=jnp.float32) * s, 'q_b': jax.random.normal(ks[5], (1,), dtype=jnp.float32) * s, 'k_w': jax.random.normal(ks[6], (1, H), dtype=jnp.float32) * s, 'k_b': jax.random.normal(ks[7], (1,), dtype=jnp.float32) * s}
    _L3_gnn_all = _L3_gnn_setup()
    _L3_gnn_in = {k: v for k, v in _L3_gnn_all.items() if k in ('fc_w', 'fc_b', 'q_w', 'q_b', 'k_w', 'k_b')}
    del _L3_gnn_all
    return {'x': x, 'adj': adj, 'L0_gnn_Wq': _L0_gnn_in['Wq'], 'L0_gnn_bq': _L0_gnn_in['bq'], 'L0_gnn_Wk': _L0_gnn_in['Wk'], 'L0_gnn_bk': _L0_gnn_in['bk'], 'L0_gnn_Wv': _L0_gnn_in['Wv'], 'L0_gnn_bv': _L0_gnn_in['bv'], 'L0_gnn_Wo': _L0_gnn_in['Wo'], 'L0_gnn_bo': _L0_gnn_in['bo'], 'L0_gnn_gamma': _L0_gnn_in['gamma'], 'L0_gnn_beta': _L0_gnn_in['beta'], 'L1_gnn_Wq': _L1_gnn_in['Wq'], 'L1_gnn_bq': _L1_gnn_in['bq'], 'L1_gnn_Wk': _L1_gnn_in['Wk'], 'L1_gnn_bk': _L1_gnn_in['bk'], 'L1_gnn_Wc': _L1_gnn_in['Wc'], 'L1_gnn_gamma': _L1_gnn_in['gamma'], 'L1_gnn_beta': _L1_gnn_in['beta'], 'L2_gnn_W_q': _L2_gnn_in['W_q'], 'L2_gnn_b_q': _L2_gnn_in['b_q'], 'L2_gnn_W_k': _L2_gnn_in['W_k'], 'L2_gnn_b_k': _L2_gnn_in['b_k'], 'L2_gnn_W_v': _L2_gnn_in['W_v'], 'L2_gnn_b_v': _L2_gnn_in['b_v'], 'L2_gnn_w_g': _L2_gnn_in['w_g'], 'L2_gnn_b_g': _L2_gnn_in['b_g'], 'L3_gnn_fc_w': _L3_gnn_in['fc_w'], 'L3_gnn_fc_b': _L3_gnn_in['fc_b'], 'L3_gnn_q_w': _L3_gnn_in['q_w'], 'L3_gnn_q_b': _L3_gnn_in['q_b'], 'L3_gnn_k_w': _L3_gnn_in['k_w'], 'L3_gnn_k_b': _L3_gnn_in['k_b']}

def reference(x, adj, L0_gnn_Wq, L0_gnn_bq, L0_gnn_Wk, L0_gnn_bk, L0_gnn_Wv, L0_gnn_bv, L0_gnn_Wo, L0_gnn_bo, L0_gnn_gamma, L0_gnn_beta, L1_gnn_Wq, L1_gnn_bq, L1_gnn_Wk, L1_gnn_bk, L1_gnn_Wc, L1_gnn_gamma, L1_gnn_beta, L2_gnn_W_q, L2_gnn_b_q, L2_gnn_W_k, L2_gnn_b_k, L2_gnn_W_v, L2_gnn_b_v, L2_gnn_w_g, L2_gnn_b_g, L3_gnn_fc_w, L3_gnn_fc_b, L3_gnn_q_w, L3_gnn_q_b, L3_gnn_k_w, L3_gnn_k_b):
    import jax
    import jax.numpy as jnp

    def _L0_gnn_ref(x, adj, Wq, bq, Wk, bk, Wv, bv, Wo, bo, gamma, beta):
        import jax, jax.numpy as jnp
        import numpy as np
        B, N, D, H = (8, 512, 256, 8)
        DK = D // H
        LN_EPS = 1e-05
        ADJ_MIN = 1e-08

        def _layer_norm(x, gamma, beta):
            mu = jnp.mean(x, axis=-1, keepdims=True)
            var = jnp.mean(jnp.square(x - mu), axis=-1, keepdims=True)
            return (x - mu) * jax.lax.rsqrt(var + LN_EPS) * gamma + beta
        b, n, d = x.shape
        q = (x @ Wq.T + bq).reshape(b, n, H, DK).transpose(0, 2, 1, 3)
        k = (x @ Wk.T + bk).reshape(b, n, H, DK).transpose(0, 2, 1, 3)
        v = (x @ Wv.T + bv).reshape(b, n, H, DK).transpose(0, 2, 1, 3)
        logits = jnp.einsum('bhqd,bhkd->bhqk', q, k) / np.sqrt(DK)
        logits = logits + jnp.log(jnp.clip(adj, ADJ_MIN, None))[:, None, :, :]
        attn = jax.nn.softmax(logits, axis=-1)
        out = jnp.einsum('bhqk,bhkd->bhqd', attn, v)
        out = out.transpose(0, 2, 1, 3).reshape(b, n, d)
        out = out @ Wo.T + bo
        return _layer_norm(x + out, gamma, beta)

    def _L1_gnn_ref(node_fts, rel_edges, Wq, bq, Wk, bk, Wc, gamma, beta):
        import jax, jax.numpy as jnp
        import numpy as np
        import math
        EMBED = 256
        DFF = 256
        B, N = (8, 1024)
        denom = math.sqrt(DFF)
        q = node_fts @ Wq + bq
        k = node_fts @ Wk + bk
        scores = jnp.einsum('bod,bid->boi', q, k) / denom
        mask = rel_edges == 0
        scores = jnp.where(mask, -1e+18, scores)
        attn = jax.nn.softmax(scores, axis=2)
        attn = jnp.where(mask, 0.0, attn)
        ctx = jnp.einsum('boi,bie->boe', attn, node_fts) @ Wc
        x = node_fts + ctx
        mu = jnp.mean(x, axis=-1, keepdims=True)
        var = jnp.mean(jnp.square(x - mu), axis=-1, keepdims=True)
        out = (x - mu) * jax.lax.rsqrt(var + 1e-05) * gamma + beta
        return out

    def _L2_gnn_ref(x, adjacency, W_q, b_q, W_k, b_k, W_v, b_v, w_g, b_g):
        import jax, jax.numpy as jnp
        import numpy as np
        NUM_HEADS = 8
        EPS = 1e-09
        B, N, D = x.shape
        H = NUM_HEADS
        hd = D // H
        Q = (x @ W_q + b_q).reshape(B, N, H, hd)
        K = (x @ W_k + b_k).reshape(B, N, H, hd)
        V = (x @ W_v + b_v).reshape(B, N, H, hd)
        scores = jnp.einsum('bihd,bjhd->bhij', Q, K) / jnp.sqrt(jnp.float32(hd))
        a = x @ w_g[:D]
        c = x @ w_g[D:]
        soul_bias = a[:, :, None] + c[:, None, :] + b_g
        scores = scores + (soul_bias + jnp.log(adjacency + EPS))[:, None, :, :]
        attn = jax.nn.softmax(scores, axis=-1)
        out = jnp.einsum('bhij,bjhd->bihd', attn, V).reshape(B, N, D)
        return out + x

    def _L3_gnn_ref(feats, adj_mat, fc_w, fc_b, q_w, q_b, k_w, k_b):
        import jax, jax.numpy as jnp
        import numpy as np
        BS, N, H = (8, 1024, 256)
        NEG_INF = -1000000000.0
        LEAKY_SLOPE = 0.01
        feat_proj = jnp.einsum('bnh,oh->bno', feats, fc_w) + fc_b
        q = jnp.einsum('bnh,oh->bno', feat_proj, q_w) + q_b
        k = jnp.einsum('bnh,oh->bno', feat_proj, k_w) + k_b
        logits = q + jnp.swapaxes(k, 2, 1)
        masked = logits + (1.0 - adj_mat) * NEG_INF
        masked = jnp.where(masked >= 0, masked, LEAKY_SLOPE * masked)
        atten = jax.nn.softmax(masked, axis=-1)
        out = jnp.einsum('bnm,bmh->bnh', atten, feat_proj)
        return out + feats
    x = _L0_gnn_ref(x, adj, L0_gnn_Wq, L0_gnn_bq, L0_gnn_Wk, L0_gnn_bk, L0_gnn_Wv, L0_gnn_bv, L0_gnn_Wo, L0_gnn_bo, L0_gnn_gamma, L0_gnn_beta)
    x = _L1_gnn_ref(x, adj, L1_gnn_Wq, L1_gnn_bq, L1_gnn_Wk, L1_gnn_bk, L1_gnn_Wc, L1_gnn_gamma, L1_gnn_beta)
    x = _L2_gnn_ref(x, adj, L2_gnn_W_q, L2_gnn_b_q, L2_gnn_W_k, L2_gnn_b_k, L2_gnn_W_v, L2_gnn_b_v, L2_gnn_w_g, L2_gnn_b_g)
    x = _L3_gnn_ref(x, adj, L3_gnn_fc_w, L3_gnn_fc_b, L3_gnn_q_w, L3_gnn_q_b, L3_gnn_k_w, L3_gnn_k_b)
    return x

_drawn_inputs = setup_inputs


def setup_inputs(seed=0):
    import zlib

    import numpy as np

    out = dict(_drawn_inputs(seed))
    spreads = {'L0_gnn_bq': (0.0, 0.1),
     'L0_gnn_bk': (0.0, 0.8),
     'L0_gnn_bv': (0.0, 0.1),
     'L0_gnn_bo': (0.0, 0.1),
     'L0_gnn_gamma': (1.0, 0.2),
     'L0_gnn_beta': (0.0, 0.1),
     'L1_gnn_bq': (0.0, 0.324),
     'L1_gnn_bk': (0.0, 0.8),
     'L1_gnn_gamma': (1.0, 0.2),
     'L1_gnn_beta': (0.0, 0.1),
     'L2_gnn_b_q': (0.0, 0.364),
     'L2_gnn_b_k': (0.0, 0.8),
     'L2_gnn_b_v': (0.0, 0.1)}
    factors = {'L3_gnn_q_w': 4.062, 'L3_gnn_k_w': 3.11}
    for name, (base, spread) in spreads.items():
        noise = np.random.default_rng([zlib.crc32(name.encode()), seed]).standard_normal(out[name].shape)
        drawn = base * np.exp(spread * noise) if base else spread * noise
        out[name] = jnp.asarray(drawn.astype(out[name].dtype))
    for name, factor in factors.items():
        out[name] = (out[name] * factor).astype(out[name].dtype)
    return out
```

```python
from contextlib import ExitStack

import concourse.bass as bass
from concourse import mybir

P = 128
D = 256
C = D // P
G = 2
H = 8
HD = D // H
R = P // HD
SLOTS = 8
LN_EPS = 1e-5
MASKED = -1.0e30
HUGE = 3.0e38

ALU = mybir.AluOpType
ACT = mybir.ActivationFunctionType
F32 = mybir.dt.float32
F32R = mybir.dt.float32r
AX_X = mybir.AxisListType.X

FIRST, LAST_EXTRA = -1, 3


def build(nc, x, adj, w, out):
    NP_ = x.shape[0] // G

    x_dram = x.rearrange("(u g) t d -> t u g d", g=G)
    adj_dram = adj.rearrange("(u g) q k -> q u g k", g=G)
    out_dram = out.rearrange("(u g) t d -> t u g d", g=G)

    with ExitStack() as ctx:
        def sb(name, *shape, dt=F32):
            return ctx.enter_context(nc.sbuf_tensor(name, [P, *shape], dt))

        def sem(name):
            return ctx.enter_context(nc.semaphore(name))

        def sems(*names):
            return [sem(n) for n in names]

        class Split:
            def __init__(self, name, *shape):
                self.hi = sb(name + "_hi", *shape, dt=F32R)
                self.lo = sb(name + "_lo", *shape, dt=F32R)

        score_ps = ctx.enter_context(nc.psum_tensor("score_ps", [P, G * C, R * P], F32))
        work = ctx.enter_context(nc.psum_tensor("work", [P, 4, 512], F32))

        wq0, wk0, wv0, wo0 = (Split(n, C, D) for n in ("wq0", "wk0", "wv0", "wo0"))
        wqk1 = Split("wqk1", C, D)
        wc1 = Split("wc1", C, D)
        wq2, wk2 = Split("wq2", C, D), Split("wk2", C, D)
        wv2 = Split("wv2", C, D + 2)
        wf3 = Split("wf3", C, D + 2)
        ident = sb("ident", P)
        ROWS = ("bv0", "bo0", "gamma0", "beta0", "gamma1", "beta1", "bv2", "bf3")
        row = {n: sb(n, D) for n in ROWS}
        wu1 = sb("wu1", D)
        COLUMNS = ("bq0", "bk0", "bq1", "bk1", "bq2", "bk2", "bf3")
        N_COL = C * len(COLUMNS) + 4 * C
        col_rows = sb("col_rows", P)
        cols = sb("cols", N_COL)
        bq0, bk0, bq1, bk1, bq2, bk2, bf3c = (cols[:, C * j:C * (j + 1)] for j in range(len(COLUMNS)))
        pairs_of = cols[:, C * len(COLUMNS):].rearrange("p (n c j) -> p n c j", n=2, c=C)
        qk3, wg2 = pairs_of[:, 0], pairs_of[:, 1]
        bq0s, bq2s = sb("bq0s", C), sb("bq2s", C)
        c1 = sb("c1", C)
        c0 = sb("c0", 1)
        bg2 = sb("bg2", 2)
        bqk3 = sb("bqk3", 2)
        add3 = sb("add3", 2)
        eps2 = sb("eps2", 1)
        count_only = sb("count_only", 16)
        half = sb("half", G)

        adjs = sb("adjs", SLOTS, G * P)
        X0, X0b = sb("X0", G, D), sb("X0b", G, D)
        X1, X2, X3 = sb("X1", G, D), sb("X2", G, D), sb("X3", G, D)
        OUT = sb("OUT", G, D)
        XT = [Split(f"XT{l}", C, G * P) for l in range(4)]
        X1T = sb("X1T", C, G * P)
        QT = {l: sb(f"QT{l}", C, G * P) for l in (0, 2)}
        KT = {l: sb(f"KT{l}", C, G * P) for l in (0, 2)}
        KD = {l: sb(f"KD{l}", G * C, R * P) for l in (0, 2)}
        V = {l: sb(f"V{l}", G, D) for l in (0, 2)}
        E = {l: sb(f"E{l}", G, H, P) for l in (0, 2)}
        ET = {l: sb(f"ET{l}", G, H, P) for l in (0, 2)}
        NM = {l: sb(f"NM{l}", G * H) for l in (0, 2)}
        SUM = {l: sb(f"SUM{l}", G * H) for l in (0, 2)}
        RS = {l: sb(f"RS{l}", G * H) for l in (0, 2)}
        BIAS0, LNADJ2, BIAS2 = sb("BIAS0", G * P), sb("LNADJ2", G * P), sb("BIAS2", G * P)
        OT0 = Split("OT0", C, G * P)
        OT2 = sb("OT2", C, G * P)
        Y = {l: sb(f"Y{l}", G, D) for l in (0, 1)}
        STAT = {l: sb(f"STAT{l}", G, 6) for l in (0, 1)}
        MV = {l: sb(f"MV{l}", G, 2) for l in (0, 1)}
        VE = {l: sb(f"VE{l}", G) for l in (0, 1)}
        RSTD = {l: sb(f"RSTD{l}", G) for l in (0, 1)}
        G1 = sb("G1", C, G * P)
        MASK1, BIAS1 = sb("MASK1", G * P), sb("BIAS1", G * P)
        U1, U1junk = sb("U1", G), sb("U1junk", G, D)
        E1, A1, A1T = sb("E1", G * P), sb("A1", G * P), sb("A1T", G * P)
        NM1, SUM1, RS1 = sb("NM1", G), sb("SUM1", G), sb("RS1", G)
        CT1 = Split("CT1", C, G * P)
        AC2 = sb("AC2", G, 2)
        F3 = sb("F3", G, D)
        QK3 = sb("QK3", G, 2)
        M3a, M3 = sb("M3a", G * P), sb("M3", G * P)
        U3, L3, E3, E3T = sb("U3", G * P), sb("L3", G * P), sb("E3", G * P), sb("E3T", G * P)
        NM3, SUM3, RS3 = sb("NM3", G), sb("SUM3", G), sb("RS3", G)
        stage = {n: t for n, t in zip(
            ("Wq0", "Wk0", "Wv0", "Wo0"),
            (ET[2].rearrange("p g h k -> p (g h k)")[:, j * 512:(j + 1) * 512].rearrange("p (c d) -> p c d", c=C)
             for j in range(4)))}
        stage.update({n: t for n, t in zip(
            ("Wq1", "Wk1", "Wc1", "fc3"),
            (E[2].rearrange("p g h k -> p (g h k)")[:, j * 512:(j + 1) * 512].rearrange("p (c d) -> p c d", c=C)
             for j in range(4)))})
        stage.update({n: t for n, t in zip(
            ("Wq2", "Wk2", "Wv2"),
            (ET[0].rearrange("p g h k -> p (g h k)")[:, j * 512:(j + 1) * 512].rearrange("p (c d) -> p c d", c=C)
             for j in range(3)))})
        wqT1 = E[0].rearrange("p g h k -> p (g h k)")[:, 0:512].rearrange("p (c d) -> p c d", c=C)
        wkT1 = E[0].rearrange("p g h k -> p (g h k)")[:, 512:1024].rearrange("p (c d) -> p c d", c=C)
        w_in = {n: sem("in_" + n) for n in stage}
        small_in = sem("small_in")
        pool_const, const_ready, dve_const = sems("pool_const", "const_ready", "dve_const")
        prep_pe, prep_hi, prep_lo, prep_plain = sems("prep_pe", "prep_hi", "prep_lo", "prep_plain")
        x_in, adj_in, out_stored = sems("x_in", "adj_in", "out_stored")
        xt_ps = sems("xt0_ps", "xt1_ps", "xt2_ps", "xt3_ps")
        q_ps = {0: sem("q0_ps"), 2: sem("q2_ps")}
        k_ps = {0: sem("k0_ps"), 2: sem("k2_ps")}
        v0_ps = sem("v0_ps")
        v2_ps = sems("v2a_ps", "v2b_ps")
        s_ps = {0: sems("s0a_ps", "s0b_ps"), 2: sems("s2a_ps", "s2b_ps")}
        et_ps = {0: sems("et0a_ps", "et0b_ps"), 2: sems("et2a_ps", "et2b_ps")}
        ot_ps = {0: sem("ot0_ps"), 2: sem("ot2_ps")}
        y0_ps, g1_ps, s1_ps, a1t_ps, ct1_ps, y1_ps = sems("y0_ps", "g1_ps", "s1_ps", "a1t_ps", "ct1_ps", "y1_ps")
        c2_ps, o2_ps, f3a_ps, f3b_ps, k3_ps, e3t_ps, o3_ps = sems(
            "c2_ps", "o2_ps", "f3a_ps", "f3b_ps", "k3_ps", "e3t_ps", "o3_ps")
        xt_hi = sems("xt0_hi", "xt1_hi", "xt2_hi", "xt3_hi")
        x1t_sb = sem("x1t_sb")
        q_sb = {0: sem("q0_sb"), 2: sem("q2_sb")}
        exp_half = {0: sems("exp0a", "exp0b"), 2: sems("exp2a", "exp2b")}
        et_sb = {0: sems("et0a_sb", "et0b_sb"), 2: sems("et2a_sb", "et2b_sb")}
        ot0_hi, ot2_sb, bias0_sb, lnadj2_sb, exp1, exp3, a1t_sb, e3t_sb, ct1_hi = sems(
            "ot0_hi", "ot2_sb", "bias0_sb", "lnadj2_sb", "exp1", "exp3", "a1t_sb", "e3t_sb", "ct1_hi")
        xt_lo = sems("xt0_lo", "xt1_lo", "xt2_lo", "xt3_lo")
        k_sb = {0: sem("k0_sb"), 2: sem("k2_sb")}
        keys_spread = {0: sem("keys0_spread"), 2: sem("keys2_spread")}
        v0_sb, clip0, x3_sb, u1_sb, g1_sb = sems("v0_sb", "clip0", "x3_sb", "u1_sb", "g1_sb")
        t_first = {0: sems("t0a_first", "t0b_first"), 2: sems("t2a_first", "t2b_first")}
        t_all = {0: sems("t0a_all", "t0b_all"), 2: sems("t2a_all", "t2b_all")}
        rs_sb = {0: sems("rs0a", "rs0b"), 2: sems("rs2a", "rs2b")}
        v2_sb = sems("v2a_sb", "v2b_sb")
        f3_sb = sems("f3a_sb", "f3b_sb")
        mask1_sb, nbias1_sb, bias1_sb, t1_all, rs1_sb, a1_sb = sems(
            "mask1_sb", "nbias1_sb", "bias1_sb", "t1_all", "rs1_sb", "a1_sb")
        bias2_sb, ot0_lo, ct1_lo, m3a_sb, u3_sb, l3_sb, nm3_sb, rs3_sb, out_sb = sems(
            "bias2_sb", "ot0_lo", "ct1_lo", "m3a_sb", "u3_sb", "l3_sb", "nm3_sb", "rs3_sb", "out_sb")
        y_sb, stat_sb, mv_sb, z_sb = ({l: sem(f"{n}{l}") for l in (0, 1)} for n in ("y_sb", "stat_sb", "mv_sb", "z_sb"))
        x0b_sb, x1_sb, x2_sb, m3_sb = sems("x0b_sb", "x1_sb", "x2_sb", "m3_sb")
        prob = {0: sems("prob0a", "prob0b"), 2: sems("prob2a", "prob2b")}
        ve_sb, rstd_sb, zg_sb = ({l: sem(f"{n}{l}") for l in (0, 1)} for n in ("ve_sb", "rstd_sb", "zg_sb"))

        bank_users = {
            0: [(3, [xt_hi[3], xt_lo[3]]), (3, [f3_sb[1]]), (2, [v2_sb[0]]), (3, [u3_sb]), (1, [a1t_sb]),
                (-1, [v0_sb]), (3, [out_sb])],
            1: [(3, [x3_sb]), (1, [g1_sb]), (2, [q_sb[2]]), (2, [v2_sb[1]]), (2, [bias2_sb]), (-1, [q_sb[0]]),
                (3, [e3t_sb])],
            2: [(3, [f3_sb[0]]), (0, [ot0_hi, ot0_lo]), (-1, [xt_hi[0], xt_lo[0]]), (1, [ct1_hi, ct1_lo]),
                (2, [ot2_sb])],
            3: [(1, [x1t_sb]), (2, [xt_hi[2], xt_lo[2]]), (2, [k_sb[2]]), (1, [t1_all]), (0, [y_sb[0]]),
                (-1, [k_sb[0]]), (1, [y_sb[1]])],
            "scores": [(0, et_sb[0]), (2, et_sb[2])],
        }

        SC = HD ** -0.5
        SC1 = D ** -0.5

        class Turn:
            def __init__(self, eng, i, multiples):
                self.eng, self.i, self.fixed = eng, i, isinstance(i, int)
                if not self.fixed:
                    for n in range(-3, 3):
                        eng.to_reg(self.count(n))
                    for n, by in multiples:
                        eng.to_reg(self.count(n) * by)

            def has(self, off):
                return not self.fixed or 0 <= self.i - off < NP_

            def count(self, n):
                return min(max(self.i + n, 0), NP_) if self.fixed else self.i + n

            def now(self, off):
                return self.count(1 - off)

            def was(self, off):
                return self.count(-off)

            def wait(self, s, n, by=1):
                if self.fixed and n <= 0:
                    return
                self.eng.wait_ge(s, n * by)

            def first_and_last(self, bank, n):
                if self.fixed:
                    for k, (off, read) in enumerate(bank_users[bank]):
                        for s in read:
                            self.wait(s, self.now(off) if k < n else self.was(off))

            def apart(self):
                if not self.fixed:
                    self.eng.wait_ge(const_ready, 1)

            def slot(self, off):
                k = (self.i - off) % SLOTS
                return adjs[:, k, :] if self.fixed else adjs[:, bass.ds(k, 1), :].rearrange("p a k -> p (a k)")

        def run(eng, turn, multiples=()):
            for i in range(FIRST, LAST_EXTRA + 1):
                turn(Turn(eng, i, multiples))
            with eng.Fori(LAST_EXTRA + 1, NP_ - 2) as i:
                turn(Turn(eng, i, multiples))
            for i in range(NP_ - 2, NP_ + LAST_EXTRA):
                turn(Turn(eng, i, multiples))

        TURNED = ["Wq0", "Wk0", "Wv0", "Wo0", "fc3", "Wq1", "Wk1"]
        STEPS = ["cols"] + TURNED + ["wqk1", "rows1", "cols3"]
        SPLIT_OF = {"Wq0": wq0, "Wk0": wk0, "Wv0": wv0, "Wo0": wo0, "fc3": wf3}
        NATURAL = [("Wc1", wc1), ("Wq2", wq2), ("Wk2", wk2), ("Wv2", wv2)]
        N_SMALL = len(ROWS) + len(COLUMNS) + 4 * C + 3

        block = ctx.enter_context(nc.Block())

        @block.sync
        def _(sp):
            sp.dma_start(X0[:], x_dram[:, 0]).then_inc(x_in, 16)
            sp.dma_start(adjs[:, 0, :].rearrange("p (g k) -> p g k", g=G), adj_dram[:, 0]).then_inc(adj_in, 16)
            for n in ("Wq0", "Wv0", "fc3", "Wk1", "Wq2", "Wv2"):
                sp.dma_start(stage[n], w[n].rearrange("(c p) d -> p c d", p=P)).then_inc(w_in[n], 16)
            for n in ROWS:
                sp.dma_start(row[n][:], w[n].rearrange("(a d) -> a d", a=1).to_broadcast([P, D])).then_inc(small_in, 16)

            sp.wait_ge(dve_const, 1)

            def spread(l, t, off):
                t.apart()
                t.wait(k_sb[l], t.now(off))
                t.wait(s_ps[l][1], t.was(off))
                for r in range(R):
                    q = slice(r * HD, (r + 1) * HD)
                    sp.dma_start(KD[l][q, :, r * P:(r + 1) * P],
                                 KT[l][q].rearrange("p c (g k) -> p (c g) k", g=G)).then_inc(keys_spread[l], 16)

            def turn(t):
                if t.has(2):
                    spread(2, t, 2)
                if t.has(-2):
                    v = t.i + 2
                    x_src = x_dram[:, v] if t.fixed else x_dram[:, bass.ds(v, 1)].rearrange("t u g d -> t (u g) d")
                    t.apart()
                    t.wait(xt_ps[0], t.now(-1))
                    t.wait(x0b_sb, t.now(-1))
                    t.wait(x_in, t.now(-1), 16)
                    sp.dma_start(X0[:], x_src).then_inc(x_in, 16)
                    t.apart()
                    t.wait(adj_in, t.now(-1), 16)
                    t.wait(lnadj2_sb, t.was(3))
                    t.wait(m3a_sb, t.was(3))
                    a_src = adj_dram[:, v] if t.fixed else adj_dram[:, bass.ds(v, 1)].rearrange("q u g k -> q (u g) k")
                    sp.dma_start(t.slot(-2).rearrange("p (g k) -> p g k", g=G), a_src).then_inc(adj_in, 16)
                if t.has(-1):
                    spread(0, t, -1)
                if t.has(3):
                    t.apart()
                    t.wait(out_sb, t.now(3))
                    v = t.i - 3
                    dst = out_dram[:, v] if t.fixed else out_dram[:, bass.ds(v, 1)].rearrange("t u g d -> t (u g) d")
                    sp.dma_start(dst, OUT[:]).then_inc(out_stored, 16)

            run(sp, turn, multiples=((2, 16),))
            sp.wait_ge(out_stored, 16 * NP_)

        @block.tensor
        def _(pe):
            def product(o, pairs):
                terms = [(a, b) for l, r in pairs for a, b in ((l[0], r[0]), (l[0], r[1]), (l[1], r[0]))]
                for n, (a, b) in enumerate(terms):
                    mm = nc.tensor.matmul(o, a, b, start=(n == 0), stop=(n == len(terms) - 1))
                return mm

            def cut(s, *idx):
                return s.hi[idx], s.lo[idx]

            pe.wait_ge(const_ready, 1)
            for n, name in enumerate(STEPS):
                bank = work[:, n % 4]
                if n >= 4:
                    pe.wait_ge(prep_hi, n - 3)
                    pe.wait_ge(prep_lo, n - 3)
                if name == "cols":
                    pe.wait_ge(small_in, 16 * N_SMALL)
                    mm = nc.tensor.transpose(bank[:, 0:N_COL], col_rows[0:N_COL, :], ident[0:N_COL, 0:N_COL])
                elif name in TURNED:
                    pe.wait_ge(w_in[name], 16)
                    for c in range(C):
                        for o in range(C):
                            mm = nc.tensor.transpose(bank[:, c * D + o * P:c * D + (o + 1) * P],
                                                     stage[name][:, o, c * P:(c + 1) * P], ident[:])
                elif name == "wqk1":
                    pe.wait_ge(prep_hi, n)
                    pe.wait_ge(prep_lo, n)
                    for m in range(C):
                        for e in range(C):
                            mm = nc.tensor.matmul(bank[:, m * D:(m + 1) * D], wqT1[:, e, m * P:(m + 1) * P],
                                                  wkT1[:, e, :], start=(e == 0), stop=(e == C - 1))
                elif name == "rows1":
                    for e in range(C):
                        nc.tensor.matmul(bank[:, 0:D], bk1[:, e:e + 1].to_broadcast([P, P]), wqT1[:, e, :],
                                         start=(e == 0), stop=(e == C - 1))
                    for e in range(C):
                        nc.tensor.matmul(bank[:, D:D + 1], bk1[:, e:e + 1].to_broadcast([P, P]), bq1[:, e:e + 1],
                                         start=(e == 0), stop=(e == C - 1))
                    for m in range(C):
                        for e in range(C):
                            mm = nc.tensor.matmul(bank[:, D + 2 + m:D + 3 + m], wkT1[:, e, m * P:(m + 1) * P],
                                                  bq1[:, e:e + 1], start=(e == 0), stop=(e == C - 1))
                else:
                    for c in range(C):
                        for o in range(C):
                            nc.tensor.matmul(bank[:, 2 * c:2 * c + 2], stage["fc3"][:, o, c * P:(c + 1) * P],
                                             qk3[:, o, :], start=(o == 0), stop=(o == C - 1))
                    for o in range(C):
                        mm = nc.tensor.matmul(bank[:, 4:6], bf3c[:, o:o + 1].to_broadcast([P, P]), qk3[:, o, :],
                                              start=(o == 0), stop=(o == C - 1))
                mm.then_inc(prep_pe, 1)
            pe.wait_ge(prep_hi, len(STEPS) + len(NATURAL) + 1)
            pe.wait_ge(prep_lo, len(STEPS) + len(NATURAL) + 1)

            def transpose_x(l, x_, bank):
                for g in range(G):
                    for c in range(C):
                        mm = nc.tensor.transpose(work[:, bank, c * G * P + g * P:c * G * P + (g + 1) * P],
                                                 x_[:, g, c * P:(c + 1) * P], ident[:])
                mm.then_inc(xt_ps[l], 1)

            def project_t(w_, l, bank):
                for m in range(C):
                    mm = product(work[:, bank, m * G * P:(m + 1) * G * P],
                                 [(cut(w_, slice(None), c, slice(m * P, (m + 1) * P)), cut(XT[l], slice(None), c))
                                  for c in range(C)])
                return mm

            def project(o, xt, g, w_):
                return product(o, [(cut(xt, slice(None), c, slice(g * P, (g + 1) * P)), cut(w_, slice(None), c))
                                   for c in range(C)])

            def scores(l, g):
                for m in range(C):
                    mm = nc.tensor.matmul(score_ps[:, g * C + m, :], QT[l][:, m, g * P:(g + 1) * P],
                                          KD[l][:, m * G + g, :], start=True, stop=True)
                mm.then_inc(s_ps[l][g], 1)

            def turn_probs(l, g):
                for h in range(H):
                    mm = nc.tensor.transpose(score_ps[:, 2 * g + h // R, (h % R) * P:(h % R + 1) * P],
                                             E[l][:, g, h, :], ident[:])
                mm.then_inc(et_ps[l][g], 1)

            def values(l, g, bank):
                for m in range(C):
                    for r in range(R):
                        h = m * R + r
                        mm = nc.tensor.matmul(work[r * HD:(r + 1) * HD, bank, m * G * P + g * P:m * G * P + (g + 1) * P],
                                              V[l][:, g, h * HD:(h + 1) * HD], ET[l][:, g, h, :], start=True, stop=True)
                if g == G - 1:
                    mm.then_inc(ot_ps[l], 1)

            def turn(t):
                if t.has(1):
                    t.wait(x1_sb, t.now(1))
                    t.wait(y_sb[1], t.was(1))
                    t.first_and_last(3, 0)
                    transpose_x(1, X1, 3)
                if t.has(0):
                    t.wait(q_sb[0], t.now(0))
                    t.wait(keys_spread[0], t.now(0), 16 * R)
                    t.wait(et_sb[2][0], t.was(2))
                    t.wait(et_sb[2][1], t.was(2))
                    t.first_and_last("scores", 0)
                    scores(0, 0)
                if t.has(3):
                    t.wait(ot2_sb, t.now(3))
                    t.wait(e3t_sb, t.was(3))
                    t.first_and_last(1, 0)
                    for g in range(G):
                        for c in range(C):
                            mm = nc.tensor.transpose(work[:, 1, g * D + c * P:g * D + (c + 1) * P],
                                                     OT2[:, c, g * P:(g + 1) * P], ident[:])
                    mm.then_inc(o2_ps, 1)
                if t.has(0):
                    scores(0, 1)
                if t.has(3):
                    t.wait(x3_sb, t.now(3))
                    t.wait(out_sb, t.was(3))
                    t.first_and_last(0, 0)
                    transpose_x(3, X3, 0)
                if t.has(1):
                    t.wait(xt_hi[1], t.now(1))
                    t.wait(xt_lo[1], t.now(1))
                    t.wait(x3_sb, t.now(3))
                    t.first_and_last(1, 1)
                    project_t(wqk1, 1, 1).then_inc(g1_ps, 1)
                if t.has(2):
                    t.wait(x2_sb, t.now(2))
                    t.wait(x1t_sb, t.now(1))
                    t.first_and_last(3, 1)
                    transpose_x(2, X2, 3)
                if t.has(3):
                    t.wait(xt_hi[3], t.now(3))
                    t.wait(xt_lo[3], t.now(3))
                    t.wait(ot2_sb, t.now(3))
                    t.first_and_last(2, 0)
                    project(work[:, 2, 0:D + 2], XT[3], 0, wf3).then_inc(f3a_ps, 1)
                    t.first_and_last(0, 1)
                    project(work[:, 0, 0:D + 2], XT[3], 1, wf3).then_inc(f3b_ps, 1)
                if t.has(2):
                    t.wait(xt_hi[2], t.now(2))
                    t.wait(xt_lo[2], t.now(2))
                    t.wait(g1_sb, t.now(1))
                    t.first_and_last(1, 2)
                    project_t(wq2, 2, 1).then_inc(q_ps[2], 1)
                    t.first_and_last(3, 2)
                    project_t(wk2, 2, 3).then_inc(k_ps[2], 1)
                if t.has(0):
                    t.wait(prob[0][0], t.now(0))
                    t.wait(t_all[0][0], t.now(0))
                    turn_probs(0, 0)
                if t.has(2):
                    t.wait(f3_sb[1], t.now(3))
                    t.first_and_last(0, 2)
                    project(work[:, 0, 0:D + 2], XT[2], 0, wv2).then_inc(v2_ps[0], 1)
                    t.wait(q_sb[2], t.now(2))
                    t.first_and_last(1, 3)
                    project(work[:, 1, 0:D + 2], XT[2], 1, wv2).then_inc(v2_ps[1], 1)
                if t.has(0):
                    t.wait(et_sb[0][0], t.now(0))
                    t.wait(f3_sb[0], t.now(3))
                    t.first_and_last(2, 1)
                    values(0, 0, 2)
                if t.has(1):
                    t.wait(g1_sb, t.now(1))
                    t.wait(x1t_sb, t.now(1))
                    t.wait(k_sb[2], t.now(2))
                    t.first_and_last(3, 3)
                    for g in range(G):
                        for c in range(C):
                            mm = nc.tensor.matmul(work[:, 3, g * P:(g + 1) * P], G1[:, c, g * P:(g + 1) * P],
                                                  X1T[:, c, g * P:(g + 1) * P], start=(c == 0), stop=(c == C - 1))
                    mm.then_inc(s1_ps, 1)
                if t.has(0):
                    t.wait(prob[0][1], t.now(0))
                    turn_probs(0, 1)
                if t.has(3):
                    t.wait(f3_sb[0], t.now(3))
                    t.wait(f3_sb[1], t.now(3))
                    t.wait(v2_sb[0], t.now(2))
                    t.first_and_last(0, 3)
                    for g in range(G):
                        mm = nc.tensor.transpose(work[:, 0, g * P:(g + 1) * P],
                                                 QK3[:, g, 1:2].to_broadcast([P, P]), ident[:])
                    mm.then_inc(k3_ps, 1)
                if t.has(2):
                    t.wait(v2_sb[0], t.now(2))
                    t.wait(v2_sb[1], t.now(2))
                    t.first_and_last(1, 4)
                    for g in range(G):
                        mm = nc.tensor.transpose(work[:, 1, g * P:(g + 1) * P],
                                                 AC2[:, g, 1:2].to_broadcast([P, P]), ident[:])
                    mm.then_inc(c2_ps, 1)
                if t.has(0):
                    t.wait(et_sb[0][1], t.now(0))
                    values(0, 1, 2)
                if t.has(0):
                    t.wait(ot0_hi, t.now(0))
                    t.wait(ot0_lo, t.now(0))
                    t.wait(t1_all, t.now(1))
                    t.first_and_last(3, 4)
                    for g in range(G):
                        mm = project(work[:, 3, g * D:(g + 1) * D], OT0, g, wo0)
                    mm.then_inc(y0_ps, 1)
                if t.has(-1):
                    t.wait(x_in, t.now(-1), 16)
                    t.wait(ot0_hi, t.now(0))
                    t.wait(ot0_lo, t.now(0))
                    t.first_and_last(2, 2)
                    transpose_x(0, X0, 2)
                if t.has(2):
                    t.wait(q_sb[2], t.now(2))
                    t.wait(keys_spread[2], t.now(2), 16 * R)
                    t.wait(et_sb[0][0], t.now(0))
                    t.wait(et_sb[0][1], t.now(0))
                    t.first_and_last("scores", 1)
                    scores(2, 0)
                    scores(2, 1)
                if t.has(1):
                    t.wait(a1_sb, t.now(1))
                    t.wait(u3_sb, t.now(3))
                    t.first_and_last(0, 4)
                    for g in range(G):
                        mm = nc.tensor.transpose(work[:, 0, g * P:(g + 1) * P], A1[:, g * P:(g + 1) * P], ident[:])
                    mm.then_inc(a1t_ps, 1)
                if t.has(-1):
                    t.wait(xt_hi[0], t.now(-1))
                    t.wait(xt_lo[0], t.now(-1))
                    t.wait(bias2_sb, t.now(2))
                    t.first_and_last(1, 5)
                    project_t(wq0, 0, 1).then_inc(q_ps[0], 1)
                    t.wait(y_sb[0], t.now(0))
                    t.first_and_last(3, 5)
                    project_t(wk0, 0, 3).then_inc(k_ps[0], 1)
                if t.has(1):
                    t.wait(a1t_sb, t.now(1))
                    t.wait(xt_hi[0], t.now(-1))
                    t.wait(xt_lo[0], t.now(-1))
                    t.first_and_last(2, 3)
                    for g in range(G):
                        for c in range(C):
                            mm = nc.tensor.matmul(work[:, 2, c * G * P + g * P:c * G * P + (g + 1) * P],
                                                  X1[:, g, c * P:(c + 1) * P], A1T[:, g * P:(g + 1) * P],
                                                  start=True, stop=True)
                    mm.then_inc(ct1_ps, 1)
                if t.has(-1):
                    t.wait(a1t_sb, t.now(1))
                    t.first_and_last(0, 5)
                    for g in range(G):
                        mm = project(work[:, 0, g * D:(g + 1) * D], XT[0], g, wv0)
                    mm.then_inc(v0_ps, 1)
                if t.has(3):
                    t.wait(exp3, t.now(3))
                    t.wait(q_sb[0], t.now(-1))
                    t.first_and_last(1, 6)
                    for g in range(G):
                        mm = nc.tensor.transpose(work[:, 1, g * P:(g + 1) * P], E3[:, g * P:(g + 1) * P], ident[:])
                    mm.then_inc(e3t_ps, 1)
                if t.has(1):
                    t.wait(ct1_hi, t.now(1))
                    t.wait(ct1_lo, t.now(1))
                    t.wait(k_sb[0], t.now(-1))
                    t.first_and_last(3, 6)
                    for g in range(G):
                        mm = project(work[:, 3, g * D:(g + 1) * D], CT1, g, wc1)
                    mm.then_inc(y1_ps, 1)
                if t.has(2):
                    t.wait(prob[2][0], t.now(2))
                    t.wait(t_all[2][0], t.now(2))
                    turn_probs(2, 0)
                if t.has(3):
                    t.wait(e3t_sb, t.now(3))
                    t.wait(v0_sb, t.now(-1))
                    t.first_and_last(0, 6)
                    for g in range(G):
                        mm = nc.tensor.matmul(work[:, 0, g * D:(g + 1) * D], E3T[:, g * P:(g + 1) * P], F3[:, g, :],
                                              start=True, stop=True)
                    mm.then_inc(o3_ps, 1)
                if t.has(2):
                    t.wait(et_sb[2][0], t.now(2))
                    t.wait(ct1_hi, t.now(1))
                    t.wait(ct1_lo, t.now(1))
                    t.first_and_last(2, 4)
                    values(2, 0, 2)
                    t.wait(prob[2][1], t.now(2))
                    turn_probs(2, 1)
                    t.wait(et_sb[2][1], t.now(2))
                    values(2, 1, 2)

            run(pe, turn, multiples=((2, 16), (1, 16 * R), (-1, 16 * R)))

        @block.scalar
        def _(act):
            nc.scalar.preload_act_table_set("natural_log_exp_and_others")
            for n in ("Wk0", "Wo0", "Wq1", "Wc1", "Wk2"):
                act.dma_start(stage[n], w[n].rearrange("(c p) d -> p c d", p=P)).then_inc(w_in[n], 16)
            for j, n in enumerate(COLUMNS):
                act.dma_start(col_rows[C * j:C * (j + 1), :], w[n].rearrange("(c p) -> c p", p=P)).then_inc(small_in, 16)
            for c in range(C):
                for j, v in enumerate((w["q_w"][0], w["k_w"][0], w["w_g"][0:D], w["w_g"][D:2 * D])):
                    n = C * len(COLUMNS) + 2 * C * (j // 2) + 2 * c + j % 2
                    act.dma_start(col_rows[n:n + 1, :], v[c * P:(c + 1) * P].rearrange("(a p) -> a p", a=1)).then_inc(small_in, 16)
            act.dma_start(bg2[:, 0:1], w["b_g"].to_broadcast([P, 1])).then_inc(small_in, 16)
            for n, j in (("q_b", 0), ("k_b", 1)):
                act.dma_start(bqk3[:, j:j + 1], w[n].to_broadcast([P, 1])).then_inc(small_in, 16)

            for n, name in enumerate(STEPS):
                act.wait_ge(prep_pe, n + 1)
                bank = work[:, n % 4]
                two = bank.rearrange("p (c d) -> p c d", c=C)
                if name == "cols":
                    ins = nc.scalar.activation(cols[:], bank[:, 0:N_COL], ACT.Copy)
                elif name in SPLIT_OF:
                    ins = nc.scalar.activation(SPLIT_OF[name].hi[:, :, 0:D], two, ACT.Copy)
                elif name == "Wq1":
                    ins = nc.scalar.activation(wqT1, two, ACT.Copy)
                elif name == "Wk1":
                    ins = nc.scalar.activation(wkT1, two, ACT.Copy)
                elif name == "wqk1":
                    ins = nc.scalar.activation(wqk1.hi[:], two, ACT.Copy, scale=SC1)
                elif name == "rows1":
                    nc.scalar.activation(wu1[:], bank[:, 0:D], ACT.Copy, scale=SC1)
                    nc.scalar.activation(c0[:], bank[:, D:D + 1], ACT.Copy, scale=SC1)
                    ins = nc.scalar.activation(c1[:], bank[:, D + 2:D + 2 + C], ACT.Copy, scale=SC1)
                else:
                    ins = nc.scalar.activation(wf3.hi[:, :, D:D + 2], bank[:, 0:4].rearrange("p (c j) -> p c j", c=C), ACT.Copy)
                ins.then_inc(prep_hi, 1)
            for name, s in NATURAL:
                act.wait_ge(w_in[name], 16)
                nc.scalar.activation(s.hi[:, :, 0:D], stage[name], ACT.Copy).then_inc(prep_hi, 1)
            act.wait_ge(prep_hi, 1)
            nc.scalar.activation(wv2.hi[:, :, D:D + 2], wg2, ACT.Copy).then_inc(prep_hi, 1)
            nc.scalar.activation(bq0s[:], bq0, ACT.Copy, scale=SC)
            nc.scalar.activation(bq2s[:], bq2, ACT.Copy, scale=SC).then_inc(prep_plain, 1)
            act.wait_ge(prep_plain, 1)
            act.wait_ge(prep_lo, len(STEPS) + len(NATURAL) + 1)
            act.wait_ge(dve_const, 1)

            def hi(l, bank, t, off):
                t.wait(xt_ps[l], t.now(off))
                nc.scalar.activation(XT[l].hi[:], work[:, bank].rearrange("p (c k) -> p c k", c=C),
                                     ACT.Copy).then_inc(xt_hi[l], 1)

            def exps(l, g, t, off, a, b):
                t.wait((t_first if b <= R else t_all)[l][g], t.now(off))
                if a == 0:
                    t.wait(rs_sb[l][g], t.was(off))
                for h in range(a, b):
                    j = g * H + h
                    ins = nc.scalar.activation(E[l][:, g, h, :], E[l][:, g, h, :], ACT.Exp, scale=-1.0,
                                               bias=NM[l][:, j:j + 1], accum_out=SUM[l][:, j:j + 1])
                if b == H:
                    ins.then_inc(exp_half[l][g], 1)

            def queries(l, bank, b_, t, off):
                t.wait(q_ps[l], t.now(off))
                t.wait(s_ps[l][1], t.was(off))
                for m in range(C):
                    ins = nc.scalar.activation(QT[l][:, m, :], work[:, bank, m * G * P:(m + 1) * G * P],
                                               ACT.Identity, scale=SC, bias=b_[:, m:m + 1])
                ins.then_inc(q_sb[l], 1)

            def turned(l, g, t, off):
                t.wait(et_ps[l][g], t.now(off))
                t.wait(ot_ps[l], t.was(off))
                nc.scalar.activation(ET[l][:, g].rearrange("p (m r) k -> p m (r k)", m=C),
                                     score_ps[:, 2 * g:2 * g + 2], ACT.Copy).then_inc(et_sb[l][g], 1)

            def turn(t):
                if t.has(1):
                    t.wait(xt_ps[1], t.now(1))
                    t.wait(s1_ps, t.was(1))
                    t.wait(xt_lo[1], t.was(1))
                    nc.scalar.activation(X1T[:], work[:, 3].rearrange("p (c k) -> p c k", c=C),
                                         ACT.Copy).then_inc(x1t_sb, 1)
                    t.wait(g1_ps, t.was(1))
                    t.wait(x1t_sb, t.now(1))
                    nc.scalar.activation(XT[1].hi[:], X1T[:], ACT.Copy).then_inc(xt_hi[1], 1)
                if t.has(0):
                    exps(0, 0, t, 0, 0, R)
                    exps(0, 0, t, 0, R, H)
                if t.has(3):
                    t.wait(f3b_ps, t.was(3))
                    hi(3, 0, t, 3)
                if t.has(0):
                    exps(0, 1, t, 0, 0, R)
                if t.has(2):
                    t.wait(v2_ps[1], t.was(2))
                    hi(2, 3, t, 2)
                if t.has(0):
                    exps(0, 1, t, 0, R, H)
                if t.has(2):
                    queries(2, 1, bq2s, t, 2)
                if t.has(0):
                    turned(0, 0, t, 0)
                if t.has(2):
                    t.wait(adj_in, t.now(2), 16)
                    t.wait(bias2_sb, t.was(2))
                    nc.scalar.activation(LNADJ2[:], t.slot(2), ACT.Ln, bias=eps2[:]).then_inc(lnadj2_sb, 1)
                if t.has(1):
                    t.wait(t1_all, t.now(1))
                    t.wait(rs1_sb, t.was(1))
                    for g in range(G):
                        ins = nc.scalar.activation(E1[:, g * P:(g + 1) * P], E1[:, g * P:(g + 1) * P], ACT.Exp,
                                                   scale=-1.0, bias=NM1[:, g:g + 1], accum_out=SUM1[:, g:g + 1])
                    ins.then_inc(exp1, 1)
                if t.has(0):
                    turned(0, 1, t, 0)
                    t.wait(ot_ps[0], t.now(0))
                    t.wait(y0_ps, t.was(0))
                    nc.scalar.activation(OT0.hi[:], work[:, 2].rearrange("p (c k) -> p c k", c=C),
                                         ACT.Copy).then_inc(ot0_hi, 1)
                if t.has(3):
                    t.wait(nm3_sb, t.now(3))
                    t.wait(e3t_ps, t.was(3))
                    t.wait(rs3_sb, t.was(3))
                    for g in range(G):
                        ins = nc.scalar.activation(E3[:, g * P:(g + 1) * P], L3[:, g * P:(g + 1) * P], ACT.Exp,
                                                   bias=NM3[:, g:g + 1], accum_out=SUM3[:, g:g + 1])
                    ins.then_inc(exp3, 1)
                if t.has(-1):
                    t.wait(v0_ps, t.was(-1))
                    hi(0, 2, t, -1)
                if t.has(2):
                    exps(2, 0, t, 2, 0, R)
                    exps(2, 0, t, 2, R, H)
                if t.has(1):
                    t.wait(a1t_ps, t.now(1))
                    t.wait(ct1_ps, t.was(1))
                    nc.scalar.activation(A1T[:], work[:, 0, 0:G * P], ACT.Copy).then_inc(a1t_sb, 1)
                if t.has(2):
                    exps(2, 1, t, 2, 0, R)
                if t.has(-1):
                    queries(0, 1, bq0s, t, -1)
                if t.has(2):
                    exps(2, 1, t, 2, R, H)
                if t.has(1):
                    t.wait(ct1_ps, t.now(1))
                    t.wait(y1_ps, t.was(1))
                    nc.scalar.activation(CT1.hi[:], work[:, 2].rearrange("p (c k) -> p c k", c=C),
                                         ACT.Copy).then_inc(ct1_hi, 1)
                if t.has(3):
                    t.wait(e3t_ps, t.now(3))
                    t.wait(o3_ps, t.was(3))
                    nc.scalar.activation(E3T[:], work[:, 1, 0:G * P], ACT.Copy).then_inc(e3t_sb, 1)
                if t.has(-1):
                    t.wait(clip0, t.now(-1))
                    nc.scalar.activation(BIAS0[:], BIAS0[:], ACT.Ln).then_inc(bias0_sb, 1)
                if t.has(2):
                    turned(2, 0, t, 2)
                    turned(2, 1, t, 2)
                    t.wait(ot_ps[2], t.now(2))
                    t.wait(o2_ps, t.was(2))
                    nc.scalar.activation(OT2[:], work[:, 2].rearrange("p (c k) -> p c k", c=C),
                                         ACT.Copy).then_inc(ot2_sb, 1)

            run(act, turn, multiples=((-1, 16),))

        @block.vector
        def _(dve):
            for l in (0, 2):
                nc.vector.memset(KD[l][:], 0.0)
            nc.vector.memset(eps2[:], 1e-9)
            nc.vector.memset(bg2[:, 1:2], 0.0).then_inc(dve_const, 1)

            def lower(s, src, hi_, scale=1.0):
                return nc.vector.scalar_tensor_tensor(out=s, in0=src, scalar=scale, in1=hi_.bitcast(F32),
                                                      op0=ALU.mult, op1=ALU.subtract)

            for n, name in enumerate(STEPS):
                dve.wait_ge(prep_hi, n + 1)
                bank = work[:, n % 4]
                two = bank.rearrange("p (c d) -> p c d", c=C)
                if name in SPLIT_OF:
                    s = SPLIT_OF[name]
                    lower(s.lo[:, :, 0:D], two, s.hi[:, :, 0:D]).then_inc(prep_lo, 1)
                elif name == "wqk1":
                    lower(wqk1.lo[:], two, wqk1.hi[:], SC1).then_inc(prep_lo, 1)
                elif name == "cols3":
                    lower(wf3.lo[:, :, D:D + 2], bank[:, 0:4].rearrange("p (c j) -> p c j", c=C), wf3.hi[:, :, D:D + 2])
                    dve.wait_ge(small_in, 16 * N_SMALL)
                    nc.vector.tensor_tensor(add3[:], bank[:, 4:6], bqk3[:], ALU.add).then_inc(prep_lo, 1)
                else:
                    nc.vector.memset(count_only[:, n:n + 1], 0.0).then_inc(prep_lo, 1)
            for n, (name, s) in enumerate(NATURAL):
                dve.wait_ge(prep_hi, len(STEPS) + n + 1)
                lower(s.lo[:, :, 0:D], stage[name], s.hi[:, :, 0:D]).then_inc(prep_lo, 1)
            dve.wait_ge(prep_hi, len(STEPS) + len(NATURAL) + 1)
            lower(wv2.lo[:, :, D:D + 2], wg2, wv2.hi[:, :, D:D + 2]).then_inc(prep_lo, 1)
            dve.wait_ge(prep_lo, len(STEPS) + len(NATURAL) + 1)
            dve.wait_ge(small_in, 16 * N_SMALL)

            def lo(l, bank, t, off):
                t.wait(xt_hi[l], t.now(off))
                nc.vector.tensor_tensor(XT[l].lo[:], work[:, bank].rearrange("p (c k) -> p c k", c=C),
                                        XT[l].hi[:].bitcast(F32), ALU.subtract).then_inc(xt_lo[l], 1)

            def shifted(l, g, bias, t, off):
                t.apart()
                t.wait(s_ps[l][g], t.now(off))
                t.wait(et_ps[l][g], t.was(off))
                for h in range(H):
                    m, r = divmod(h, R)
                    j = g * H + h
                    ins = nc.vector.tensor_tensor_reduce(
                        out=E[l][:, g, h, :], in0=score_ps[:, g * C + m, r * P:(r + 1) * P],
                        in1=bias[:, g * P:(g + 1) * P], scale=-1.0, scalar=HUGE, op0=ALU.add, op1=ALU.min,
                        accum_out=NM[l][:, j:j + 1])
                    if h == R - 1:
                        ins.then_inc(t_first[l][g], 1)
                ins.then_inc(t_all[l][g], 1)

            def inverse(l, g, t, off):
                t.wait(exp_half[l][g], t.now(off))
                t.wait(prob[l][g], t.was(off))
                nc.vector.reciprocal(RS[l][:, g * H:(g + 1) * H], SUM[l][:, g * H:(g + 1) * H]).then_inc(rs_sb[l][g], 1)

            def keys(l, bank, b_, t, off):
                t.wait(k_ps[l], t.now(off))
                t.wait(keys_spread[l], t.was(off), 16 * R)
                for m in range(C):
                    ins = nc.vector.tensor_scalar(KT[l][:, m, :], work[:, bank, m * G * P:(m + 1) * G * P],
                                                  b_[:, m:m + 1], None, ALU.add)
                ins.then_inc(k_sb[l], 1)

            def both(r_):
                return r_[:].unsqueeze(1).to_broadcast([P, G, D])

            def normed(l, y_ps, bank, res, t, off):
                t.wait(y_ps, t.now(off))
                t.wait((x1_sb, x2_sb)[l], t.was(off))
                nc.vector.tensor_tensor(Y[l][:], work[:, bank].rearrange("p (g d) -> p g d", g=G), res,
                                        ALU.add).then_inc(y_sb[l], 1)
                t.wait(y_sb[l], t.now(off))
                for g in range(G):
                    ins = nc.vector.bn_stats(STAT[l][:, g, :], Y[l][:, g, :])
                ins.then_inc(stat_sb[l], 1)
                t.apart()
                t.wait(stat_sb[l], t.now(off))
                for g in range(G):
                    ins = nc.vector.bn_aggr(MV[l][:, g, :], STAT[l][:, g, :])
                ins.then_inc(mv_sb[l], 1)

            def scaled(l, t, off):
                t.wait(rstd_sb[l], t.now(off))
                for g in range(G):
                    ins = nc.vector.tensor_scalar(Y[l][:, g, :], Y[l][:, g, :], MV[l][:, g, 0:1], RSTD[l][:, g:g + 1],
                                                  ALU.subtract, ALU.mult)
                ins.then_inc(z_sb[l], 1)

            def turn(t):
                if t.has(1):
                    t.wait(xt_hi[1], t.now(1))
                    nc.vector.tensor_tensor(XT[1].lo[:], X1T[:], XT[1].hi[:].bitcast(F32),
                                            ALU.subtract).then_inc(xt_lo[1], 1)
                if t.has(0):
                    t.apart()
                    t.wait(bias0_sb, t.now(0))
                    shifted(0, 0, BIAS0, t, 0)
                if t.has(3):
                    t.wait(o2_ps, t.now(3))
                    t.wait(x2_sb, t.now(3))
                    t.wait(xt_ps[3], t.was(3))
                    t.wait(out_sb, t.was(3))
                    nc.vector.tensor_tensor(X3[:], work[:, 1].rearrange("p (g d) -> p g d", g=G), X2[:],
                                            ALU.add).then_inc(x3_sb, 1)
                if t.has(0):
                    shifted(0, 1, BIAS0, t, 0)
                if t.has(3):
                    lo(3, 0, t, 3)
                if t.has(0):
                    inverse(0, 0, t, 0)
                if t.has(1):
                    t.wait(g1_ps, t.now(1))
                    t.wait(s1_ps, t.was(1))
                    for m in range(C):
                        ins = nc.vector.tensor_scalar(G1[:, m, :], work[:, 1, m * G * P:(m + 1) * G * P], c1[:, m:m + 1],
                                                      None, ALU.add)
                    ins.then_inc(g1_sb, 1)
                if t.has(2):
                    lo(2, 3, t, 2)
                if t.has(3):
                    for g, (ps, bank) in enumerate(((f3a_ps, 2), (f3b_ps, 0))):
                        t.wait(ps, t.now(3))
                        t.wait(o3_ps, t.was(3))
                        t.wait(k3_ps, t.was(3))
                        t.wait(u3_sb, t.was(3))
                        nc.vector.tensor_tensor(QK3[:, g, :], work[:, bank, D:D + 2], add3[:], ALU.add)
                        nc.vector.tensor_tensor(F3[:, g, :], work[:, bank, 0:D], row["bf3"][:],
                                                ALU.add).then_inc(f3_sb[g], 1)
                if t.has(0):
                    inverse(0, 1, t, 0)
                if t.has(2):
                    keys(2, 3, bk2, t, 2)
                if t.has(1):
                    t.wait(x1_sb, t.now(1))
                    t.wait(bias1_sb, t.was(1))
                    for g in range(G):
                        ins = nc.vector.tensor_tensor_reduce(
                            out=U1junk[:, g, :], in0=X1[:, g, :], in1=wu1[:], scale=1.0, scalar=0.0, op0=ALU.mult,
                            op1=ALU.add, accum_out=U1[:, g:g + 1])
                    ins.then_inc(u1_sb, 1)
                    t.wait(adj_in, t.now(1), 16)
                    t.wait(a1_sb, t.was(1))
                    nc.vector.tensor_scalar(MASK1[:], t.slot(1), 0.0, None, ALU.not_equal).then_inc(mask1_sb, 1)
                    t.wait(t1_all, t.was(1))
                    nc.vector.tensor_scalar(BIAS1[:], t.slot(1), 0.0, MASKED, ALU.is_equal, ALU.mult).then_inc(nbias1_sb, 1)
                    t.wait(nbias1_sb, t.now(1))
                    t.wait(u1_sb, t.now(1))
                    for g in range(G):
                        ins = nc.vector.tensor_scalar(BIAS1[:, g * P:(g + 1) * P], BIAS1[:, g * P:(g + 1) * P],
                                                      U1[:, g:g + 1], c0[:, 0:1], ALU.add, ALU.add)
                    ins.then_inc(bias1_sb, 1)
                if t.has(3):
                    t.wait(adj_in, t.now(3), 16)
                    t.wait(m3_sb, t.was(3))
                    nc.vector.tensor_scalar(M3a[:], t.slot(3), -1.0, 1.0, ALU.mult, ALU.add).then_inc(m3a_sb, 1)
                if t.has(2):
                    for g in range(G):
                        t.wait(v2_ps[g], t.now(2))
                        t.wait(ot_ps[2], t.was(2))
                        t.wait(c2_ps, t.was(2))
                        t.wait(bias2_sb, t.was(2))
                        nc.vector.tensor_tensor(AC2[:, g, :], work[:, g, D:D + 2], bg2[:], ALU.add)
                        nc.vector.tensor_tensor(V[2][:, g, :], work[:, g, 0:D], row["bv2"][:],
                                                ALU.add).then_inc(v2_sb[g], 1)
                if t.has(1):
                    t.apart()
                    t.wait(s1_ps, t.now(1))
                    t.wait(bias1_sb, t.now(1))
                    for g in range(G):
                        ins = nc.vector.tensor_tensor_reduce(
                            out=E1[:, g * P:(g + 1) * P], in0=work[:, 3, g * P:(g + 1) * P],
                            in1=BIAS1[:, g * P:(g + 1) * P], scale=-1.0, scalar=HUGE, op0=ALU.add, op1=ALU.min,
                            accum_out=NM1[:, g:g + 1])
                    ins.then_inc(t1_all, 1)
                if t.has(3):
                    t.wait(k3_ps, t.now(3))
                    t.wait(m3_sb, t.now(3))
                    t.wait(f3_sb[1], t.now(3))
                    t.wait(l3_sb, t.was(3))
                    for g in range(G):
                        ins = nc.vector.scalar_tensor_tensor(
                            out=U3[:, g * P:(g + 1) * P], in0=work[:, 0, g * P:(g + 1) * P], scalar=QK3[:, g, 0:1],
                            in1=M3[:, g * P:(g + 1) * P], op0=ALU.add, op1=ALU.add)
                    ins.then_inc(u3_sb, 1)
                    t.wait(u3_sb, t.now(3))
                    t.wait(exp3, t.was(3))
                    nc.vector.scalar_tensor_tensor(out=L3[:], in0=U3[:], scalar=0.01, in1=U3[:], op0=ALU.mult,
                                                   op1=ALU.max).then_inc(l3_sb, 1)
                    t.wait(l3_sb, t.now(3))
                    nc.vector.tensor_reduce(NM3[:], L3[:].rearrange("p (g k) -> p g k", g=G), AX_X, ALU.max,
                                            negate=True).then_inc(nm3_sb, 1)
                if t.has(2):
                    t.wait(c2_ps, t.now(2))
                    t.wait(v2_sb[1], t.now(2))
                    t.wait(lnadj2_sb, t.now(2))
                    t.wait(t_all[2][1], t.was(2))
                    for g in range(G):
                        ins = nc.vector.scalar_tensor_tensor(
                            out=BIAS2[:, g * P:(g + 1) * P], in0=work[:, 1, g * P:(g + 1) * P], scalar=AC2[:, g, 0:1],
                            in1=LNADJ2[:, g * P:(g + 1) * P], op0=ALU.add, op1=ALU.add)
                    ins.then_inc(bias2_sb, 1)
                if t.has(0):
                    t.wait(ot0_hi, t.now(0))
                    nc.vector.tensor_tensor(OT0.lo[:], work[:, 2].rearrange("p (c k) -> p c k", c=C),
                                            OT0.hi[:].bitcast(F32), ALU.subtract).then_inc(ot0_lo, 1)
                if t.has(1):
                    t.wait(exp1, t.now(1))
                    nc.vector.reciprocal(RS1[:], SUM1[:]).then_inc(rs1_sb, 1)
                    t.wait(rs1_sb, t.now(1))
                    t.wait(mask1_sb, t.now(1))
                    t.wait(a1t_ps, t.was(1))
                    for g in range(G):
                        ins = nc.vector.scalar_tensor_tensor(
                            out=A1[:, g * P:(g + 1) * P], in0=E1[:, g * P:(g + 1) * P], scalar=RS1[:, g:g + 1],
                            in1=MASK1[:, g * P:(g + 1) * P], op0=ALU.mult, op1=ALU.mult)
                    ins.then_inc(a1_sb, 1)
                if t.has(0):
                    t.wait(x0b_sb, t.now(0))
                    normed(0, y0_ps, 3, X0b[:], t, 0)
                if t.has(-1):
                    lo(0, 2, t, -1)
                    t.wait(adj_in, t.now(-1), 16)
                    t.wait(t_all[0][1], t.was(-1))
                    nc.vector.tensor_scalar(BIAS0[:], t.slot(-1), 1e-8, None, ALU.max).then_inc(clip0, 1)
                if t.has(2):
                    t.apart()
                    t.wait(bias2_sb, t.now(2))
                    shifted(2, 0, BIAS2, t, 2)
                if t.has(0):
                    scaled(0, t, 0)
                if t.has(2):
                    shifted(2, 1, BIAS2, t, 2)
                if t.has(-1):
                    keys(0, 3, bk0, t, -1)
                if t.has(2):
                    inverse(2, 0, t, 2)
                if t.has(1):
                    t.wait(ct1_hi, t.now(1))
                    nc.vector.tensor_tensor(CT1.lo[:], work[:, 2].rearrange("p (c k) -> p c k", c=C),
                                            CT1.hi[:].bitcast(F32), ALU.subtract).then_inc(ct1_lo, 1)
                if t.has(2):
                    inverse(2, 1, t, 2)
                if t.has(-1):
                    t.wait(v0_ps, t.now(-1))
                    t.wait(ot_ps[0], t.was(-1))
                    nc.vector.tensor_tensor(V[0][:], work[:, 0].rearrange("p (g d) -> p g d", g=G), both(row["bv0"]),
                                            ALU.add).then_inc(v0_sb, 1)
                if t.has(1):
                    normed(1, y1_ps, 3, X1[:], t, 1)
                if t.has(3):
                    t.wait(exp3, t.now(3))
                    nc.vector.reciprocal(RS3[:], SUM3[:]).then_inc(rs3_sb, 1)
                    t.wait(rs3_sb, t.now(3))
                    t.wait(o3_ps, t.now(3))
                    t.wait(out_stored, t.was(3), 16)
                    for g in range(G):
                        ins = nc.vector.scalar_tensor_tensor(out=OUT[:, g, :], in0=work[:, 0, g * D:(g + 1) * D],
                                                             scalar=RS3[:, g:g + 1], in1=X3[:, g, :],
                                                             op0=ALU.mult, op1=ALU.add)
                    ins.then_inc(out_sb, 1)
                if t.has(1):
                    scaled(1, t, 1)

            run(dve, turn, multiples=((2, 16), (0, 16), (-2, 16), (-3, 16), (1, 16 * R), (-2, 16 * R)))

        @block.gpsimd
        def _(pool):
            nc.gpsimd.memset(half[:], -0.5)
            nc.gpsimd.memset(ident[:], 0.0).then_inc(pool_const, 1)
            pool.wait_ge(pool_const, 1)
            nc.gpsimd.affine_select(out=ident[:], in_=ident[:], compare_op=ALU.not_equal, fill=1.0, base=0,
                                    pattern=[[-1, P]], channel_multiplier=1).then_inc(const_ready, 1)
            pool.wait_ge(small_in, 16 * N_SMALL)

            def both(r_):
                return r_[:].unsqueeze(1).to_broadcast([P, G, D])

            def probs(l, g, t, off):
                t.wait(rs_sb[l][g], t.now(off))
                nc.gpsimd.tensor_tensor(E[l][:, g], E[l][:, g],
                                        RS[l][:, g * H:(g + 1) * H].unsqueeze(2).to_broadcast([P, H, P]),
                                        ALU.mult).then_inc(prob[l][g], 1)

            def rstd(l, t, off):
                t.apart()
                t.wait(mv_sb[l], t.now(off))
                nc.gpsimd.tensor_scalar(VE[l][:], MV[l][:, :, 1], LN_EPS, None, ALU.add).then_inc(ve_sb[l], 1)
                t.wait(ve_sb[l], t.now(off))
                t.wait(z_sb[l], t.was(off))
                nc.gpsimd.tensor_tensor(RSTD[l][:], VE[l][:], half[:], ALU.pow).then_inc(rstd_sb[l], 1)

            def gamma(l, t, off):
                t.wait(z_sb[l], t.now(off))
                nc.gpsimd.tensor_tensor(Y[l][:], Y[l][:], both(row[f"gamma{l}"]), ALU.mult).then_inc(zg_sb[l], 1)

            def turn(t):
                if t.has(2):
                    t.wait(zg_sb[1], t.now(2))
                    t.wait(xt_ps[2], t.was(2))
                    t.wait(x3_sb, t.was(2))
                    nc.gpsimd.tensor_tensor(X2[:], Y[1][:], both(row["beta1"]), ALU.add).then_inc(x2_sb, 1)
                if t.has(0):
                    probs(0, 0, t, 0)
                if t.has(3):
                    t.apart()
                    t.wait(m3a_sb, t.now(3))
                    t.wait(u3_sb, t.was(3))
                    nc.gpsimd.tensor_scalar(M3[:], M3a[:], -1.0e9, None, ALU.mult).then_inc(m3_sb, 1)
                if t.has(0):
                    probs(0, 1, t, 0)
                    rstd(0, t, 0)
                if t.has(-1):
                    t.wait(x_in, t.now(-1), 16)
                    t.wait(y_sb[0], t.was(-1))
                    nc.gpsimd.tensor_tensor(X0b[:], X0[:], both(row["bo0"]), ALU.add).then_inc(x0b_sb, 1)
                if t.has(2):
                    probs(2, 0, t, 2)
                if t.has(0):
                    gamma(0, t, 0)
                if t.has(2):
                    probs(2, 1, t, 2)
                if t.has(0):
                    t.wait(zg_sb[0], t.now(0))
                    t.wait(xt_ps[1], t.was(0))
                    t.wait(ct1_ps, t.was(0))
                    t.wait(u1_sb, t.was(0))
                    t.wait(y_sb[1], t.was(0))
                    nc.gpsimd.tensor_tensor(X1[:], Y[0][:], both(row["beta0"]), ALU.add).then_inc(x1_sb, 1)
                if t.has(1):
                    rstd(1, t, 1)
                    gamma(1, t, 1)

            run(pool, turn, multiples=((2, 16),))


_INS = {
    "x": "x", "adj": "adj",
    "Wq0": "L0_gnn_Wq", "bq0": "L0_gnn_bq", "Wk0": "L0_gnn_Wk", "bk0": "L0_gnn_bk", "Wv0": "L0_gnn_Wv",
    "bv0": "L0_gnn_bv", "Wo0": "L0_gnn_Wo", "bo0": "L0_gnn_bo", "gamma0": "L0_gnn_gamma", "beta0": "L0_gnn_beta",
    "Wq1": "L1_gnn_Wq", "bq1": "L1_gnn_bq", "Wk1": "L1_gnn_Wk", "bk1": "L1_gnn_bk", "Wc1": "L1_gnn_Wc",
    "gamma1": "L1_gnn_gamma", "beta1": "L1_gnn_beta",
    "Wq2": "L2_gnn_W_q", "bq2": "L2_gnn_b_q", "Wk2": "L2_gnn_W_k", "bk2": "L2_gnn_b_k", "Wv2": "L2_gnn_W_v",
    "bv2": "L2_gnn_b_v", "w_g": "L2_gnn_w_g", "b_g": "L2_gnn_b_g",
    "fc3": "L3_gnn_fc_w", "bf3": "L3_gnn_fc_b", "q_w": "L3_gnn_q_w", "q_b": "L3_gnn_q_b",
    "k_w": "L3_gnn_k_w", "k_b": "L3_gnn_k_b",
}


def kernel(**inputs):
    import numpy as np
    import concourse.bacc as bacc
    from concourse.bass_utils import run_bass_kernel_spmd

    nc = bacc.Bacc("TRN2", target_bir_lowering=False, num_devices=1)
    arrays, aps = {}, {}
    for short, name in _INS.items():
        a = np.ascontiguousarray(inputs[name])
        if a.ndim == 0:
            a = a.reshape(1)
        arrays[f"in_{short}"] = a
        aps[short] = nc.dram_tensor(f"in_{short}", a.shape, mybir.dt.from_np(a.dtype), kind="ExternalInput").ap()
    out = nc.dram_tensor("out_0", aps["x"].shape, F32, kind="ExternalOutput").ap()
    build(nc, aps["x"], aps["adj"], aps, out)
    r = run_bass_kernel_spmd(nc, [arrays], core_ids=[0])
    return r.results[0]["out_0"]
```

```python
from contextlib import ExitStack

import concourse.bass as bass
from concourse import mybir

P = 128
D = 256
C = D // P
G = 2
H = 8
HD = D // H
R = P // HD
SLOTS = 8
LN_EPS = 1e-5
MASKED = -1.0e30
HUGE = 3.0e38

ALU = mybir.AluOpType
ACT = mybir.ActivationFunctionType
F32 = mybir.dt.float32
F32R = mybir.dt.float32r
AX_X = mybir.AxisListType.X

FIRST, LAST_EXTRA = -1, 3


def build(nc, x, adj, w, out):
    NP_ = x.shape[0] // G

    x_dram = x.rearrange("(u g) t d -> t u g d", g=G)
    adj_dram = adj.rearrange("(u g) q k -> q u g k", g=G)
    out_dram = out.rearrange("(u g) t d -> t u g d", g=G)

    with ExitStack() as ctx:
        def sb(name, *shape, dt=F32):
            return ctx.enter_context(nc.sbuf_tensor(name, [P, *shape], dt))

        def sem(name):
            return ctx.enter_context(nc.semaphore(name))

        def sems(*names):
            return [sem(n) for n in names]

        class Split:
            def __init__(self, name, *shape):
                self.hi = sb(name + "_hi", *shape, dt=F32R)
                self.lo = sb(name + "_lo", *shape, dt=F32R)

        score_ps = ctx.enter_context(nc.psum_tensor("score_ps", [P, G * C, R * P], F32))
        work = ctx.enter_context(nc.psum_tensor("work", [P, 4, 512], F32))

        wq0, wk0, wv0, wo0 = (Split(n, C, D) for n in ("wq0", "wk0", "wv0", "wo0"))
        wqk1 = Split("wqk1", C, D)
        wc1 = Split("wc1", C, D)
        wq2, wk2 = Split("wq2", C, D), Split("wk2", C, D)
        wv2 = Split("wv2", C, D + 2)
        wf3 = Split("wf3", C, D + 2)
        ident = sb("ident", P)
        ROWS = ("bv0", "bo0", "gamma0", "beta0", "gamma1", "beta1", "bv2", "bf3")
        row = {n: sb(n, D) for n in ROWS}
        wu1 = sb("wu1", D)
        COLUMNS = ("bq0", "bk0", "bq1", "bk1", "bq2", "bk2", "bf3")
        N_COL = C * len(COLUMNS) + 4 * C
        col_rows = sb("col_rows", P)
        cols = sb("cols", N_COL)
        bq0, bk0, bq1, bk1, bq2, bk2, bf3c = (cols[:, C * j:C * (j + 1)] for j in range(len(COLUMNS)))
        pairs_of = cols[:, C * len(COLUMNS):].rearrange("p (n c j) -> p n c j", n=2, c=C)
        qk3, wg2 = pairs_of[:, 0], pairs_of[:, 1]
        bq0s, bq2s = sb("bq0s", C), sb("bq2s", C)
        c1 = sb("c1", C)
        c0 = sb("c0", 1)
        bg2 = sb("bg2", 2)
        bqk3 = sb("bqk3", 2)
        add3 = sb("add3", 2)
        eps2 = sb("eps2", 1)
        count_only = sb("count_only", 16)
        half = sb("half", G)

        adjs = sb("adjs", SLOTS, G * P)
        X0, X0b = sb("X0", G, D), sb("X0b", G, D)
        X1, X2, X3 = sb("X1", G, D), sb("X2", G, D), sb("X3", G, D)
        OUT = sb("OUT", G, D)
        XT = [Split(f"XT{l}", C, G * P) for l in range(4)]
        X1T = sb("X1T", C, G * P)
        QT = {l: sb(f"QT{l}", C, G * P) for l in (0, 2)}
        KT = {l: sb(f"KT{l}", C, G * P) for l in (0, 2)}
        KD = {l: sb(f"KD{l}", G * C, R * P) for l in (0, 2)}
        V = {l: sb(f"V{l}", G, D) for l in (0, 2)}
        E = {l: sb(f"E{l}", G, H, P) for l in (0, 2)}
        ET = {l: sb(f"ET{l}", G, H, P) for l in (0, 2)}
        NM = {l: sb(f"NM{l}", G * H) for l in (0, 2)}
        SUM = {l: sb(f"SUM{l}", G * H) for l in (0, 2)}
        RS = {l: sb(f"RS{l}", G * H) for l in (0, 2)}
        BIAS0, LNADJ2, BIAS2 = sb("BIAS0", G * P), sb("LNADJ2", G * P), sb("BIAS2", G * P)
        OT0 = Split("OT0", C, G * P)
        OT2 = sb("OT2", C, G * P)
        Y = {l: sb(f"Y{l}", G, D) for l in (0, 1)}
        STAT = {l: sb(f"STAT{l}", G, 6) for l in (0, 1)}
        MV = {l: sb(f"MV{l}", G, 2) for l in (0, 1)}
        VE = {l: sb(f"VE{l}", G) for l in (0, 1)}
        RSTD = {l: sb(f"RSTD{l}", G) for l in (0, 1)}
        G1 = sb("G1", C, G * P)
        MASK1, BIAS1 = sb("MASK1", G * P), sb("BIAS1", G * P)
        U1, U1junk = sb("U1", G), sb("U1junk", G, D)
        E1, A1, A1T = sb("E1", G * P), sb("A1", G * P), sb("A1T", G * P)
        NM1, SUM1, RS1 = sb("NM1", G), sb("SUM1", G), sb("RS1", G)
        CT1 = Split("CT1", C, G * P)
        AC2 = sb("AC2", G, 2)
        F3 = sb("F3", G, D)
        QK3 = sb("QK3", G, 2)
        M3a, M3 = sb("M3a", G * P), sb("M3", G * P)
        U3, L3, E3, E3T = sb("U3", G * P), sb("L3", G * P), sb("E3", G * P), sb("E3T", G * P)
        NM3, SUM3, RS3 = sb("NM3", G), sb("SUM3", G), sb("RS3", G)
        stage = {n: t for n, t in zip(
            ("Wq0", "Wk0", "Wv0", "Wo0"),
            (ET[2].rearrange("p g h k -> p (g h k)")[:, j * 512:(j + 1) * 512].rearrange("p (c d) -> p c d", c=C)
             for j in range(4)))}
        stage.update({n: t for n, t in zip(
            ("Wq1", "Wk1", "Wc1", "fc3"),
            (E[2].rearrange("p g h k -> p (g h k)")[:, j * 512:(j + 1) * 512].rearrange("p (c d) -> p c d", c=C)
             for j in range(4)))})
        stage.update({n: t for n, t in zip(
            ("Wq2", "Wk2", "Wv2"),
            (ET[0].rearrange("p g h k -> p (g h k)")[:, j * 512:(j + 1) * 512].rearrange("p (c d) -> p c d", c=C)
             for j in range(3)))})
        wqT1 = E[0].rearrange("p g h k -> p (g h k)")[:, 0:512].rearrange("p (c d) -> p c d", c=C)
        wkT1 = E[0].rearrange("p g h k -> p (g h k)")[:, 512:1024].rearrange("p (c d) -> p c d", c=C)
        w_in = {n: sem("in_" + n) for n in stage}
        small_in = sem("small_in")
        pool_const, const_ready, dve_const = sems("pool_const", "const_ready", "dve_const")
        prep_pe, prep_hi, prep_lo, prep_plain = sems("prep_pe", "prep_hi", "prep_lo", "prep_plain")
        x_in, adj_in, out_stored = sems("x_in", "adj_in", "out_stored")
        xt_ps = sems("xt0_ps", "xt1_ps", "xt2_ps", "xt3_ps")
        q_ps = {0: sem("q0_ps"), 2: sem("q2_ps")}
        k_ps = {0: sem("k0_ps"), 2: sem("k2_ps")}
        v0_ps = sem("v0_ps")
        y_ps = sems("y0_ps", "y1_ps")
        f3_ps = sems("f3a_ps", "f3b_ps")
        v2_ps = sems("v2a_ps", "v2b_ps")
        s_ps = {0: sems("s0a_ps", "s0b_ps"), 2: sems("s2a_ps", "s2b_ps")}
        et_ps = {0: sems("et0a_ps", "et0b_ps"), 2: sems("et2a_ps", "et2b_ps")}
        ot_ps = {0: sems("ot0a_ps", "ot0b_ps"), 2: sems("ot2a_ps", "ot2b_ps")}
        g1_ps, s1_ps, a1t_ps, ct1_ps = sems("g1_ps", "s1_ps", "a1t_ps", "ct1_ps")
        c2_ps, o2_ps, k3_ps, e3t_ps, o3_ps = sems("c2_ps", "o2_ps", "k3_ps", "e3t_ps", "o3_ps")
        xt_hi = sems("xt0_hi", "xt1_hi", "xt2_hi", "xt3_hi")
        x1t_sb = sem("x1t_sb")
        q_sb = {0: sem("q0_sb"), 2: sem("q2_sb")}
        exp_all = {0: sems("exp0a", "exp0b"), 2: sems("exp2a", "exp2b")}
        et_sb = {0: sems("et0a_sb", "et0b_sb"), 2: sems("et2a_sb", "et2b_sb")}
        ot0_hi, ot2_sb, bias0_sb, lnadj2_sb, exp1, exp3, a1t_sb, e3t_sb, ct1_hi = sems(
            "ot0_hi", "ot2_sb", "bias0_sb", "lnadj2_sb", "exp1", "exp3", "a1t_sb", "e3t_sb", "ct1_hi")
        xt_lo = sems("xt0_lo", "xt1_lo", "xt2_lo", "xt3_lo")
        k_sb = {0: sem("k0_sb"), 2: sem("k2_sb")}
        keys_spread = {0: sem("keys0_spread"), 2: sem("keys2_spread")}
        v0_sb, clip0, x3_sb, u1_sb, g1_sb = sems("v0_sb", "clip0", "x3_sb", "u1_sb", "g1_sb")
        t_first = {0: sems("t0a_first", "t0b_first"), 2: sems("t2a_first", "t2b_first")}
        t_all = {0: sems("t0a_all", "t0b_all"), 2: sems("t2a_all", "t2b_all")}
        rs_sb = {0: sems("rs0a", "rs0b"), 2: sems("rs2a", "rs2b")}
        v2_sb = sems("v2a_sb", "v2b_sb")
        f3_sb = sems("f3a_sb", "f3b_sb")
        mask1_sb, nbias1_sb, bias1_sb, t1_all, rs1_sb, a1_sb = sems(
            "mask1_sb", "nbias1_sb", "bias1_sb", "t1_all", "rs1_sb", "a1_sb")
        bias2_sb, ot0_lo, ct1_lo, m3a_sb, u3_sb, l3_sb, nm3_sb, rs3_sb, out_sb = sems(
            "bias2_sb", "ot0_lo", "ct1_lo", "m3a_sb", "u3_sb", "l3_sb", "nm3_sb", "rs3_sb", "out_sb")
        y_sb, stat_sb, mv_sb, z_sb = ({l: sem(f"{n}{l}") for l in (0, 1)} for n in ("y_sb", "stat_sb", "mv_sb", "z_sb"))
        x0b_sb, x1_sb, x2_sb, m3_sb = sems("x0b_sb", "x1_sb", "x2_sb", "m3_sb")
        prob = {0: sems("prob0a", "prob0b"), 2: sems("prob2a", "prob2b")}
        ve_sb, rstd_sb, zg_sb = ({l: sem(f"{n}{l}") for l in (0, 1)} for n in ("ve_sb", "rstd_sb", "zg_sb"))

        bank_users = {
            0: [(0, [v0_sb]), (2, [k_sb[2]]), (1, [t1_all]), (1, [ct1_hi, ct1_lo]), (1, [y_sb[1]]), (2, [ot2_sb])],
            1: [(1, [x1t_sb]), (3, [f3_sb[0]]), (1, [g1_sb]), (2, [v2_sb[0]]), (-1, [xt_hi[0], xt_lo[0]]), (0,
                [y_sb[0]]), (-1, [q_sb[0]])],
            2: [(3, [xt_hi[3], xt_lo[3]]), (3, [f3_sb[1]]), (3, [u3_sb]), (2, [v2_sb[1]]), (2, [bias2_sb]), (0,
                [ot0_hi, ot0_lo])],
            3: [(3, [x3_sb]), (2, [xt_hi[2], xt_lo[2]]), (2, [q_sb[2]]), (3, [e3t_sb]), (1, [a1t_sb]), (-1,
                [k_sb[0]]), (3, [out_sb])],
            "scores0": [(0, [et_sb[0][0]]), (2, [t_all[2][0]]), (2, [et_sb[2][0]]), (-1, [t_all[0][0]])],
            "scores1": [(0, [t_all[0][1]]), (0, [et_sb[0][1]]), (2, [t_all[2][1]]), (2, [et_sb[2][1]])],
        }

        def by_chunk(bank):
            return work[:, bank].rearrange("p (c k) -> p c k", c=C)

        def by_graph(bank):
            return work[:, bank].rearrange("p (g d) -> p g d", g=G)

        SC = HD ** -0.5
        SC1 = D ** -0.5

        class Turn:
            def __init__(self, eng, i, multiples):
                self.eng, self.i, self.fixed = eng, i, isinstance(i, int)
                if not self.fixed:
                    for n in range(-3, 4):
                        eng.to_reg(self.count(n))
                    for n, by in multiples:
                        eng.to_reg(self.count(n) * by)

            def has(self, off):
                return not self.fixed or 0 <= self.i - off < NP_

            def count(self, n):
                return min(max(self.i + n, 0), NP_) if self.fixed else self.i + n

            def now(self, off):
                return self.count(1 - off)

            def was(self, off):
                return self.count(-off)

            def wait_ge(self, s, n, by=1):
                if self.fixed and n <= 0:
                    return
                self.eng.wait_ge(s, n * by)

            def first_and_last(self, bank, n):
                if self.fixed:
                    for k, (off, read) in enumerate(bank_users[bank]):
                        for s in read:
                            self.wait_ge(s, self.now(off) if k < n else self.was(off))

            def apart(self):
                if not self.fixed:
                    self.eng.wait_ge(const_ready, 1)

            def slot(self, off):
                k = (self.i - off) % SLOTS
                return adjs[:, k, :] if self.fixed else adjs[:, bass.ds(k, 1), :].rearrange("p a k -> p (a k)")

        def run(eng, turn, multiples=()):
            for i in range(FIRST, LAST_EXTRA + 1):
                turn(Turn(eng, i, multiples))
            with eng.Fori(LAST_EXTRA + 1, NP_ - 2) as i:
                turn(Turn(eng, i, multiples))
            for i in range(NP_ - 2, NP_ + LAST_EXTRA):
                turn(Turn(eng, i, multiples))

        TURNED = ["Wq0", "Wk0", "Wv0", "Wo0", "fc3", "Wq1", "Wk1"]
        STEPS = ["cols"] + TURNED + ["wqk1", "rows1", "cols3"]
        SPLIT_OF = {"Wq0": wq0, "Wk0": wk0, "Wv0": wv0, "Wo0": wo0, "fc3": wf3}
        NATURAL = [("Wc1", wc1), ("Wq2", wq2), ("Wk2", wk2), ("Wv2", wv2)]
        N_SMALL = len(ROWS) + len(COLUMNS) + 4 * C + 3

        block = ctx.enter_context(nc.Block())

        @block.sync
        def _(sp):
            sp.dma_start(X0[:], x_dram[:, 0]).then_inc(x_in, 16)
            sp.dma_start(adjs[:, 0, :].rearrange("p (g k) -> p g k", g=G), adj_dram[:, 0]).then_inc(adj_in, 16)
            for n in ("Wq0", "Wv0", "fc3", "Wk1", "Wq2", "Wv2"):
                sp.dma_start(stage[n], w[n].rearrange("(c p) d -> p c d", p=P)).then_inc(w_in[n], 16)
            for n in ROWS:
                sp.dma_start(row[n][:], w[n].rearrange("(a d) -> a d", a=1).to_broadcast([P, D])).then_inc(small_in, 16)

            sp.wait_ge(dve_const, 1)

            def spread(l):
                for r in range(R):
                    q = slice(r * HD, (r + 1) * HD)
                    sp.dma_start(KD[l][q, :, r * P:(r + 1) * P],
                                 KT[l][q].rearrange("p c (g k) -> p (c g) k", g=G)).then_inc(keys_spread[l], 16)

            def turn(t):
                if t.has(-1):
                    t.apart()
                    t.wait_ge(k_sb[0], t.now(-1))
                    t.wait_ge(s_ps[0][1], t.was(-1))
                    spread(0)
                if t.has(-2):
                    t.apart()
                    t.wait_ge(xt_ps[0], t.was(-2))
                    t.wait_ge(x0b_sb, t.was(-2))
                    t.wait_ge(x_in, t.was(-2), 16)
                    v = t.i + 2
                    x_src = x_dram[:, v] if t.fixed else x_dram[:, bass.ds(v, 1)].rearrange("t u g d -> t (u g) d")
                    sp.dma_start(X0[:], x_src).then_inc(x_in, 16)
                    t.apart()
                    t.wait_ge(adj_in, t.was(-2), 16)
                    t.wait_ge(lnadj2_sb, t.was(2))
                    t.wait_ge(m3a_sb, t.was(2))
                    a_src = adj_dram[:, v] if t.fixed else adj_dram[:, bass.ds(v, 1)].rearrange("q u g k -> q (u g) k")
                    sp.dma_start(t.slot(-2).rearrange("p (g k) -> p g k", g=G), a_src).then_inc(adj_in, 16)
                if t.has(3):
                    t.apart()
                    t.wait_ge(out_sb, t.now(3))
                    v = t.i - 3
                    dst = out_dram[:, v] if t.fixed else out_dram[:, bass.ds(v, 1)].rearrange("t u g d -> t (u g) d")
                    sp.dma_start(dst, OUT[:]).then_inc(out_stored, 16)
                if t.has(1):
                    t.apart()
                    t.wait_ge(k_sb[2], t.now(1))
                    t.wait_ge(s_ps[2][1], t.was(1))
                    spread(2)

            run(sp, turn, multiples=((2, 16),))
            sp.wait_ge(out_stored, 16 * NP_)

        @block.tensor
        def _(pe):
            def product(o, pairs):
                terms = [(a, b) for l, r in pairs for a, b in ((l[0], r[0]), (l[0], r[1]), (l[1], r[0]))]
                for n, (a, b) in enumerate(terms):
                    mm = nc.tensor.matmul(o, a, b, start=(n == 0), stop=(n == len(terms) - 1))
                return mm

            def cut(s, *idx):
                return s.hi[idx], s.lo[idx]

            pe.wait_ge(const_ready, 1)
            for n, name in enumerate(STEPS):
                bank = work[:, n % 4]
                if n >= 4:
                    pe.wait_ge(prep_hi, n - 3)
                    pe.wait_ge(prep_lo, n - 3)
                if name == "cols":
                    pe.wait_ge(small_in, 16 * N_SMALL)
                    mm = nc.tensor.transpose(bank[:, 0:N_COL], col_rows[0:N_COL, :], ident[0:N_COL, 0:N_COL])
                elif name in TURNED:
                    pe.wait_ge(w_in[name], 16)
                    for c in range(C):
                        for o in range(C):
                            mm = nc.tensor.transpose(bank[:, c * D + o * P:c * D + (o + 1) * P],
                                                     stage[name][:, o, c * P:(c + 1) * P], ident[:])
                elif name == "wqk1":
                    pe.wait_ge(prep_hi, n)
                    pe.wait_ge(prep_lo, n)
                    for m in range(C):
                        for e in range(C):
                            mm = nc.tensor.matmul(bank[:, m * D:(m + 1) * D], wqT1[:, e, m * P:(m + 1) * P],
                                                  wkT1[:, e, :], start=(e == 0), stop=(e == C - 1))
                elif name == "rows1":
                    for e in range(C):
                        nc.tensor.matmul(bank[:, 0:D], bk1[:, e:e + 1].to_broadcast([P, P]), wqT1[:, e, :],
                                         start=(e == 0), stop=(e == C - 1))
                    for e in range(C):
                        nc.tensor.matmul(bank[:, D:D + 1], bk1[:, e:e + 1].to_broadcast([P, P]), bq1[:, e:e + 1],
                                         start=(e == 0), stop=(e == C - 1))
                    for m in range(C):
                        for e in range(C):
                            mm = nc.tensor.matmul(bank[:, D + 2 + m:D + 3 + m], wkT1[:, e, m * P:(m + 1) * P],
                                                  bq1[:, e:e + 1], start=(e == 0), stop=(e == C - 1))
                else:
                    for c in range(C):
                        for o in range(C):
                            nc.tensor.matmul(bank[:, 2 * c:2 * c + 2], stage["fc3"][:, o, c * P:(c + 1) * P],
                                             qk3[:, o, :], start=(o == 0), stop=(o == C - 1))
                    for o in range(C):
                        mm = nc.tensor.matmul(bank[:, 4:6], bf3c[:, o:o + 1].to_broadcast([P, P]), qk3[:, o, :],
                                              start=(o == 0), stop=(o == C - 1))
                mm.then_inc(prep_pe, 1)
            pe.wait_ge(prep_hi, len(STEPS) + len(NATURAL) + 1)
            pe.wait_ge(prep_lo, len(STEPS) + len(NATURAL) + 1)

            def transpose_x(l, x_, bank):
                for g in range(G):
                    for c in range(C):
                        mm = nc.tensor.transpose(work[:, bank, c * G * P + g * P:c * G * P + (g + 1) * P],
                                                 x_[:, g, c * P:(c + 1) * P], ident[:])
                mm.then_inc(xt_ps[l], 1)

            def project_t(w_, l, bank):
                for m in range(C):
                    mm = product(work[:, bank, m * G * P:(m + 1) * G * P],
                                 [(cut(w_, slice(None), c, slice(m * P, (m + 1) * P)), cut(XT[l], slice(None), c))
                                  for c in range(C)])
                return mm

            def project(o, xt, g, w_):
                return product(o, [(cut(xt, slice(None), c, slice(g * P, (g + 1) * P)), cut(w_, slice(None), c))
                                   for c in range(C)])

            def scores(l, g):
                for m in range(C):
                    mm = nc.tensor.matmul(score_ps[:, g * C + m, :], QT[l][:, m, g * P:(g + 1) * P],
                                          KD[l][:, m * G + g, :], start=True, stop=True)
                mm.then_inc(s_ps[l][g], 1)

            def turn_probs(l, g):
                for h in range(H):
                    mm = nc.tensor.transpose(score_ps[:, 2 * g + h // R, (h % R) * P:(h % R + 1) * P],
                                             E[l][:, g, h, :], ident[:])
                mm.then_inc(et_ps[l][g], 1)

            def values(l, g, bank):
                for m in range(C):
                    for r in range(R):
                        h = m * R + r
                        mm = nc.tensor.matmul(work[r * HD:(r + 1) * HD, bank, m * G * P + g * P:m * G * P + (g + 1) * P],
                                              V[l][:, g, h * HD:(h + 1) * HD], ET[l][:, g, h, :], start=True, stop=True)
                mm.then_inc(ot_ps[l][g], 1)

            def turn(t):
                if t.has(0):
                    t.wait_ge(q_sb[0], t.now(0))
                    t.wait_ge(keys_spread[0], t.now(0), 16 * R)
                    t.wait_ge(et_sb[2][1], t.was(2))
                    t.first_and_last("scores1", 0)
                    scores(0, 1)
                if t.has(3):
                    t.wait_ge(ot2_sb, t.now(3))
                    t.wait_ge(out_sb, t.was(3))
                    t.first_and_last(3, 0)
                    for g in range(G):
                        for c in range(C):
                            mm = nc.tensor.transpose(work[:, 3, g * D + c * P:g * D + (c + 1) * P],
                                                     OT2[:, c, g * P:(g + 1) * P], ident[:])
                    mm.then_inc(o2_ps, 1)
                if t.has(0):
                    t.wait_ge(xt_lo[0], t.now(0))
                    t.wait_ge(ot2_sb, t.was(2))
                    t.first_and_last(0, 0)
                    for g in range(G):
                        mm = project(work[:, 0, g * D:(g + 1) * D], XT[0], g, wv0)
                    mm.then_inc(v0_ps, 1)
                if t.has(3):
                    t.wait_ge(x3_sb, t.now(3))
                    t.wait_ge(ot0_hi, t.was(0))
                    t.wait_ge(ot0_lo, t.was(0))
                    t.first_and_last(2, 0)
                    transpose_x(3, X3, 2)
                if t.has(1):
                    t.wait_ge(x1_sb, t.now(1))
                    t.wait_ge(q_sb[0], t.was(-1))
                    t.first_and_last(1, 0)
                    transpose_x(1, X1, 1)
                if t.has(2):
                    t.wait_ge(x2_sb, t.now(2))
                    t.wait_ge(x3_sb, t.now(3))
                    t.first_and_last(3, 1)
                    transpose_x(2, X2, 3)
                if t.has(3):
                    t.wait_ge(xt_lo[3], t.now(3))
                    t.wait_ge(x1t_sb, t.now(1))
                    t.first_and_last(1, 1)
                    project(work[:, 1, 0:D + 2], XT[3], 0, wf3).then_inc(f3_ps[0], 1)
                    t.wait_ge(xt_lo[3], t.now(3))
                    t.wait_ge(xt_hi[3], t.now(3))
                    t.first_and_last(2, 1)
                    project(work[:, 2, 0:D + 2], XT[3], 1, wf3).then_inc(f3_ps[1], 1)
                if t.has(2):
                    t.wait_ge(xt_lo[2], t.now(2))
                    t.wait_ge(v0_sb, t.now(0))
                    t.first_and_last(0, 1)
                    project_t(wk2, 2, 0).then_inc(k_ps[2], 1)
                if t.has(1):
                    t.wait_ge(xt_lo[1], t.now(1))
                    t.wait_ge(f3_sb[0], t.now(3))
                    t.first_and_last(1, 2)
                    project_t(wqk1, 1, 1).then_inc(g1_ps, 1)
                if t.has(3):
                    t.wait_ge(f3_sb[1], t.now(3))
                    t.first_and_last(2, 2)
                    for g in range(G):
                        mm = nc.tensor.transpose(work[:, 2, g * P:(g + 1) * P], QK3[:, g, 1:2].to_broadcast([P, P]), ident[:])
                    mm.then_inc(k3_ps, 1)
                if t.has(2):
                    t.wait_ge(xt_lo[2], t.now(2))
                    t.wait_ge(xt_hi[2], t.now(2))
                    t.first_and_last(3, 2)
                    project_t(wq2, 2, 3).then_inc(q_ps[2], 1)
                if t.has(0):
                    t.wait_ge(prob[0][0], t.now(0))
                    t.wait_ge(t_all[0][0], t.was(-1))
                    t.first_and_last("scores0", 0)
                    turn_probs(0, 0)
                if t.has(2):
                    t.wait_ge(xt_lo[2], t.now(2))
                    t.wait_ge(g1_sb, t.now(1))
                    t.first_and_last(1, 3)
                    project(work[:, 1, 0:D + 2], XT[2], 0, wv2).then_inc(v2_ps[0], 1)
                    t.wait_ge(xt_lo[2], t.now(2))
                    t.wait_ge(u3_sb, t.now(3))
                    t.first_and_last(2, 3)
                    project(work[:, 2, 0:D + 2], XT[2], 1, wv2).then_inc(v2_ps[1], 1)
                if t.has(1):
                    t.wait_ge(g1_sb, t.now(1))
                    t.wait_ge(x1t_sb, t.now(1))
                    t.wait_ge(k_sb[2], t.now(2))
                    t.first_and_last(0, 2)
                    for g in range(G):
                        for c in range(C):
                            mm = nc.tensor.matmul(work[:, 0, g * P:(g + 1) * P], G1[:, c, g * P:(g + 1) * P],
                                                  X1T[:, c, g * P:(g + 1) * P], start=(c == 0), stop=(c == C - 1))
                    mm.then_inc(s1_ps, 1)
                if t.has(0):
                    t.wait_ge(prob[0][1], t.now(0))
                    t.wait_ge(t_all[0][1], t.now(0))
                    t.first_and_last("scores1", 1)
                    turn_probs(0, 1)
                if t.has(2):
                    t.wait_ge(v2_sb[1], t.now(2))
                    t.first_and_last(2, 4)
                    for g in range(G):
                        mm = nc.tensor.transpose(work[:, 2, g * P:(g + 1) * P], AC2[:, g, 1:2].to_broadcast([P, P]), ident[:])
                    mm.then_inc(c2_ps, 1)
                if t.has(3):
                    t.wait_ge(exp3, t.now(3))
                    t.wait_ge(q_sb[2], t.now(2))
                    t.first_and_last(3, 3)
                    for g in range(G):
                        mm = nc.tensor.transpose(work[:, 3, g * P:(g + 1) * P], E3[:, g * P:(g + 1) * P], ident[:])
                    mm.then_inc(e3t_ps, 1)
                if t.has(2):
                    t.wait_ge(q_sb[2], t.now(2))
                    t.wait_ge(keys_spread[2], t.now(2), 16 * R)
                    t.wait_ge(et_sb[0][0], t.now(0))
                    t.first_and_last("scores0", 1)
                    scores(2, 0)
                if t.has(0):
                    t.wait_ge(et_sb[0][0], t.now(0))
                    t.wait_ge(v0_sb, t.now(0))
                    t.wait_ge(bias2_sb, t.now(2))
                    t.first_and_last(2, 5)
                    values(0, 0, 2)
                if t.has(-1):
                    t.wait_ge(x_in, t.now(-1), 16)
                    t.wait_ge(v2_sb[0], t.now(2))
                    t.first_and_last(1, 4)
                    transpose_x(0, X0, 1)
                if t.has(1):
                    t.wait_ge(a1_sb, t.now(1))
                    t.wait_ge(e3t_sb, t.now(3))
                    t.first_and_last(3, 4)
                    for g in range(G):
                        mm = nc.tensor.transpose(work[:, 3, g * P:(g + 1) * P], A1[:, g * P:(g + 1) * P], ident[:])
                    mm.then_inc(a1t_ps, 1)
                if t.has(0):
                    t.wait_ge(et_sb[0][1], t.now(0))
                    t.wait_ge(v0_sb, t.now(0))
                    values(0, 1, 2)
                if t.has(2):
                    t.wait_ge(q_sb[2], t.now(2))
                    t.wait_ge(keys_spread[2], t.now(2), 16 * R)
                    t.wait_ge(et_sb[0][1], t.now(0))
                    t.first_and_last("scores1", 2)
                    scores(2, 1)
                if t.has(0):
                    t.wait_ge(ot0_lo, t.now(0))
                    t.wait_ge(xt_hi[0], t.now(-1))
                    t.wait_ge(xt_lo[0], t.now(-1))
                    t.first_and_last(1, 5)
                    for g in range(G):
                        mm = project(work[:, 1, g * D:(g + 1) * D], OT0, g, wo0)
                    mm.then_inc(y_ps[0], 1)
                if t.has(-1):
                    t.wait_ge(xt_lo[0], t.now(-1))
                    t.wait_ge(a1t_sb, t.now(1))
                    t.first_and_last(3, 5)
                    project_t(wk0, 0, 3).then_inc(k_ps[0], 1)
                if t.has(1):
                    t.wait_ge(a1t_sb, t.now(1))
                    t.wait_ge(t1_all, t.now(1))
                    t.first_and_last(0, 3)
                    for g in range(G):
                        for c in range(C):
                            mm = nc.tensor.matmul(work[:, 0, c * G * P + g * P:c * G * P + (g + 1) * P],
                                                  X1[:, g, c * P:(c + 1) * P], A1T[:, g * P:(g + 1) * P], start=True, stop=True)
                    mm.then_inc(ct1_ps, 1)
                if t.has(-1):
                    t.wait_ge(xt_lo[0], t.now(-1))
                    t.wait_ge(y_sb[0], t.now(0))
                    t.first_and_last(1, 6)
                    project_t(wq0, 0, 1).then_inc(q_ps[0], 1)
                if t.has(2):
                    t.wait_ge(prob[2][0], t.now(2))
                    t.wait_ge(t_all[2][0], t.now(2))
                    t.first_and_last("scores0", 2)
                    turn_probs(2, 0)
                if t.has(3):
                    t.wait_ge(e3t_sb, t.now(3))
                    t.wait_ge(k_sb[0], t.now(-1))
                    t.first_and_last(3, 6)
                    for g in range(G):
                        mm = nc.tensor.matmul(work[:, 3, g * D:(g + 1) * D], E3T[:, g * P:(g + 1) * P], F3[:, g, :],
                                              start=True, stop=True)
                    mm.then_inc(o3_ps, 1)
                if t.has(1):
                    t.wait_ge(ct1_lo, t.now(1))
                    t.wait_ge(ct1_hi, t.now(1))
                    t.first_and_last(0, 4)
                    for g in range(G):
                        mm = project(work[:, 0, g * D:(g + 1) * D], CT1, g, wc1)
                    mm.then_inc(y_ps[1], 1)
                if t.has(2):
                    t.wait_ge(prob[2][1], t.now(2))
                    t.wait_ge(t_all[2][1], t.now(2))
                    t.first_and_last("scores1", 3)
                    turn_probs(2, 1)
                if t.has(-1):
                    t.wait_ge(q_sb[0], t.now(-1))
                    t.wait_ge(keys_spread[0], t.now(-1), 16 * R)
                    t.wait_ge(et_sb[2][0], t.now(2))
                    t.first_and_last("scores0", 3)
                    scores(0, 0)
                if t.has(2):
                    t.wait_ge(et_sb[2][0], t.now(2))
                    t.wait_ge(v2_sb[1], t.now(2))
                    t.wait_ge(y_sb[1], t.now(1))
                    t.first_and_last(0, 5)
                    values(2, 0, 0)
                    t.wait_ge(et_sb[2][1], t.now(2))
                    t.wait_ge(v2_sb[1], t.now(2))
                    values(2, 1, 0)

            run(pe, turn, multiples=((-1, 16 * R), (1, 16 * R), (2, 16), (2, 16 * R),))

        @block.scalar
        def _(act):
            nc.scalar.preload_act_table_set("natural_log_exp_and_others")
            for n in ("Wk0", "Wo0", "Wq1", "Wc1", "Wk2"):
                act.dma_start(stage[n], w[n].rearrange("(c p) d -> p c d", p=P)).then_inc(w_in[n], 16)
            for j, n in enumerate(COLUMNS):
                act.dma_start(col_rows[C * j:C * (j + 1), :], w[n].rearrange("(c p) -> c p", p=P)).then_inc(small_in, 16)
            for c in range(C):
                for j, v in enumerate((w["q_w"][0], w["k_w"][0], w["w_g"][0:D], w["w_g"][D:2 * D])):
                    n = C * len(COLUMNS) + 2 * C * (j // 2) + 2 * c + j % 2
                    act.dma_start(col_rows[n:n + 1, :], v[c * P:(c + 1) * P].rearrange("(a p) -> a p", a=1)).then_inc(small_in, 16)
            act.dma_start(bg2[:, 0:1], w["b_g"].to_broadcast([P, 1])).then_inc(small_in, 16)
            for n, j in (("q_b", 0), ("k_b", 1)):
                act.dma_start(bqk3[:, j:j + 1], w[n].to_broadcast([P, 1])).then_inc(small_in, 16)

            for n, name in enumerate(STEPS):
                act.wait_ge(prep_pe, n + 1)
                bank = work[:, n % 4]
                two = bank.rearrange("p (c d) -> p c d", c=C)
                if name == "cols":
                    ins = nc.scalar.activation(cols[:], bank[:, 0:N_COL], ACT.Copy)
                elif name in SPLIT_OF:
                    ins = nc.scalar.activation(SPLIT_OF[name].hi[:, :, 0:D], two, ACT.Copy)
                elif name == "Wq1":
                    ins = nc.scalar.activation(wqT1, two, ACT.Copy)
                elif name == "Wk1":
                    ins = nc.scalar.activation(wkT1, two, ACT.Copy)
                elif name == "wqk1":
                    ins = nc.scalar.activation(wqk1.hi[:], two, ACT.Copy, scale=SC1)
                elif name == "rows1":
                    nc.scalar.activation(wu1[:], bank[:, 0:D], ACT.Copy, scale=SC1)
                    nc.scalar.activation(c0[:], bank[:, D:D + 1], ACT.Copy, scale=SC1)
                    ins = nc.scalar.activation(c1[:], bank[:, D + 2:D + 2 + C], ACT.Copy, scale=SC1)
                else:
                    ins = nc.scalar.activation(wf3.hi[:, :, D:D + 2], bank[:, 0:4].rearrange("p (c j) -> p c j", c=C), ACT.Copy)
                ins.then_inc(prep_hi, 1)
            for name, s in NATURAL:
                act.wait_ge(w_in[name], 16)
                nc.scalar.activation(s.hi[:, :, 0:D], stage[name], ACT.Copy).then_inc(prep_hi, 1)
            act.wait_ge(prep_hi, 1)
            nc.scalar.activation(wv2.hi[:, :, D:D + 2], wg2, ACT.Copy).then_inc(prep_hi, 1)
            nc.scalar.activation(bq0s[:], bq0, ACT.Copy, scale=SC)
            nc.scalar.activation(bq2s[:], bq2, ACT.Copy, scale=SC).then_inc(prep_plain, 1)
            act.wait_ge(prep_plain, 1)
            act.wait_ge(prep_lo, len(STEPS) + len(NATURAL) + 1)
            act.wait_ge(dve_const, 1)

            def exps(l, g, a, b):
                for h in range(a, b):
                    j = g * H + h
                    ins = nc.scalar.activation(E[l][:, g, h, :], E[l][:, g, h, :], ACT.Exp, scale=-1.0,
                                               bias=NM[l][:, j:j + 1], accum_out=SUM[l][:, j:j + 1])
                return ins

            def queries(l, bank, b_):
                for m in range(C):
                    ins = nc.scalar.activation(QT[l][:, m, :], work[:, bank, m * G * P:(m + 1) * G * P],
                                               ACT.Identity, scale=SC, bias=b_[:, m:m + 1])
                ins.then_inc(q_sb[l], 1)

            def turned(l, g):
                nc.scalar.activation(ET[l][:, g].rearrange("p (m r) k -> p m (r k)", m=C),
                                     score_ps[:, 2 * g:2 * g + 2], ACT.Copy).then_inc(et_sb[l][g], 1)

            def turn(t):
                if t.has(3):
                    t.wait_ge(xt_ps[3], t.now(3))
                    t.wait_ge(f3_ps[1], t.was(3))
                    t.wait_ge(xt_lo[3], t.was(3))
                    nc.scalar.activation(XT[3].hi[:], by_chunk(2), ACT.Copy).then_inc(xt_hi[3], 1)
                if t.has(1):
                    t.wait_ge(xt_ps[1], t.now(1))
                    t.wait_ge(s1_ps, t.was(1))
                    t.wait_ge(xt_lo[1], t.was(1))
                    t.wait_ge(xt_hi[1], t.was(1))
                    nc.scalar.activation(X1T[:], by_chunk(1), ACT.Copy).then_inc(x1t_sb, 1)
                if t.has(2):
                    t.wait_ge(xt_ps[2], t.now(2))
                    t.wait_ge(v2_ps[1], t.was(2))
                    t.wait_ge(xt_lo[2], t.was(2))
                    nc.scalar.activation(XT[2].hi[:], by_chunk(3), ACT.Copy).then_inc(xt_hi[2], 1)
                if t.has(1):
                    t.wait_ge(x1t_sb, t.now(1))
                    t.wait_ge(g1_ps, t.was(1))
                    nc.scalar.activation(XT[1].hi[:], X1T[:], ACT.Copy).then_inc(xt_hi[1], 1)
                if t.has(0):
                    t.wait_ge(t_first[0][1], t.now(0))
                    t.wait_ge(rs_sb[0][1], t.was(0))
                    exps(0, 1, 0, R)
                    t.wait_ge(t_all[0][1], t.now(0))
                    exps(0, 1, R, H).then_inc(exp_all[0][1], 1)
                    t.wait_ge(et_ps[0][0], t.now(0))
                    t.wait_ge(ot_ps[0][0], t.was(0))
                    turned(0, 0)
                if t.has(2):
                    t.wait_ge(q_ps[2], t.now(2))
                    t.wait_ge(s_ps[2][1], t.was(2))
                    queries(2, 3, bq2s)
                    t.wait_ge(adj_in, t.now(2), 16)
                    t.wait_ge(bias2_sb, t.was(2))
                    nc.scalar.activation(LNADJ2[:], t.slot(2), ACT.Ln, bias=eps2[:]).then_inc(lnadj2_sb, 1)
                if t.has(3):
                    t.wait_ge(nm3_sb, t.now(3))
                    t.wait_ge(e3t_ps, t.was(3))
                    t.wait_ge(rs3_sb, t.was(3))
                    for g in range(G):
                        ins = nc.scalar.activation(E3[:, g * P:(g + 1) * P], L3[:, g * P:(g + 1) * P], ACT.Exp,
                                                   bias=NM3[:, g:g + 1], accum_out=SUM3[:, g:g + 1])
                    ins.then_inc(exp3, 1)
                if t.has(1):
                    t.wait_ge(t1_all, t.now(1))
                    t.wait_ge(a1_sb, t.was(1))
                    for g in range(G):
                        ins = nc.scalar.activation(E1[:, g * P:(g + 1) * P], E1[:, g * P:(g + 1) * P], ACT.Exp,
                                                   scale=-1.0, bias=NM1[:, g:g + 1], accum_out=SUM1[:, g:g + 1])
                    ins.then_inc(exp1, 1)
                if t.has(0):
                    t.wait_ge(et_ps[0][1], t.now(0))
                    t.wait_ge(ot_ps[0][1], t.was(0))
                    turned(0, 1)
                if t.has(3):
                    t.wait_ge(e3t_ps, t.now(3))
                    t.wait_ge(o3_ps, t.was(3))
                    nc.scalar.activation(E3T[:], work[:, 3, 0:G * P], ACT.Copy).then_inc(e3t_sb, 1)
                if t.has(-1):
                    t.wait_ge(clip0, t.now(-1))
                    t.wait_ge(t_all[0][1], t.was(-1))
                    nc.scalar.activation(BIAS0[:], BIAS0[:], ACT.Ln).then_inc(bias0_sb, 1)
                    t.wait_ge(xt_ps[0], t.now(-1))
                    t.wait_ge(v0_ps, t.was(-1))
                    t.wait_ge(xt_lo[0], t.was(-1))
                    nc.scalar.activation(XT[0].hi[:], by_chunk(1), ACT.Copy).then_inc(xt_hi[0], 1)
                if t.has(1):
                    t.wait_ge(a1t_ps, t.now(1))
                    t.wait_ge(ct1_ps, t.was(1))
                    nc.scalar.activation(A1T[:], work[:, 3, 0:G * P], ACT.Copy).then_inc(a1t_sb, 1)
                if t.has(0):
                    t.wait_ge(ot_ps[0][1], t.now(0))
                    t.wait_ge(y_ps[0], t.was(0))
                    t.wait_ge(ot0_lo, t.was(0))
                    nc.scalar.activation(OT0.hi[:], by_chunk(2), ACT.Copy).then_inc(ot0_hi, 1)
                if t.has(2):
                    t.wait_ge(t_first[2][0], t.now(2))
                    t.wait_ge(rs_sb[2][0], t.was(2))
                    exps(2, 0, 0, R)
                    t.wait_ge(t_all[2][0], t.now(2))
                    exps(2, 0, R, H).then_inc(exp_all[2][0], 1)
                    t.wait_ge(t_first[2][1], t.now(2))
                    t.wait_ge(rs_sb[2][1], t.was(2))
                    exps(2, 1, 0, R)
                    t.wait_ge(t_all[2][1], t.now(2))
                    exps(2, 1, R, H).then_inc(exp_all[2][1], 1)
                if t.has(1):
                    t.wait_ge(ct1_ps, t.now(1))
                    t.wait_ge(y_ps[1], t.was(1))
                    t.wait_ge(ct1_lo, t.was(1))
                    nc.scalar.activation(CT1.hi[:], by_chunk(0), ACT.Copy).then_inc(ct1_hi, 1)
                if t.has(2):
                    t.wait_ge(et_ps[2][0], t.now(2))
                    t.wait_ge(ot_ps[2][0], t.was(2))
                    turned(2, 0)
                if t.has(-1):
                    t.wait_ge(q_ps[0], t.now(-1))
                    t.wait_ge(s_ps[0][1], t.was(-1))
                    queries(0, 1, bq0s)
                if t.has(2):
                    t.wait_ge(et_ps[2][1], t.now(2))
                    t.wait_ge(ot_ps[2][1], t.was(2))
                    turned(2, 1)
                    t.wait_ge(ot_ps[2][1], t.now(2))
                    t.wait_ge(o2_ps, t.was(2))
                    nc.scalar.activation(OT2[:], by_chunk(0), ACT.Copy).then_inc(ot2_sb, 1)
                if t.has(-1):
                    t.wait_ge(t_first[0][0], t.now(-1))
                    t.wait_ge(rs_sb[0][0], t.was(-1))
                    exps(0, 0, 0, R)
                    t.wait_ge(t_all[0][0], t.now(-1))
                    exps(0, 0, R, H).then_inc(exp_all[0][0], 1)

            run(act, turn, multiples=((-1, 16),))

        @block.vector
        def _(dve):
            for l in (0, 2):
                nc.vector.memset(KD[l][:], 0.0)
            nc.vector.memset(eps2[:], 1e-9)
            nc.vector.memset(bg2[:, 1:2], 0.0).then_inc(dve_const, 1)

            def lower(s, src, hi_, scale=1.0):
                return nc.vector.scalar_tensor_tensor(out=s, in0=src, scalar=scale, in1=hi_.bitcast(F32),
                                                      op0=ALU.mult, op1=ALU.subtract)

            for n, name in enumerate(STEPS):
                dve.wait_ge(prep_hi, n + 1)
                bank = work[:, n % 4]
                two = bank.rearrange("p (c d) -> p c d", c=C)
                if name in SPLIT_OF:
                    s = SPLIT_OF[name]
                    lower(s.lo[:, :, 0:D], two, s.hi[:, :, 0:D]).then_inc(prep_lo, 1)
                elif name == "wqk1":
                    lower(wqk1.lo[:], two, wqk1.hi[:], SC1).then_inc(prep_lo, 1)
                elif name == "cols3":
                    lower(wf3.lo[:, :, D:D + 2], bank[:, 0:4].rearrange("p (c j) -> p c j", c=C), wf3.hi[:, :, D:D + 2])
                    dve.wait_ge(small_in, 16 * N_SMALL)
                    nc.vector.tensor_tensor(add3[:], bank[:, 4:6], bqk3[:], ALU.add).then_inc(prep_lo, 1)
                else:
                    nc.vector.memset(count_only[:, n:n + 1], 0.0).then_inc(prep_lo, 1)
            for n, (name, s) in enumerate(NATURAL):
                dve.wait_ge(prep_hi, len(STEPS) + n + 1)
                lower(s.lo[:, :, 0:D], stage[name], s.hi[:, :, 0:D]).then_inc(prep_lo, 1)
            dve.wait_ge(prep_hi, len(STEPS) + len(NATURAL) + 1)
            lower(wv2.lo[:, :, D:D + 2], wg2, wv2.hi[:, :, D:D + 2]).then_inc(prep_lo, 1)
            dve.wait_ge(prep_lo, len(STEPS) + len(NATURAL) + 1)
            dve.wait_ge(small_in, 16 * N_SMALL)

            def shifted(l, g, bias):
                for h in range(H):
                    m, r = divmod(h, R)
                    j = g * H + h
                    ins = nc.vector.tensor_tensor_reduce(
                        out=E[l][:, g, h, :], in0=score_ps[:, g * C + m, r * P:(r + 1) * P],
                        in1=bias[:, g * P:(g + 1) * P], scale=-1.0, scalar=HUGE, op0=ALU.add, op1=ALU.min,
                        accum_out=NM[l][:, j:j + 1])
                    if h == R - 1:
                        ins.then_inc(t_first[l][g], 1)
                ins.then_inc(t_all[l][g], 1)

            def inverse(l, g):
                nc.vector.reciprocal(RS[l][:, g * H:(g + 1) * H], SUM[l][:, g * H:(g + 1) * H]).then_inc(rs_sb[l][g], 1)

            def keys(l, bank, b_):
                for m in range(C):
                    ins = nc.vector.tensor_scalar(KT[l][:, m, :], work[:, bank, m * G * P:(m + 1) * G * P],
                                                  b_[:, m:m + 1], None, ALU.add)
                ins.then_inc(k_sb[l], 1)

            def both(r_):
                return r_[:].unsqueeze(1).to_broadcast([P, G, D])

            def turn(t):
                if t.has(2):
                    t.wait_ge(v2_ps[0], t.now(2))
                    t.wait_ge(ot_ps[2][0], t.was(2))
                    t.wait_ge(bias2_sb, t.was(2))
                    nc.vector.tensor_tensor(AC2[:, 0, :], work[:, 1, D:D + 2], bg2[:], ALU.add)
                    nc.vector.tensor_tensor(V[2][:, 0, :], work[:, 1, 0:D], row["bv2"][:], ALU.add).then_inc(v2_sb[0], 1)
                if t.has(1):
                    t.wait_ge(adj_in, t.now(1), 16)
                    t.wait_ge(u1_sb, t.now(1))
                    t.wait_ge(t1_all, t.was(1))
                    nc.vector.tensor_scalar(BIAS1[:], t.slot(1), 0.0, MASKED, ALU.is_equal, ALU.mult).then_inc(nbias1_sb, 1)
                    t.wait_ge(nbias1_sb, t.now(1))
                    for g in range(G):
                        ins = nc.vector.tensor_scalar(BIAS1[:, g * P:(g + 1) * P], BIAS1[:, g * P:(g + 1) * P],
                                                      U1[:, g:g + 1], c0[:, 0:1], ALU.add, ALU.add)
                    ins.then_inc(bias1_sb, 1)
                if t.has(2):
                    t.wait_ge(v2_ps[1], t.now(2))
                    t.wait_ge(ot_ps[2][1], t.was(2))
                    t.wait_ge(bias2_sb, t.was(2))
                    nc.vector.tensor_tensor(AC2[:, 1, :], work[:, 2, D:D + 2], bg2[:], ALU.add)
                    nc.vector.tensor_tensor(V[2][:, 1, :], work[:, 2, 0:D], row["bv2"][:], ALU.add).then_inc(v2_sb[1], 1)
                if t.has(1):
                    t.apart()
                    t.wait_ge(s1_ps, t.now(1))
                    t.wait_ge(bias1_sb, t.now(1))
                    t.wait_ge(a1_sb, t.was(1))
                    for g in range(G):
                        ins = nc.vector.tensor_tensor_reduce(
                            out=E1[:, g * P:(g + 1) * P], in0=work[:, 0, g * P:(g + 1) * P],
                            in1=BIAS1[:, g * P:(g + 1) * P], scale=-1.0, scalar=HUGE, op0=ALU.add, op1=ALU.min,
                            accum_out=NM1[:, g:g + 1])
                    ins.then_inc(t1_all, 1)
                if t.has(2):
                    t.wait_ge(c2_ps, t.now(2))
                    t.wait_ge(lnadj2_sb, t.now(2))
                    t.wait_ge(t_all[2][1], t.was(2))
                    for g in range(G):
                        ins = nc.vector.scalar_tensor_tensor(
                            out=BIAS2[:, g * P:(g + 1) * P], in0=work[:, 2, g * P:(g + 1) * P], scalar=AC2[:, g, 0:1],
                            in1=LNADJ2[:, g * P:(g + 1) * P], op0=ALU.add, op1=ALU.add)
                    ins.then_inc(bias2_sb, 1)
                if t.has(1):
                    t.wait_ge(adj_in, t.now(1), 16)
                    t.wait_ge(a1_sb, t.was(1))
                    nc.vector.tensor_scalar(MASK1[:], t.slot(1), 0.0, None, ALU.not_equal).then_inc(mask1_sb, 1)
                if t.has(3):
                    t.wait_ge(exp3, t.now(3))
                    t.wait_ge(out_sb, t.was(3))
                    nc.vector.reciprocal(RS3[:], SUM3[:]).then_inc(rs3_sb, 1)
                if t.has(1):
                    t.wait_ge(exp1, t.now(1))
                    t.wait_ge(mask1_sb, t.now(1))
                    t.wait_ge(a1t_ps, t.was(1))
                    nc.vector.reciprocal(RS1[:], SUM1[:]).then_inc(rs1_sb, 1)
                    t.wait_ge(rs1_sb, t.now(1))
                    for g in range(G):
                        ins = nc.vector.scalar_tensor_tensor(
                            out=A1[:, g * P:(g + 1) * P], in0=E1[:, g * P:(g + 1) * P], scalar=RS1[:, g:g + 1],
                            in1=MASK1[:, g * P:(g + 1) * P], op0=ALU.mult, op1=ALU.mult)
                    ins.then_inc(a1_sb, 1)
                if t.has(-1):
                    t.wait_ge(adj_in, t.now(-1), 16)
                    t.wait_ge(t_all[0][1], t.was(-1))
                    nc.vector.tensor_scalar(BIAS0[:], t.slot(-1), 1e-8, None, ALU.max).then_inc(clip0, 1)
                if t.has(2):
                    t.apart()
                    t.wait_ge(s_ps[2][0], t.now(2))
                    t.wait_ge(bias2_sb, t.now(2))
                    t.wait_ge(et_ps[2][0], t.was(2))
                    shifted(2, 0, BIAS2)
                if t.has(-1):
                    t.wait_ge(xt_hi[0], t.now(-1))
                    t.wait_ge(v0_ps, t.was(-1))
                    nc.vector.tensor_tensor(XT[0].lo[:], by_chunk(1), XT[0].hi[:].bitcast(F32),
                                            ALU.subtract).then_inc(xt_lo[0], 1)
                if t.has(0):
                    t.wait_ge(ot0_hi, t.now(0))
                    t.wait_ge(y_ps[0], t.was(0))
                    nc.vector.tensor_tensor(OT0.lo[:], by_chunk(2), OT0.hi[:].bitcast(F32),
                                            ALU.subtract).then_inc(ot0_lo, 1)
                if t.has(2):
                    t.apart()
                    t.wait_ge(s_ps[2][1], t.now(2))
                    t.wait_ge(t_all[2][0], t.now(2))
                    t.wait_ge(et_ps[2][1], t.was(2))
                    shifted(2, 1, BIAS2)
                if t.has(0):
                    t.wait_ge(y_ps[0], t.now(0))
                    t.wait_ge(x0b_sb, t.now(0))
                    t.wait_ge(x1_sb, t.was(0))
                    nc.vector.tensor_tensor(Y[0][:], by_graph(1), X0b[:], ALU.add).then_inc(y_sb[0], 1)
                if t.has(2):
                    t.wait_ge(exp_all[2][0], t.now(2))
                    t.wait_ge(prob[2][0], t.was(2))
                    inverse(2, 0)
                    t.wait_ge(adj_in, t.now(2), 16)
                    t.wait_ge(m3_sb, t.was(2))
                    nc.vector.tensor_scalar(M3a[:], t.slot(2), -1.0, 1.0, ALU.mult, ALU.add).then_inc(m3a_sb, 1)
                if t.has(0):
                    t.apart()
                    t.wait_ge(y_sb[0], t.now(0))
                    t.wait_ge(z_sb[0], t.was(0))
                    for g in range(G):
                        ins = nc.vector.bn_stats(STAT[0][:, g, :], Y[0][:, g, :])
                    ins.then_inc(stat_sb[0], 1)
                    t.apart()
                    t.wait_ge(stat_sb[0], t.now(0))
                    for g in range(G):
                        ins = nc.vector.bn_aggr(MV[0][:, g, :], STAT[0][:, g, :])
                    ins.then_inc(mv_sb[0], 1)
                if t.has(-1):
                    t.wait_ge(k_ps[0], t.now(-1))
                    t.wait_ge(keys_spread[0], t.was(-1), 16 * R)
                    keys(0, 3, bk0)
                if t.has(2):
                    t.wait_ge(exp_all[2][1], t.now(2))
                    t.wait_ge(prob[2][1], t.was(2))
                    inverse(2, 1)
                if t.has(1):
                    t.wait_ge(ct1_hi, t.now(1))
                    t.wait_ge(y_ps[1], t.was(1))
                    nc.vector.tensor_tensor(CT1.lo[:], by_chunk(0), CT1.hi[:].bitcast(F32),
                                            ALU.subtract).then_inc(ct1_lo, 1)
                if t.has(3):
                    t.wait_ge(o3_ps, t.now(3))
                    t.wait_ge(rs3_sb, t.now(3))
                    t.wait_ge(out_stored, t.was(3), 16)
                    for g in range(G):
                        ins = nc.vector.scalar_tensor_tensor(out=OUT[:, g, :], in0=work[:, 3, g * D:(g + 1) * D],
                                                             scalar=RS3[:, g:g + 1], in1=X3[:, g, :],
                                                             op0=ALU.mult, op1=ALU.add)
                    ins.then_inc(out_sb, 1)
                if t.has(0):
                    t.wait_ge(rstd_sb[0], t.now(0))
                    for g in range(G):
                        ins = nc.vector.tensor_scalar(Y[0][:, g, :], Y[0][:, g, :], MV[0][:, g, 0:1], RSTD[0][:, g:g + 1],
                                                      ALU.subtract, ALU.mult)
                    ins.then_inc(z_sb[0], 1)
                if t.has(1):
                    t.wait_ge(y_ps[1], t.now(1))
                    t.wait_ge(x1_sb, t.now(1))
                    t.wait_ge(x2_sb, t.was(1))
                    nc.vector.tensor_tensor(Y[1][:], by_graph(0), X1[:], ALU.add).then_inc(y_sb[1], 1)
                    t.apart()
                    t.wait_ge(y_sb[1], t.now(1))
                    t.wait_ge(z_sb[1], t.was(1))
                    for g in range(G):
                        ins = nc.vector.bn_stats(STAT[1][:, g, :], Y[1][:, g, :])
                    ins.then_inc(stat_sb[1], 1)
                    t.apart()
                    t.wait_ge(stat_sb[1], t.now(1))
                    for g in range(G):
                        ins = nc.vector.bn_aggr(MV[1][:, g, :], STAT[1][:, g, :])
                    ins.then_inc(mv_sb[1], 1)
                if t.has(-1):
                    t.apart()
                    t.wait_ge(s_ps[0][0], t.now(-1))
                    t.wait_ge(bias0_sb, t.now(-1))
                    t.wait_ge(et_ps[0][0], t.was(-1))
                    shifted(0, 0, BIAS0)
                if t.has(1):
                    t.wait_ge(rstd_sb[1], t.now(1))
                    for g in range(G):
                        ins = nc.vector.tensor_scalar(Y[1][:, g, :], Y[1][:, g, :], MV[1][:, g, 0:1], RSTD[1][:, g:g + 1],
                                                      ALU.subtract, ALU.mult)
                    ins.then_inc(z_sb[1], 1)
                if t.has(2):
                    t.wait_ge(o2_ps, t.now(2))
                    t.wait_ge(xt_ps[3], t.was(2))
                    t.wait_ge(out_sb, t.was(2))
                    nc.vector.tensor_tensor(X3[:], by_graph(3), X2[:], ALU.add).then_inc(x3_sb, 1)
                if t.has(-1):
                    t.apart()
                    t.wait_ge(s_ps[0][1], t.now(-1))
                    t.wait_ge(bias0_sb, t.now(-1))
                    t.wait_ge(t_all[0][0], t.now(-1))
                    t.wait_ge(et_ps[0][1], t.was(-1))
                    shifted(0, 1, BIAS0)
                    t.wait_ge(exp_all[0][0], t.now(-1))
                    t.wait_ge(prob[0][0], t.was(-1))
                    inverse(0, 0)
                if t.has(2):
                    t.wait_ge(xt_hi[3], t.now(2))
                    t.wait_ge(f3_ps[1], t.was(2))
                    nc.vector.tensor_tensor(XT[3].lo[:], by_chunk(2), XT[3].hi[:].bitcast(F32),
                                            ALU.subtract).then_inc(xt_lo[3], 1)
                if t.has(-1):
                    t.wait_ge(v0_ps, t.now(-1))
                    t.wait_ge(ot_ps[0][1], t.was(-1))
                    nc.vector.tensor_tensor(V[0][:], by_graph(0), both(row["bv0"]), ALU.add).then_inc(v0_sb, 1)
                if t.has(1):
                    t.wait_ge(xt_hi[2], t.now(1))
                    t.wait_ge(v2_ps[1], t.was(1))
                    nc.vector.tensor_tensor(XT[2].lo[:], by_chunk(3), XT[2].hi[:].bitcast(F32),
                                            ALU.subtract).then_inc(xt_lo[2], 1)
                if t.has(2):
                    t.wait_ge(f3_ps[0], t.now(2))
                    t.wait_ge(o3_ps, t.was(2))
                    t.wait_ge(u3_sb, t.was(2))
                    nc.vector.tensor_tensor(QK3[:, 0, :], work[:, 1, D:D + 2], add3[:], ALU.add)
                    nc.vector.tensor_tensor(F3[:, 0, :], work[:, 1, 0:D], row["bf3"][:], ALU.add).then_inc(f3_sb[0], 1)
                if t.has(0):
                    t.wait_ge(xt_hi[1], t.now(0))
                    t.wait_ge(g1_ps, t.was(0))
                    nc.vector.tensor_tensor(XT[1].lo[:], X1T[:], XT[1].hi[:].bitcast(F32), ALU.subtract).then_inc(xt_lo[1], 1)
                if t.has(2):
                    t.wait_ge(f3_ps[1], t.now(2))
                    t.wait_ge(o3_ps, t.was(2))
                    t.wait_ge(u3_sb, t.was(2))
                    nc.vector.tensor_tensor(QK3[:, 1, :], work[:, 2, D:D + 2], add3[:], ALU.add)
                    nc.vector.tensor_tensor(F3[:, 1, :], work[:, 2, 0:D], row["bf3"][:], ALU.add).then_inc(f3_sb[1], 1)
                if t.has(0):
                    t.wait_ge(x1_sb, t.now(0))
                    t.wait_ge(bias1_sb, t.was(0))
                    for g in range(G):
                        ins = nc.vector.tensor_tensor_reduce(
                            out=U1junk[:, g, :], in0=X1[:, g, :], in1=wu1[:], scale=1.0, scalar=0.0, op0=ALU.mult,
                            op1=ALU.add, accum_out=U1[:, g:g + 1])
                    ins.then_inc(u1_sb, 1)
                if t.has(-1):
                    t.wait_ge(exp_all[0][1], t.now(-1))
                    t.wait_ge(prob[0][1], t.was(-1))
                    inverse(0, 1)
                if t.has(0):
                    t.wait_ge(g1_ps, t.now(0))
                    t.wait_ge(s1_ps, t.was(0))
                    for m in range(C):
                        ins = nc.vector.tensor_scalar(G1[:, m, :], work[:, 1, m * G * P:(m + 1) * G * P], c1[:, m:m + 1],
                                                      None, ALU.add)
                    ins.then_inc(g1_sb, 1)
                if t.has(2):
                    t.wait_ge(k3_ps, t.now(2))
                    t.wait_ge(m3_sb, t.now(2))
                    t.wait_ge(nm3_sb, t.was(2))
                    for g in range(G):
                        ins = nc.vector.scalar_tensor_tensor(
                            out=U3[:, g * P:(g + 1) * P], in0=work[:, 2, g * P:(g + 1) * P], scalar=QK3[:, g, 0:1],
                            in1=M3[:, g * P:(g + 1) * P], op0=ALU.add, op1=ALU.add)
                    ins.then_inc(u3_sb, 1)
                if t.has(1):
                    t.wait_ge(k_ps[2], t.now(1))
                    t.wait_ge(keys_spread[2], t.was(1), 16 * R)
                    keys(2, 0, bk2)
                if t.has(2):
                    t.wait_ge(u3_sb, t.now(2))
                    t.wait_ge(exp3, t.was(2))
                    nc.vector.scalar_tensor_tensor(out=L3[:], in0=U3[:], scalar=0.01, in1=U3[:], op0=ALU.mult,
                                                   op1=ALU.max).then_inc(l3_sb, 1)
                    t.wait_ge(l3_sb, t.now(2))
                    nc.vector.tensor_reduce(NM3[:], L3[:].rearrange("p (g k) -> p g k", g=G), AX_X, ALU.max,
                                            negate=True).then_inc(nm3_sb, 1)

            run(dve, turn, multiples=((-3, 16), (-1, 16), (-1, 16 * R), (0, 16), (1, 16 * R), (2, 16),))

        @block.gpsimd
        def _(pool):
            nc.gpsimd.memset(half[:], -0.5)
            nc.gpsimd.memset(ident[:], 0.0).then_inc(pool_const, 1)
            pool.wait_ge(pool_const, 1)
            nc.gpsimd.affine_select(out=ident[:], in_=ident[:], compare_op=ALU.not_equal, fill=1.0, base=0,
                                    pattern=[[-1, P]], channel_multiplier=1).then_inc(const_ready, 1)
            pool.wait_ge(small_in, 16 * N_SMALL)

            def both(r_):
                return r_[:].unsqueeze(1).to_broadcast([P, G, D])

            def probs(l, g):
                nc.gpsimd.tensor_tensor(E[l][:, g], E[l][:, g],
                                        RS[l][:, g * H:(g + 1) * H].unsqueeze(2).to_broadcast([P, H, P]),
                                        ALU.mult).then_inc(prob[l][g], 1)

            def turn(t):
                if t.has(1):
                    t.apart()
                    t.wait_ge(mv_sb[1], t.now(1))
                    t.wait_ge(z_sb[1], t.was(1))
                    nc.gpsimd.tensor_scalar(VE[1][:], MV[1][:, :, 1], LN_EPS, None, ALU.add).then_inc(ve_sb[1], 1)
                    t.wait_ge(ve_sb[1], t.now(1))
                    nc.gpsimd.tensor_tensor(RSTD[1][:], VE[1][:], half[:], ALU.pow).then_inc(rstd_sb[1], 1)
                    t.wait_ge(z_sb[1], t.now(1))
                    nc.gpsimd.tensor_tensor(Y[1][:], Y[1][:], both(row["gamma1"]), ALU.mult).then_inc(zg_sb[1], 1)
                    t.wait_ge(zg_sb[1], t.now(1))
                    t.wait_ge(xt_ps[2], t.was(1))
                    t.wait_ge(x3_sb, t.was(1))
                    nc.gpsimd.tensor_tensor(X2[:], Y[1][:], both(row["beta1"]), ALU.add).then_inc(x2_sb, 1)
                if t.has(-1):
                    t.wait_ge(x_in, t.now(-1), 16)
                    t.wait_ge(y_sb[0], t.was(-1))
                    nc.gpsimd.tensor_tensor(X0b[:], X0[:], both(row["bo0"]), ALU.add).then_inc(x0b_sb, 1)
                    t.wait_ge(rs_sb[0][0], t.now(-1))
                    probs(0, 0)
                if t.has(2):
                    t.apart()
                    t.wait_ge(m3a_sb, t.now(2))
                    t.wait_ge(u3_sb, t.was(2))
                    nc.gpsimd.tensor_scalar(M3[:], M3a[:], -1.0e9, None, ALU.mult).then_inc(m3_sb, 1)
                if t.has(-1):
                    t.wait_ge(rs_sb[0][1], t.now(-1))
                    probs(0, 1)
                if t.has(1):
                    t.wait_ge(rs_sb[2][0], t.now(1))
                    probs(2, 0)
                if t.has(-1):
                    t.apart()
                    t.wait_ge(mv_sb[0], t.now(-1))
                    t.wait_ge(z_sb[0], t.was(-1))
                    nc.gpsimd.tensor_scalar(VE[0][:], MV[0][:, :, 1], LN_EPS, None, ALU.add).then_inc(ve_sb[0], 1)
                    t.wait_ge(ve_sb[0], t.now(-1))
                    nc.gpsimd.tensor_tensor(RSTD[0][:], VE[0][:], half[:], ALU.pow).then_inc(rstd_sb[0], 1)
                if t.has(1):
                    t.wait_ge(rs_sb[2][1], t.now(1))
                    probs(2, 1)
                if t.has(-1):
                    t.wait_ge(z_sb[0], t.now(-1))
                    nc.gpsimd.tensor_tensor(Y[0][:], Y[0][:], both(row["gamma0"]), ALU.mult).then_inc(zg_sb[0], 1)
                    t.wait_ge(zg_sb[0], t.now(-1))
                    t.wait_ge(ct1_ps, t.was(-1))
                    t.wait_ge(y_sb[1], t.was(-1))
                    nc.gpsimd.tensor_tensor(X1[:], Y[0][:], both(row["beta0"]), ALU.add).then_inc(x1_sb, 1)

            run(pool, turn, multiples=((2, 16),))


_INS = {
    "x": "x", "adj": "adj",
    "Wq0": "L0_gnn_Wq", "bq0": "L0_gnn_bq", "Wk0": "L0_gnn_Wk", "bk0": "L0_gnn_bk", "Wv0": "L0_gnn_Wv",
    "bv0": "L0_gnn_bv", "Wo0": "L0_gnn_Wo", "bo0": "L0_gnn_bo", "gamma0": "L0_gnn_gamma", "beta0": "L0_gnn_beta",
    "Wq1": "L1_gnn_Wq", "bq1": "L1_gnn_bq", "Wk1": "L1_gnn_Wk", "bk1": "L1_gnn_bk", "Wc1": "L1_gnn_Wc",
    "gamma1": "L1_gnn_gamma", "beta1": "L1_gnn_beta",
    "Wq2": "L2_gnn_W_q", "bq2": "L2_gnn_b_q", "Wk2": "L2_gnn_W_k", "bk2": "L2_gnn_b_k", "Wv2": "L2_gnn_W_v",
    "bv2": "L2_gnn_b_v", "w_g": "L2_gnn_w_g", "b_g": "L2_gnn_b_g",
    "fc3": "L3_gnn_fc_w", "bf3": "L3_gnn_fc_b", "q_w": "L3_gnn_q_w", "q_b": "L3_gnn_q_b",
    "k_w": "L3_gnn_k_w", "k_b": "L3_gnn_k_b",
}


def kernel(**inputs):
    import numpy as np
    import concourse.bacc as bacc
    from concourse.bass_utils import run_bass_kernel_spmd

    nc = bacc.Bacc("TRN2", target_bir_lowering=False, num_devices=1)
    arrays, aps = {}, {}
    for short, name in _INS.items():
        a = np.ascontiguousarray(inputs[name])
        if a.ndim == 0:
            a = a.reshape(1)
        arrays[f"in_{short}"] = a
        aps[short] = nc.dram_tensor(f"in_{short}", a.shape, mybir.dt.from_np(a.dtype), kind="ExternalInput").ap()
    out = nc.dram_tensor("out_0", aps["x"].shape, F32, kind="ExternalOutput").ap()
    build(nc, aps["x"], aps["adj"], aps, out)
    r = run_bass_kernel_spmd(nc, [arrays], core_ids=[0])
    return r.results[0]["out_0"]
```

```python
from contextlib import ExitStack

import concourse.bass as bass
from concourse import mybir

P = 128
D = 256
C = D // P
G = 2
H = 8
HD = D // H
R = P // HD
SLOTS = 8
LN_EPS = 1e-5
MASKED = -1.0e30
HUGE = 3.0e38

ALU = mybir.AluOpType
ACT = mybir.ActivationFunctionType
F32 = mybir.dt.float32
F32R = mybir.dt.float32r
AX_X = mybir.AxisListType.X

FIRST, LAST_EXTRA = -1, 3


def build(nc, x, adj, w, out):
    NP_ = x.shape[0] // G

    x_dram = x.rearrange("(u g) t d -> t u g d", g=G)
    adj_dram = adj.rearrange("(u g) q k -> q u g k", g=G)
    out_dram = out.rearrange("(u g) t d -> t u g d", g=G)

    with ExitStack() as ctx:
        def sb(name, *shape, dt=F32):
            return ctx.enter_context(nc.sbuf_tensor(name, [P, *shape], dt))

        def sem(name):
            return ctx.enter_context(nc.semaphore(name))

        def sems(*names):
            return [sem(n) for n in names]

        class Split:
            def __init__(self, name, *shape):
                self.hi = sb(name + "_hi", *shape, dt=F32R)
                self.lo = sb(name + "_lo", *shape, dt=F32R)

        class Joined:
            def __init__(self, name, *shape):
                self.both = sb(name, 2, *shape, dt=F32R)
                self.hi, self.lo = self.both[:, 0], self.both[:, 1]

        score_ps = ctx.enter_context(nc.psum_tensor("score_ps", [P, G * C, R * P], F32))
        work = ctx.enter_context(nc.psum_tensor("work", [P, 4, 512], F32))

        wq0, wk0, wv0, wo0 = (Split(n, C, D) for n in ("wq0", "wk0", "wv0", "wo0"))
        wqk1 = Split("wqk1", C, D)
        wc1 = Split("wc1", C, D)
        wq2, wk2 = Split("wq2", C, D), Split("wk2", C, D)
        wv2 = Split("wv2", C, D + 2)
        wf3 = Split("wf3", C, D + 2)
        ident = sb("ident", P)
        ROWS = ("bv0", "bo0", "gamma0", "beta0", "gamma1", "beta1", "bv2", "bf3")
        row = {n: sb(n, D) for n in ROWS}
        wu1 = sb("wu1", D)
        COLUMNS = ("bq0", "bk0", "bq1", "bk1", "bq2", "bk2", "bf3")
        N_COL = C * len(COLUMNS) + 4 * C
        col_rows = sb("col_rows", P)
        cols = sb("cols", N_COL)
        bq0, bk0, bq1, bk1, bq2, bk2, bf3c = (cols[:, C * j:C * (j + 1)] for j in range(len(COLUMNS)))
        pairs_of = cols[:, C * len(COLUMNS):].rearrange("p (n j c) -> p n c j", n=2, c=C)
        qk3, wg2 = pairs_of[:, 0], pairs_of[:, 1]
        bq0s, bq2s = sb("bq0s", C), sb("bq2s", C)
        c1 = sb("c1", C)
        c0 = sb("c0", 1)
        bg2 = sb("bg2", 2)
        bqk3 = sb("bqk3", 2)
        add3 = sb("add3", 2)
        eps2 = sb("eps2", 1)
        count_only = sb("count_only", 16)
        half = sb("half", G)

        adjs = sb("adjs", SLOTS, G * P)
        X0, X0b = sb("X0", G, D), sb("X0b", G, D)
        X1, X2, X3 = sb("X1", G, D), sb("X2", G, D), sb("X3", G, D)
        OUT = sb("OUT", G, D)
        XT = [Split(f"XT{l}", C, G * P) for l in range(4)]
        X1T = sb("X1T", C, G * P)
        QT = {l: Split(f"QT{l}", C, G * P) for l in (0, 2)}
        KT = Joined("KT", C, G * P)
        KD = Joined("KD", G * C, R * P)
        V = {l: sb(f"V{l}", G, D) for l in (0, 2)}
        E = {l: sb(f"E{l}", G, H, P) for l in (0, 2)}
        ET = {l: sb(f"ET{l}", G, H, P) for l in (0, 2)}
        NM = {l: sb(f"NM{l}", G * H) for l in (0, 2)}
        SUM = {l: sb(f"SUM{l}", G * H) for l in (0, 2)}
        RS = {l: sb(f"RS{l}", G * H) for l in (0, 2)}
        BIAS0, LNADJ2, BIAS2 = sb("BIAS0", G * P), sb("LNADJ2", G * P), sb("BIAS2", G * P)
        OT0 = Split("OT0", C, G * P)
        OT2 = sb("OT2", C, G * P)
        Y = {l: sb(f"Y{l}", G, D) for l in (0, 1)}
        STAT = {l: sb(f"STAT{l}", G, 6) for l in (0, 1)}
        MV = {l: sb(f"MV{l}", G, 2) for l in (0, 1)}
        VE = {l: sb(f"VE{l}", G) for l in (0, 1)}
        RSTD = {l: sb(f"RSTD{l}", G) for l in (0, 1)}
        G1 = sb("G1", C, G * P)
        MASK1, BIAS1 = sb("MASK1", G * P), sb("BIAS1", G * P)
        U1, U1junk = sb("U1", G), sb("U1junk", G, D)
        E1, A1, A1T = sb("E1", G * P), sb("A1", G * P), sb("A1T", G * P)
        NM1, SUM1, RS1 = sb("NM1", G), sb("SUM1", G), sb("RS1", G)
        CT1 = Split("CT1", C, G * P)
        AC2 = sb("AC2", G, 2)
        F3 = sb("F3", G, D)
        QK3 = sb("QK3", G, 2)
        M3 = sb("M3", G * P)
        U3, L3, E3, E3T = sb("U3", G * P), sb("L3", G * P), sb("E3", G * P), sb("E3T", G * P)
        NM3, SUM3, RS3 = sb("NM3", G), sb("SUM3", G), sb("RS3", G)
        stage = {n: t for n, t in zip(
            ("Wq0", "Wk0", "Wv0", "Wo0"),
            (ET[2].rearrange("p g h k -> p (g h k)")[:, j * 512:(j + 1) * 512].rearrange("p (c d) -> p c d", c=C)
             for j in range(4)))}
        stage.update({n: t for n, t in zip(
            ("Wq1", "Wk1", "Wc1", "fc3"),
            (E[2].rearrange("p g h k -> p (g h k)")[:, j * 512:(j + 1) * 512].rearrange("p (c d) -> p c d", c=C)
             for j in range(4)))})
        stage.update({n: t for n, t in zip(
            ("Wq2", "Wk2", "Wv2"),
            (ET[0].rearrange("p g h k -> p (g h k)")[:, j * 512:(j + 1) * 512].rearrange("p (c d) -> p c d", c=C)
             for j in range(3)))})
        wqT1 = E[0].rearrange("p g h k -> p (g h k)")[:, 0:512].rearrange("p (c d) -> p c d", c=C)
        wkT1 = E[0].rearrange("p g h k -> p (g h k)")[:, 512:1024].rearrange("p (c d) -> p c d", c=C)
        w_in = {n: sem("in_" + n) for n in stage}
        small_in, rows_in = sems("small_in", "rows_in")
        pool_const, const_ready, dve_const = sems("pool_const", "const_ready", "dve_const")
        prep_pe, prep_hi, prep_lo, prep_plain = sems("prep_pe", "prep_hi", "prep_lo", "prep_plain")
        x_in, adj_in, out_stored = sems("x_in", "adj_in", "out_stored")
        xt_ps = sems("xt0_ps", "xt1_ps", "xt2_ps", "xt3_ps")
        q_ps = {0: sem("q0_ps"), 2: sem("q2_ps")}
        k_ps = {0: sem("k0_ps"), 2: sem("k2_ps")}
        v0_ps = sem("v0_ps")
        y_ps = sems("y0_ps", "y1_ps")
        f3_ps = sems("f3a_ps", "f3b_ps")
        v2_ps = sems("v2a_ps", "v2b_ps")
        s_ps = {0: sems("s0a_ps", "s0b_ps"), 2: sems("s2a_ps", "s2b_ps")}
        et_ps = {0: sems("et0a_ps", "et0b_ps"), 2: sems("et2a_ps", "et2b_ps")}
        ot_ps = {0: sems("ot0a_ps", "ot0b_ps"), 2: sems("ot2a_ps", "ot2b_ps")}
        g1_ps, s1_ps, a1t_ps, ct1_ps = sems("g1_ps", "s1_ps", "a1t_ps", "ct1_ps")
        c2_ps, o2_ps, k3_ps, e3t_ps, o3_ps = sems("c2_ps", "o2_ps", "k3_ps", "e3t_ps", "o3_ps")
        xt_hi = sems("xt0_hi", "xt1_hi", "xt2_hi", "xt3_hi")
        x1t_sb = sem("x1t_sb")
        q_hi = {0: sem("q0_hi"), 2: sem("q2_hi")}
        k_hi = {0: sem("k0_hi"), 2: sem("k2_hi")}
        exp_all = {0: sems("exp0a", "exp0b"), 2: sems("exp2a", "exp2b")}
        et_sb = {0: sems("et0a_sb", "et0b_sb"), 2: sems("et2a_sb", "et2b_sb")}
        ot0_hi, ot2_sb, bias0_sb, lnadj2_sb, exp1, exp3, a1t_sb, e3t_sb, ct1_hi = sems(
            "ot0_hi", "ot2_sb", "bias0_sb", "lnadj2_sb", "exp1", "exp3", "a1t_sb", "e3t_sb", "ct1_hi")
        xt_lo = sems("xt0_lo", "xt1_lo", "xt2_lo", "xt3_lo")
        q_lo = {0: sem("q0_lo"), 2: sem("q2_lo")}
        k_lo = {0: sem("k0_lo"), 2: sem("k2_lo")}
        keys_spread = {0: sem("keys0_spread"), 2: sem("keys2_spread")}
        v0_sb, clip0, x3_sb, u1_sb, g1_sb = sems("v0_sb", "clip0", "x3_sb", "u1_sb", "g1_sb")
        t_first = {0: sems("t0a_first", "t0b_first"), 2: sems("t2a_first", "t2b_first")}
        t_all = {0: sems("t0a_all", "t0b_all"), 2: sems("t2a_all", "t2b_all")}
        rs_sb = {0: sems("rs0a", "rs0b"), 2: sems("rs2a", "rs2b")}
        v2_sb = sems("v2a_sb", "v2b_sb")
        f3_sb = sems("f3a_sb", "f3b_sb")
        mask1_sb, nbias1_sb, bias1_sb, t1_all, rs1_sb, a1_sb = sems(
            "mask1_sb", "nbias1_sb", "bias1_sb", "t1_all", "rs1_sb", "a1_sb")
        bias2_sb, ot0_lo, ct1_lo, u3_sb, l3_sb, nm3_sb, rs3_sb, out_sb = sems(
            "bias2_sb", "ot0_lo", "ct1_lo", "u3_sb", "l3_sb", "nm3_sb", "rs3_sb", "out_sb")
        y_sb, stat_sb, mv_sb, z_sb = ({l: sem(f"{n}{l}") for l in (0, 1)} for n in ("y_sb", "stat_sb", "mv_sb", "z_sb"))
        x0b_sb, x1_sb, x2_sb, m3_sb = sems("x0b_sb", "x1_sb", "x2_sb", "m3_sb")
        prob = {0: sems("prob0a", "prob0b"), 2: sems("prob2a", "prob2b")}
        ve_sb, rstd_sb, zg_sb = ({l: sem(f"{n}{l}") for l in (0, 1)} for n in ("ve_sb", "rstd_sb", "zg_sb"))

        bank_users = {
            0: [(2, [k_hi[2], k_lo[2]]), (2, [q_hi[2], q_lo[2]]), (0, [y_sb[0]]), (-1, [k_hi[0], k_lo[0]]), (2,
                [ot2_sb]), (2, [x3_sb]), (2, [xt_hi[3], xt_lo[3]])],
            1: [(2, [v2_sb[0]]), (1, [g1_sb]), (1, [t1_all]), (0, [ot0_hi, ot0_lo]), (-1, [q_hi[0], q_lo[0]]), (1,
                [xt_hi[2], xt_lo[2]])],
            2: [(3, [f3_sb[0]]), (3, [f3_sb[1]]), (3, [u3_sb]), (2, [bias2_sb]), (1, [a1t_sb]), (3, [e3t_sb]), (3,
                [out_sb])],
            3: [(2, [v2_sb[1]]), (-1, [xt_hi[0], xt_lo[0]]), (1, [ct1_hi, ct1_lo]), (1, [y_sb[1]]), (-1, [v0_sb]),
                (0, [x1t_sb])],
            "scores0": [(0, [et_sb[0][0]]), (2, [t_all[2][0]]), (2, [et_sb[2][0]]), (-1, [t_all[0][0]])],
            "scores1": [(0, [et_sb[0][1]]), (2, [t_all[2][1]]), (2, [et_sb[2][1]]), (-1, [t_all[0][1]])],
            "KD": [(-1, [s_ps[0][0], s_ps[0][1]]), (1, [s_ps[2][0], s_ps[2][1]])],
            "KT": [(-1, [k_lo[0], (keys_spread[0], 16 * R)]), (1, [k_lo[2], (keys_spread[2], 16 * R)])],
        }

        def by_chunk(bank):
            return work[:, bank].rearrange("p (c k) -> p c k", c=C)

        def by_graph(bank):
            return work[:, bank].rearrange("p (g d) -> p g d", g=G)

        def turned(l, g):
            return ET[l][:, g].rearrange("p (m r) k -> p m (r k)", m=C)

        SC = HD ** -0.5
        SC1 = D ** -0.5

        class Turn:
            def __init__(self, eng, i, multiples):
                self.eng, self.i, self.fixed = eng, i, isinstance(i, int)
                if not self.fixed:
                    for n in range(-3, 4):
                        eng.to_reg(self.count(n))
                    for n, by in multiples:
                        eng.to_reg(self.count(n) * by)

            def has(self, off):
                return not self.fixed or 0 <= self.i - off < NP_

            def count(self, n):
                return min(max(self.i + n, 0), NP_) if self.fixed else self.i + n

            def now(self, off):
                return self.count(1 - off)

            def was(self, off):
                return self.count(-off)

            def wait_ge(self, s, n, by=1):
                if self.fixed and n <= 0:
                    return
                self.eng.wait_ge(s, n * by)

            def first_and_last(self, bank, n):
                if self.fixed:
                    for k, (off, read) in enumerate(bank_users[bank]):
                        for s in read:
                            s, by = s if isinstance(s, tuple) else (s, 1)
                            self.wait_ge(s, self.now(off) if k < n else self.was(off), by)

            def apart(self):
                if not self.fixed:
                    self.eng.wait_ge(const_ready, 1)

            def slot(self, off):
                k = (self.i - off) % SLOTS
                return adjs[:, k, :] if self.fixed else adjs[:, bass.ds(k, 1), :].rearrange("p a k -> p (a k)")

        def run(eng, turn, multiples=()):
            for i in range(FIRST, LAST_EXTRA + 1):
                turn(Turn(eng, i, multiples))
            with eng.Fori(LAST_EXTRA + 1, NP_ - 2) as i:
                turn(Turn(eng, i, multiples))
            for i in range(NP_ - 2, NP_ + LAST_EXTRA):
                turn(Turn(eng, i, multiples))

        TURNED = ["Wq0", "Wk0", "Wv0", "Wo0", "fc3", "Wq1", "Wk1"]
        STEPS = TURNED + ["cols", "wqk1", "rows1", "cols3"]
        SCALE_OF = {"Wq0": HD ** -0.5, "Wq2": HD ** -0.5}
        SPLIT_OF = {"Wq0": wq0, "Wk0": wk0, "Wv0": wv0, "Wo0": wo0, "fc3": wf3}
        NATURAL = [("Wc1", wc1), ("Wq2", wq2), ("Wk2", wk2), ("Wv2", wv2)]
        N_SMALL, N_ROWS = len(COLUMNS) + 3, len(ROWS) + 3

        block = ctx.enter_context(nc.Block())

        @block.sync
        def _(sp):
            sp.dma_start(X0[:], x_dram[:, 0]).then_inc(x_in, 16)
            sp.dma_start(adjs[:, 0, :].rearrange("p (g k) -> p g k", g=G), adj_dram[:, 0]).then_inc(adj_in, 16)
            for n in ("Wq0", "Wv0", "fc3", "Wk1", "Wq2", "Wv2"):
                sp.dma_start(stage[n], w[n].rearrange("(c p) d -> p c d", p=P)).then_inc(w_in[n], 16)

            sp.wait_ge(dve_const, 1)

            def spread(l):
                for r in range(R):
                    q = slice(r * HD, (r + 1) * HD)
                    sp.dma_start(KD.both[q, :, :, r * P:(r + 1) * P].bitcast(F32).rearrange("p s n k -> p (s n) k"),
                                 KT.both[q].bitcast(F32).rearrange("p s c (g k) -> p (s c g) k", g=G)
                                 ).then_inc(keys_spread[l], 16)

            def turn(t):
                if t.has(-1):
                    t.apart()
                    t.wait_ge(k_lo[0], t.now(-1))
                    t.wait_ge(s_ps[2][1], t.was(1))
                    t.first_and_last("KD", 0)
                    spread(0)
                if t.has(1):
                    t.apart()
                    t.wait_ge(k_lo[2], t.now(1))
                    t.wait_ge(s_ps[0][1], t.now(-1))
                    t.first_and_last("KD", 1)
                    spread(2)
                if t.has(-2):
                    t.apart()
                    t.wait_ge(xt_ps[0], t.was(-2))
                    t.wait_ge(x0b_sb, t.was(-2))
                    t.wait_ge(x_in, t.was(-2), 16)
                    v = t.i + 2
                    x_src = x_dram[:, v] if t.fixed else x_dram[:, bass.ds(v, 1)].rearrange("t u g d -> t (u g) d")
                    sp.dma_start(X0[:], x_src).then_inc(x_in, 16)
                    t.apart()
                    t.wait_ge(adj_in, t.was(-2), 16)
                    t.wait_ge(lnadj2_sb, t.was(0))
                    t.wait_ge(m3_sb, t.was(1))
                    t.wait_ge(mask1_sb, t.was(0))
                    t.wait_ge(nbias1_sb, t.was(0))
                    a_src = adj_dram[:, v] if t.fixed else adj_dram[:, bass.ds(v, 1)].rearrange("q u g k -> q (u g) k")
                    sp.dma_start(t.slot(-2).rearrange("p (g k) -> p g k", g=G), a_src).then_inc(adj_in, 16)
                if t.has(3):
                    t.apart()
                    t.wait_ge(out_sb, t.now(3))
                    v = t.i - 3
                    dst = out_dram[:, v] if t.fixed else out_dram[:, bass.ds(v, 1)].rearrange("t u g d -> t (u g) d")
                    sp.dma_start(dst, OUT[:]).then_inc(out_stored, 16)

            run(sp, turn, multiples=((2, 16),))
            sp.wait_ge(out_stored, 16 * NP_)

        @block.tensor
        def _(pe):
            def product(o, pairs):
                terms = [(a, b) for l, r in pairs for a, b in ((l[0], r[0]), (l[0], r[1]), (l[1], r[0]))]
                for n, (a, b) in enumerate(terms):
                    mm = nc.tensor.matmul(o, a, b, start=(n == 0), stop=(n == len(terms) - 1))
                return mm

            def cut(s, *idx):
                return s.hi[idx], s.lo[idx]

            pe.wait_ge(const_ready, 1)
            for n, name in enumerate(STEPS):
                bank = work[:, n % 4]
                if n >= 4:
                    pe.wait_ge(prep_hi, n - 3)
                    pe.wait_ge(prep_lo, n - 3)
                if name == "cols":
                    pe.wait_ge(small_in, 16 * N_SMALL)
                    mm = nc.tensor.transpose(bank[:, 0:N_COL], col_rows[0:N_COL, :], ident[0:N_COL, 0:N_COL])
                elif name in TURNED:
                    pe.wait_ge(w_in[name], 16)
                    for c in range(C):
                        for o in range(C):
                            mm = nc.tensor.transpose(bank[:, c * D + o * P:c * D + (o + 1) * P],
                                                     stage[name][:, o, c * P:(c + 1) * P], ident[:])
                elif name == "wqk1":
                    pe.wait_ge(prep_hi, n)
                    pe.wait_ge(prep_lo, n)
                    for m in range(C):
                        for e in range(C):
                            mm = nc.tensor.matmul(bank[:, m * D:(m + 1) * D], wqT1[:, e, m * P:(m + 1) * P],
                                                  wkT1[:, e, :], start=(e == 0), stop=(e == C - 1))
                elif name == "rows1":
                    for e in range(C):
                        nc.tensor.matmul(bank[:, 0:D], bk1[:, e:e + 1].to_broadcast([P, P]), wqT1[:, e, :],
                                         start=(e == 0), stop=(e == C - 1))
                    for e in range(C):
                        nc.tensor.matmul(bank[:, D:D + 1], bk1[:, e:e + 1].to_broadcast([P, P]), bq1[:, e:e + 1],
                                         start=(e == 0), stop=(e == C - 1))
                    for m in range(C):
                        for e in range(C):
                            mm = nc.tensor.matmul(bank[:, D + 2 + m:D + 3 + m], wkT1[:, e, m * P:(m + 1) * P],
                                                  bq1[:, e:e + 1], start=(e == 0), stop=(e == C - 1))
                else:
                    for c in range(C):
                        for o in range(C):
                            nc.tensor.matmul(bank[:, 2 * c:2 * c + 2], stage["fc3"][:, o, c * P:(c + 1) * P],
                                             qk3[:, o, :], start=(o == 0), stop=(o == C - 1))
                    for o in range(C):
                        mm = nc.tensor.matmul(bank[:, 4:6], bf3c[:, o:o + 1].to_broadcast([P, P]), qk3[:, o, :],
                                              start=(o == 0), stop=(o == C - 1))
                mm.then_inc(prep_pe, 1)
            pe.wait_ge(prep_hi, len(STEPS) + len(NATURAL) + 1)
            pe.wait_ge(prep_lo, len(STEPS) + len(NATURAL) + 1)

            def transpose_x(l, x_, bank):
                for g in range(G):
                    for c in range(C):
                        mm = nc.tensor.transpose(work[:, bank, c * G * P + g * P:c * G * P + (g + 1) * P],
                                                 x_[:, g, c * P:(c + 1) * P], ident[:])
                mm.then_inc(xt_ps[l], 1)

            def project_t(w_, l, bank):
                for m in range(C):
                    mm = product(work[:, bank, m * G * P:(m + 1) * G * P],
                                 [(cut(w_, slice(None), c, slice(m * P, (m + 1) * P)), cut(XT[l], slice(None), c))
                                  for c in range(C)])
                return mm

            def project(o, xt, g, w_):
                return product(o, [(cut(xt, slice(None), c, slice(g * P, (g + 1) * P)), cut(w_, slice(None), c))
                                   for c in range(C)])

            def scores(l, g):
                for m in range(C):
                    mm = product(score_ps[:, g * C + m, :],
                                 [(cut(QT[l], slice(None), m, slice(g * P, (g + 1) * P)), cut(KD, slice(None), m * G + g))])
                mm.then_inc(s_ps[l][g], 1)

            def turn_probs(l, g):
                for h in range(H):
                    mm = nc.tensor.transpose(score_ps[:, 2 * g + h // R, (h % R) * P:(h % R + 1) * P],
                                             E[l][:, g, h, :], ident[:])
                mm.then_inc(et_ps[l][g], 1)

            def values(l, g, bank):
                for m in range(C):
                    for r in range(R):
                        h = m * R + r
                        mm = nc.tensor.matmul(work[r * HD:(r + 1) * HD, bank, m * G * P + g * P:m * G * P + (g + 1) * P],
                                              V[l][:, g, h * HD:(h + 1) * HD], ET[l][:, g, h, :], start=True, stop=True)
                mm.then_inc(ot_ps[l][g], 1)

            def turn(t):
                if t.has(3):
                    t.wait_ge(xt_lo[3], t.now(3))
                    t.wait_ge(out_sb, t.was(3))
                    t.first_and_last(2, 0)
                    project(work[:, 2, 0:D + 2], XT[3], 0, wf3).then_inc(f3_ps[0], 1)
                if t.has(2):
                    t.wait_ge(xt_lo[2], t.now(2))
                    t.wait_ge(xt_lo[3], t.was(2))
                    t.first_and_last(0, 0)
                    project_t(wk2, 2, 0).then_inc(k_ps[2], 1)
                    t.first_and_last(1, 0)
                    project(work[:, 1, 0:D + 2], XT[2], 0, wv2).then_inc(v2_ps[0], 1)
                    t.wait_ge(x1t_sb, t.was(0))
                    t.first_and_last(3, 0)
                    project(work[:, 3, 0:D + 2], XT[2], 1, wv2).then_inc(v2_ps[1], 1)
                if t.has(3):
                    t.wait_ge(f3_sb[0], t.now(3))
                    t.first_and_last(2, 1)
                    project(work[:, 2, 0:D + 2], XT[3], 1, wf3).then_inc(f3_ps[1], 1)
                if t.has(1):
                    t.wait_ge(xt_lo[1], t.now(1))
                    t.wait_ge(v2_sb[0], t.now(2))
                    t.first_and_last(1, 1)
                    project_t(wqk1, 1, 1).then_inc(g1_ps, 1)
                if t.has(3):
                    t.wait_ge(f3_sb[1], t.now(3))
                    t.first_and_last(2, 2)
                    for g in range(G):
                        mm = nc.tensor.transpose(work[:, 2, g * P:(g + 1) * P], QK3[:, g, 1:2].to_broadcast([P, P]), ident[:])
                    mm.then_inc(k3_ps, 1)
                if t.has(2):
                    t.wait_ge(k_lo[2], t.now(2))
                    t.first_and_last(0, 1)
                    project_t(wq2, 2, 0).then_inc(q_ps[2], 1)
                    t.wait_ge(v2_sb[1], t.now(2))
                    t.wait_ge(u3_sb, t.now(3))
                    t.first_and_last(2, 3)
                    for g in range(G):
                        mm = nc.tensor.transpose(work[:, 2, g * P:(g + 1) * P], AC2[:, g, 1:2].to_broadcast([P, P]), ident[:])
                    mm.then_inc(c2_ps, 1)
                if t.has(0):
                    t.wait_ge(prob[0][0], t.now(0))
                    t.first_and_last("scores0", 0)
                    turn_probs(0, 0)
                if t.has(1):
                    t.wait_ge(g1_sb, t.now(1))
                    t.first_and_last(1, 2)
                    for g in range(G):
                        for c in range(C):
                            mm = nc.tensor.matmul(work[:, 1, g * P:(g + 1) * P], G1[:, c, g * P:(g + 1) * P],
                                                  X1T[:, c, g * P:(g + 1) * P], start=(c == 0), stop=(c == C - 1))
                    mm.then_inc(s1_ps, 1)
                if t.has(0):
                    t.wait_ge(prob[0][1], t.now(0))
                    t.first_and_last("scores1", 0)
                    turn_probs(0, 1)
                if t.has(2):
                    t.wait_ge(q_lo[2], t.now(2))
                    t.wait_ge(keys_spread[2], t.now(2), 16 * R)
                    t.wait_ge(et_sb[0][0], t.now(0))
                    t.first_and_last("scores0", 1)
                    scores(2, 0)
                if t.has(0):
                    t.wait_ge(et_sb[0][0], t.now(0))
                    t.wait_ge(v0_sb, t.now(0))
                    t.wait_ge(t1_all, t.now(1))
                    t.first_and_last(1, 3)
                    values(0, 0, 1)
                if t.has(1):
                    t.wait_ge(a1_sb, t.now(1))
                    t.wait_ge(bias2_sb, t.now(2))
                    t.first_and_last(2, 4)
                    for g in range(G):
                        mm = nc.tensor.transpose(work[:, 2, g * P:(g + 1) * P], A1[:, g * P:(g + 1) * P], ident[:])
                    mm.then_inc(a1t_ps, 1)
                if t.has(-1):
                    t.wait_ge(x_in, t.now(-1), 16)
                    t.wait_ge(v2_sb[1], t.now(2))
                    t.first_and_last(3, 1)
                    transpose_x(0, X0, 3)
                if t.has(0):
                    t.wait_ge(et_sb[0][1], t.now(0))
                    values(0, 1, 1)
                if t.has(2):
                    t.wait_ge(et_sb[0][1], t.now(0))
                    t.first_and_last("scores1", 1)
                    scores(2, 1)
                if t.has(3):
                    t.wait_ge(exp3, t.now(3))
                    t.wait_ge(a1t_sb, t.now(1))
                    t.first_and_last(2, 5)
                    for g in range(G):
                        mm = nc.tensor.transpose(work[:, 2, g * P:(g + 1) * P], E3[:, g * P:(g + 1) * P], ident[:])
                    mm.then_inc(e3t_ps, 1)
                if t.has(0):
                    t.wait_ge(ot0_lo, t.now(0))
                    t.wait_ge(q_lo[2], t.now(2))
                    t.first_and_last(0, 2)
                    for g in range(G):
                        mm = project(work[:, 0, g * D:(g + 1) * D], OT0, g, wo0)
                    mm.then_inc(y_ps[0], 1)
                if t.has(-1):
                    t.wait_ge(xt_lo[0], t.now(-1))
                    t.wait_ge(ot0_lo, t.now(0))
                    t.first_and_last(1, 4)
                    project_t(wq0, 0, 1).then_inc(q_ps[0], 1)
                if t.has(1):
                    t.wait_ge(a1t_sb, t.now(1))
                    t.wait_ge(xt_lo[0], t.now(-1))
                    t.first_and_last(3, 2)
                    for g in range(G):
                        for c in range(C):
                            mm = nc.tensor.matmul(work[:, 3, c * G * P + g * P:c * G * P + (g + 1) * P],
                                                  X1[:, g, c * P:(c + 1) * P], A1T[:, g * P:(g + 1) * P], start=True, stop=True)
                    mm.then_inc(ct1_ps, 1)
                if t.has(-1):
                    t.wait_ge(y_sb[0], t.now(0))
                    t.first_and_last(0, 3)
                    project_t(wk0, 0, 0).then_inc(k_ps[0], 1)
                if t.has(2):
                    t.wait_ge(prob[2][0], t.now(2))
                    t.first_and_last("scores0", 2)
                    turn_probs(2, 0)
                if t.has(1):
                    t.wait_ge(ct1_lo, t.now(1))
                    t.first_and_last(3, 3)
                    for g in range(G):
                        mm = project(work[:, 3, g * D:(g + 1) * D], CT1, g, wc1)
                    mm.then_inc(y_ps[1], 1)
                if t.has(2):
                    t.wait_ge(et_sb[2][0], t.now(2))
                    t.wait_ge(k_lo[0], t.now(-1))
                    t.first_and_last(0, 4)
                    values(2, 0, 0)
                    t.wait_ge(prob[2][1], t.now(2))
                    t.first_and_last("scores1", 2)
                    turn_probs(2, 1)
                if t.has(3):
                    t.wait_ge(e3t_sb, t.now(3))
                    t.first_and_last(2, 6)
                    for g in range(G):
                        mm = nc.tensor.matmul(work[:, 2, g * D:(g + 1) * D], E3T[:, g * P:(g + 1) * P], F3[:, g, :],
                                              start=True, stop=True)
                    mm.then_inc(o3_ps, 1)
                if t.has(2):
                    t.wait_ge(et_sb[2][1], t.now(2))
                    values(2, 1, 0)
                if t.has(-1):
                    t.wait_ge(y_sb[1], t.now(1))
                    t.first_and_last(3, 4)
                    for g in range(G):
                        mm = project(work[:, 3, g * D:(g + 1) * D], XT[0], g, wv0)
                    mm.then_inc(v0_ps, 1)
                if t.has(2):
                    t.wait_ge(ot2_sb, t.now(2))
                    t.first_and_last(0, 5)
                    for g in range(G):
                        for c in range(C):
                            mm = nc.tensor.transpose(work[:, 0, g * D + c * P:g * D + (c + 1) * P],
                                                     OT2[:, c, g * P:(g + 1) * P], ident[:])
                    mm.then_inc(o2_ps, 1)
                if t.has(-1):
                    t.wait_ge(q_lo[0], t.now(-1))
                    t.wait_ge(keys_spread[0], t.now(-1), 16 * R)
                    t.wait_ge(et_sb[2][0], t.now(2))
                    t.first_and_last("scores0", 3)
                    scores(0, 0)
                if t.has(2):
                    t.wait_ge(x3_sb, t.now(2))
                    t.first_and_last(0, 6)
                    transpose_x(3, X3, 0)
                if t.has(0):
                    t.wait_ge(x1_sb, t.now(0))
                    t.wait_ge(v0_sb, t.now(-1))
                    t.first_and_last(3, 5)
                    transpose_x(1, X1, 3)
                if t.has(1):
                    t.wait_ge(x2_sb, t.now(1))
                    t.wait_ge(q_lo[0], t.now(-1))
                    t.first_and_last(1, 5)
                    transpose_x(2, X2, 1)
                if t.has(-1):
                    t.wait_ge(et_sb[2][1], t.now(2))
                    t.first_and_last("scores1", 3)
                    scores(0, 1)

            run(pe, turn, multiples=((-1, 16 * R), (2, 16), (2, 16 * R),))

        @block.scalar
        def _(act):
            nc.scalar.preload_act_table_set("natural_log_exp_and_others")
            for n in ("Wk0", "Wo0", "Wq1", "Wc1", "Wk2"):
                act.dma_start(stage[n], w[n].rearrange("(c p) d -> p c d", p=P)).then_inc(w_in[n], 16)
            for j, n in enumerate(COLUMNS):
                act.dma_start(col_rows[C * j:C * (j + 1), :], w[n].rearrange("(c p) -> c p", p=P)).then_inc(small_in, 16)
            for n, v in ((C * len(COLUMNS), w["q_w"][0]), (C * (len(COLUMNS) + 1), w["k_w"][0]),
                         (C * (len(COLUMNS) + 2), w["w_g"])):
                k = v.shape[0] // P
                act.dma_start(col_rows[n:n + k, :], v.rearrange("(c p) -> c p", p=P)).then_inc(small_in, 16)

            for n, name in enumerate(STEPS):
                act.wait_ge(prep_pe, n + 1)
                bank = work[:, n % 4]
                two = bank.rearrange("p (c d) -> p c d", c=C)
                if name == "cols":
                    ins = nc.scalar.activation(cols[:], bank[:, 0:N_COL], ACT.Copy)
                elif name in SPLIT_OF:
                    ins = nc.scalar.activation(SPLIT_OF[name].hi[:, :, 0:D], two, ACT.Copy,
                                               scale=SCALE_OF.get(name, 1.0))
                elif name == "Wq1":
                    ins = nc.scalar.activation(wqT1, two, ACT.Copy)
                elif name == "Wk1":
                    ins = nc.scalar.activation(wkT1, two, ACT.Copy)
                elif name == "wqk1":
                    ins = nc.scalar.activation(wqk1.hi[:], two, ACT.Copy, scale=SC1)
                elif name == "rows1":
                    nc.scalar.activation(wu1[:], bank[:, 0:D], ACT.Copy, scale=SC1)
                    nc.scalar.activation(c0[:], bank[:, D:D + 1], ACT.Copy, scale=SC1)
                    ins = nc.scalar.activation(c1[:], bank[:, D + 2:D + 2 + C], ACT.Copy, scale=SC1)
                else:
                    ins = nc.scalar.activation(wf3.hi[:, :, D:D + 2], bank[:, 0:4].rearrange("p (c j) -> p c j", c=C), ACT.Copy)
                ins.then_inc(prep_hi, 1)
            for name, s in NATURAL:
                act.wait_ge(w_in[name], 16)
                nc.scalar.activation(s.hi[:, :, 0:D], stage[name], ACT.Copy,
                                     scale=SCALE_OF.get(name, 1.0)).then_inc(prep_hi, 1)
            act.wait_ge(prep_hi, STEPS.index("cols") + 1)
            nc.scalar.activation(wv2.hi[:, :, D:D + 2], wg2, ACT.Copy).then_inc(prep_hi, 1)
            nc.scalar.activation(bq0s[:], bq0, ACT.Copy, scale=SC)
            nc.scalar.activation(bq2s[:], bq2, ACT.Copy, scale=SC).then_inc(prep_plain, 1)
            act.wait_ge(prep_plain, 1)
            act.wait_ge(prep_lo, len(STEPS) + len(NATURAL) + 1)
            act.wait_ge(dve_const, 1)

            def exps(l, g, a, b):
                for h in range(a, b):
                    j = g * H + h
                    ins = nc.scalar.activation(E[l][:, g, h, :], E[l][:, g, h, :], ACT.Exp, scale=-1.0,
                                               bias=NM[l][:, j:j + 1], accum_out=SUM[l][:, j:j + 1])
                return ins

            def biased_hi(s, bank, b_):
                for m in range(C):
                    ins = nc.scalar.activation(s.hi[:, m, :], work[:, bank, m * G * P:(m + 1) * G * P],
                                               ACT.Identity, bias=b_[:, m:m + 1])
                return ins

            def turn(t):
                if t.has(1):
                    t.wait_ge(t1_all, t.now(1))
                    t.wait_ge(a1_sb, t.was(1))
                    for g in range(G):
                        ins = nc.scalar.activation(E1[:, g * P:(g + 1) * P], E1[:, g * P:(g + 1) * P], ACT.Exp,
                                                   scale=-1.0, bias=NM1[:, g:g + 1], accum_out=SUM1[:, g:g + 1])
                    ins.then_inc(exp1, 1)
                if t.has(0):
                    t.wait_ge(et_ps[0][1], t.now(0))
                    t.wait_ge(ot_ps[0][1], t.was(0))
                    nc.scalar.activation(turned(0, 1), score_ps[:, 2:4], ACT.Copy).then_inc(et_sb[0][1], 1)
                if t.has(3):
                    t.wait_ge(nm3_sb, t.now(3))
                    t.wait_ge(e3t_ps, t.was(3))
                    t.wait_ge(rs3_sb, t.was(3))
                    for g in range(G):
                        ins = nc.scalar.activation(E3[:, g * P:(g + 1) * P], L3[:, g * P:(g + 1) * P], ACT.Exp,
                                                   bias=NM3[:, g:g + 1], accum_out=SUM3[:, g:g + 1])
                    ins.then_inc(exp3, 1)
                if t.has(1):
                    t.wait_ge(a1t_ps, t.now(1))
                    t.wait_ge(ct1_ps, t.was(1))
                    nc.scalar.activation(A1T[:], work[:, 2, 0:G * P], ACT.Copy).then_inc(a1t_sb, 1)
                if t.has(-1):
                    t.wait_ge(xt_ps[0], t.now(-1))
                    t.wait_ge(v0_ps, t.was(-1))
                    nc.scalar.activation(XT[0].hi[:], by_chunk(3), ACT.Copy).then_inc(xt_hi[0], 1)
                if t.has(0):
                    t.wait_ge(ot_ps[0][1], t.now(0))
                    t.wait_ge(y_ps[0], t.was(0))
                    nc.scalar.activation(OT0.hi[:], by_chunk(1), ACT.Copy).then_inc(ot0_hi, 1)
                if t.has(2):
                    t.wait_ge(t_first[2][0], t.now(2))
                    t.wait_ge(rs_sb[2][0], t.was(2))
                    exps(2, 0, 0, R)
                    t.wait_ge(t_all[2][0], t.now(2))
                    exps(2, 0, R, H).then_inc(exp_all[2][0], 1)
                    t.wait_ge(t_first[2][1], t.now(2))
                    t.wait_ge(rs_sb[2][1], t.was(2))
                    exps(2, 1, 0, R)
                    t.wait_ge(t_all[2][1], t.now(2))
                    exps(2, 1, R, H).then_inc(exp_all[2][1], 1)
                if t.has(-1):
                    t.wait_ge(k_ps[0], t.now(-1))
                    t.wait_ge(keys_spread[2], t.was(1), 16 * R)
                    t.first_and_last("KT", 0)
                    biased_hi(KT, 0, bk0).then_inc(k_hi[0], 1)
                if t.has(2):
                    t.wait_ge(et_ps[2][0], t.now(2))
                    t.wait_ge(ot_ps[2][0], t.was(2))
                    nc.scalar.activation(turned(2, 0), score_ps[:, 0:2], ACT.Copy).then_inc(et_sb[2][0], 1)
                if t.has(-1):
                    t.wait_ge(clip0, t.now(-1))
                    t.wait_ge(t_all[0][1], t.was(-1))
                    nc.scalar.activation(BIAS0[:], BIAS0[:], ACT.Ln).then_inc(bias0_sb, 1)
                    t.wait_ge(q_ps[0], t.now(-1))
                    biased_hi(QT[0], 1, bq0s).then_inc(q_hi[0], 1)
                if t.has(3):
                    t.wait_ge(e3t_ps, t.now(3))
                    t.wait_ge(o3_ps, t.was(3))
                    nc.scalar.activation(E3T[:], work[:, 2, 0:G * P], ACT.Copy).then_inc(e3t_sb, 1)
                if t.has(2):
                    t.wait_ge(et_ps[2][1], t.now(2))
                    t.wait_ge(ot_ps[2][1], t.was(2))
                    nc.scalar.activation(turned(2, 1), score_ps[:, 2:4], ACT.Copy).then_inc(et_sb[2][1], 1)
                    t.wait_ge(ot_ps[2][1], t.now(2))
                    t.wait_ge(o2_ps, t.was(2))
                    nc.scalar.activation(OT2[:], by_chunk(0), ACT.Copy).then_inc(ot2_sb, 1)
                    t.wait_ge(xt_ps[3], t.now(2))
                    t.wait_ge(f3_ps[1], t.was(2))
                    nc.scalar.activation(XT[3].hi[:], by_chunk(0), ACT.Copy).then_inc(xt_hi[3], 1)
                if t.has(0):
                    t.wait_ge(xt_ps[1], t.now(0))
                    t.wait_ge(s1_ps, t.was(0))
                    nc.scalar.activation(X1T[:], by_chunk(3), ACT.Copy).then_inc(x1t_sb, 1)
                if t.has(1):
                    t.wait_ge(xt_ps[2], t.now(1))
                    t.wait_ge(q_ps[2], t.was(1))
                    nc.scalar.activation(XT[2].hi[:], by_chunk(1), ACT.Copy).then_inc(xt_hi[2], 1)
                if t.has(-1):
                    t.wait_ge(t_first[0][0], t.now(-1))
                    t.wait_ge(rs_sb[0][0], t.was(-1))
                    exps(0, 0, 0, R)
                    t.wait_ge(t_all[0][0], t.now(-1))
                    exps(0, 0, R, H).then_inc(exp_all[0][0], 1)
                if t.has(1):
                    t.wait_ge(k_ps[2], t.now(1))
                    t.wait_ge(keys_spread[0], t.now(-1), 16 * R)
                    t.first_and_last("KT", 1)
                    biased_hi(KT, 0, bk2).then_inc(k_hi[2], 1)
                if t.has(-1):
                    t.wait_ge(t_first[0][1], t.now(-1))
                    t.wait_ge(rs_sb[0][1], t.was(-1))
                    exps(0, 1, 0, R)
                    t.wait_ge(t_all[0][1], t.now(-1))
                    exps(0, 1, R, H).then_inc(exp_all[0][1], 1)
                if t.has(0):
                    t.wait_ge(g1_ps, t.now(0))
                    for m in range(C):
                        ins = nc.scalar.activation(G1[:, m, :], work[:, 1, m * G * P:(m + 1) * G * P], ACT.Identity,
                                                   bias=c1[:, m:m + 1])
                    ins.then_inc(g1_sb, 1)
                if t.has(1):
                    t.wait_ge(q_ps[2], t.now(1))
                    t.wait_ge(s_ps[2][1], t.was(1))
                    biased_hi(QT[2], 0, bq2s).then_inc(q_hi[2], 1)
                if t.has(0):
                    t.wait_ge(adj_in, t.now(0), 16)
                    t.wait_ge(bias2_sb, t.was(0))
                    nc.scalar.activation(LNADJ2[:], t.slot(0), ACT.Ln, bias=eps2[:]).then_inc(lnadj2_sb, 1)
                if t.has(-1):
                    t.wait_ge(et_ps[0][0], t.now(-1))
                    t.wait_ge(ot_ps[0][0], t.was(-1))
                    nc.scalar.activation(turned(0, 0), score_ps[:, 0:2], ACT.Copy).then_inc(et_sb[0][0], 1)

            run(act, turn, multiples=((-1, 16 * R), (1, 16), (2, 16 * R),))

        @block.vector
        def _(dve):
            nc.vector.memset(KD.both[:].bitcast(F32), 0.0)
            nc.vector.memset(eps2[:], 1e-9)
            nc.vector.memset(bg2[:, 1:2], 0.0).then_inc(dve_const, 1)

            def lower(s, src, hi_, scale=1.0):
                return nc.vector.scalar_tensor_tensor(out=s, in0=src, scalar=scale, in1=hi_.bitcast(F32),
                                                      op0=ALU.mult, op1=ALU.subtract)

            for n, name in enumerate(STEPS):
                dve.wait_ge(prep_hi, n + 1)
                bank = work[:, n % 4]
                two = bank.rearrange("p (c d) -> p c d", c=C)
                if name in SPLIT_OF:
                    s = SPLIT_OF[name]
                    lower(s.lo[:, :, 0:D], two, s.hi[:, :, 0:D], SCALE_OF.get(name, 1.0)).then_inc(prep_lo, 1)
                elif name == "wqk1":
                    lower(wqk1.lo[:], two, wqk1.hi[:], SC1).then_inc(prep_lo, 1)
                elif name == "cols3":
                    lower(wf3.lo[:, :, D:D + 2], bank[:, 0:4].rearrange("p (c j) -> p c j", c=C), wf3.hi[:, :, D:D + 2])
                    dve.wait_ge(rows_in, 16 * N_ROWS)
                    nc.vector.tensor_tensor(add3[:], bank[:, 4:6], bqk3[:], ALU.add).then_inc(prep_lo, 1)
                else:
                    nc.vector.memset(count_only[:, n:n + 1], 0.0).then_inc(prep_lo, 1)
            for n, (name, s) in enumerate(NATURAL):
                dve.wait_ge(prep_hi, len(STEPS) + n + 1)
                lower(s.lo[:, :, 0:D], stage[name], s.hi[:, :, 0:D], SCALE_OF.get(name, 1.0)).then_inc(prep_lo, 1)
            dve.wait_ge(prep_hi, len(STEPS) + len(NATURAL) + 1)
            lower(wv2.lo[:, :, D:D + 2], wg2, wv2.hi[:, :, D:D + 2]).then_inc(prep_lo, 1)
            dve.wait_ge(prep_lo, len(STEPS) + len(NATURAL) + 1)
            dve.wait_ge(rows_in, 16 * N_ROWS)

            def shifted(l, g, bias):
                for h in range(H):
                    m, r = divmod(h, R)
                    j = g * H + h
                    ins = nc.vector.tensor_tensor_reduce(
                        out=E[l][:, g, h, :], in0=score_ps[:, g * C + m, r * P:(r + 1) * P],
                        in1=bias[:, g * P:(g + 1) * P], scale=-1.0, scalar=HUGE, op0=ALU.add, op1=ALU.min,
                        accum_out=NM[l][:, j:j + 1])
                    if h == R - 1:
                        ins.then_inc(t_first[l][g], 1)
                ins.then_inc(t_all[l][g], 1)

            def inverse(l, g):
                nc.vector.reciprocal(RS[l][:, g * H:(g + 1) * H], SUM[l][:, g * H:(g + 1) * H]).then_inc(rs_sb[l][g], 1)

            def biased_lo(s, bank, b_):
                for m in range(C):
                    ins = nc.vector.scalar_tensor_tensor(out=s.lo[:, m, :], in0=work[:, bank, m * G * P:(m + 1) * G * P],
                                                         scalar=b_[:, m:m + 1], in1=s.hi[:, m, :].bitcast(F32),
                                                         op0=ALU.add, op1=ALU.subtract)
                return ins

            def both(r_):
                return r_[:].unsqueeze(1).to_broadcast([P, G, D])

            def turn(t):
                if t.has(1):
                    t.apart()
                    t.wait_ge(s1_ps, t.now(1))
                    t.wait_ge(bias1_sb, t.now(1))
                    t.wait_ge(a1_sb, t.was(1))
                    for g in range(G):
                        ins = nc.vector.tensor_tensor_reduce(
                            out=E1[:, g * P:(g + 1) * P], in0=work[:, 1, g * P:(g + 1) * P],
                            in1=BIAS1[:, g * P:(g + 1) * P], scale=-1.0, scalar=HUGE, op0=ALU.add, op1=ALU.min,
                            accum_out=NM1[:, g:g + 1])
                    ins.then_inc(t1_all, 1)
                if t.has(3):
                    t.wait_ge(u3_sb, t.now(3))
                    t.wait_ge(exp3, t.was(3))
                    nc.vector.scalar_tensor_tensor(out=L3[:], in0=U3[:], scalar=0.01, in1=U3[:], op0=ALU.mult,
                                                   op1=ALU.max).then_inc(l3_sb, 1)
                    t.wait_ge(l3_sb, t.now(3))
                    nc.vector.tensor_reduce(NM3[:], L3[:].rearrange("p (g k) -> p g k", g=G), AX_X, ALU.max,
                                            negate=True).then_inc(nm3_sb, 1)
                if t.has(1):
                    t.wait_ge(exp1, t.now(1))
                    t.wait_ge(mask1_sb, t.now(1))
                    t.wait_ge(a1t_ps, t.was(1))
                    nc.vector.reciprocal(RS1[:], SUM1[:]).then_inc(rs1_sb, 1)
                    t.wait_ge(rs1_sb, t.now(1))
                    for g in range(G):
                        ins = nc.vector.scalar_tensor_tensor(
                            out=A1[:, g * P:(g + 1) * P], in0=E1[:, g * P:(g + 1) * P], scalar=RS1[:, g:g + 1],
                            in1=MASK1[:, g * P:(g + 1) * P], op0=ALU.mult, op1=ALU.mult)
                    ins.then_inc(a1_sb, 1)
                if t.has(2):
                    t.apart()
                    t.wait_ge(s_ps[2][0], t.now(2))
                    t.wait_ge(bias2_sb, t.now(2))
                    t.wait_ge(et_ps[2][0], t.was(2))
                    shifted(2, 0, BIAS2)
                if t.has(-1):
                    t.wait_ge(xt_hi[0], t.now(-1))
                    t.wait_ge(v0_ps, t.was(-1))
                    nc.vector.tensor_tensor(XT[0].lo[:], by_chunk(3), XT[0].hi[:].bitcast(F32),
                                            ALU.subtract).then_inc(xt_lo[0], 1)
                if t.has(0):
                    t.wait_ge(ot0_hi, t.now(0))
                    t.wait_ge(y_ps[0], t.was(0))
                    nc.vector.tensor_tensor(OT0.lo[:], by_chunk(1), OT0.hi[:].bitcast(F32),
                                            ALU.subtract).then_inc(ot0_lo, 1)
                if t.has(2):
                    t.apart()
                    t.wait_ge(s_ps[2][1], t.now(2))
                    t.wait_ge(t_all[2][0], t.now(2))
                    t.wait_ge(et_ps[2][1], t.was(2))
                    shifted(2, 1, BIAS2)
                if t.has(0):
                    t.wait_ge(y_ps[0], t.now(0))
                    t.wait_ge(x0b_sb, t.now(0))
                    t.wait_ge(x1_sb, t.was(0))
                    nc.vector.tensor_tensor(Y[0][:], by_graph(0), X0b[:], ALU.add).then_inc(y_sb[0], 1)
                if t.has(2):
                    t.wait_ge(exp_all[2][0], t.now(2))
                    inverse(2, 0)
                if t.has(0):
                    t.apart()
                    t.wait_ge(y_sb[0], t.now(0))
                    for g in range(G):
                        ins = nc.vector.bn_stats(STAT[0][:, g, :], Y[0][:, g, :])
                    ins.then_inc(stat_sb[0], 1)
                    t.apart()
                    t.wait_ge(stat_sb[0], t.now(0))
                    for g in range(G):
                        ins = nc.vector.bn_aggr(MV[0][:, g, :], STAT[0][:, g, :])
                    ins.then_inc(mv_sb[0], 1)
                if t.has(1):
                    t.wait_ge(ct1_ps, t.now(1))
                    t.wait_ge(y_ps[1], t.was(1))
                    nc.vector.tensor_copy(CT1.hi[:], by_chunk(3)).then_inc(ct1_hi, 1)
                if t.has(-1):
                    t.wait_ge(adj_in, t.now(-1), 16)
                    t.wait_ge(t_all[0][1], t.was(-1))
                    nc.vector.tensor_scalar(BIAS0[:], t.slot(-1), 1e-8, None, ALU.max).then_inc(clip0, 1)
                if t.has(1):
                    t.wait_ge(ct1_hi, t.now(1))
                    nc.vector.tensor_tensor(CT1.lo[:], by_chunk(3), CT1.hi[:].bitcast(F32),
                                            ALU.subtract).then_inc(ct1_lo, 1)
                if t.has(2):
                    t.wait_ge(exp_all[2][1], t.now(2))
                    inverse(2, 1)
                if t.has(0):
                    t.wait_ge(rstd_sb[0], t.now(0))
                    for g in range(G):
                        ins = nc.vector.tensor_scalar(Y[0][:, g, :], Y[0][:, g, :], MV[0][:, g, 0:1], RSTD[0][:, g:g + 1],
                                                      ALU.subtract, ALU.mult)
                    ins.then_inc(z_sb[0], 1)
                if t.has(-1):
                    t.wait_ge(k_hi[0], t.now(-1))
                    biased_lo(KT, 0, bk0).then_inc(k_lo[0], 1)
                if t.has(1):
                    t.wait_ge(y_ps[1], t.now(1))
                    t.wait_ge(x2_sb, t.was(1))
                    nc.vector.tensor_tensor(Y[1][:], by_graph(3), X1[:], ALU.add).then_inc(y_sb[1], 1)
                if t.has(3):
                    t.wait_ge(exp3, t.now(3))
                    t.wait_ge(out_sb, t.was(3))
                    nc.vector.reciprocal(RS3[:], SUM3[:]).then_inc(rs3_sb, 1)
                if t.has(1):
                    t.apart()
                    t.wait_ge(y_sb[1], t.now(1))
                    for g in range(G):
                        ins = nc.vector.bn_stats(STAT[1][:, g, :], Y[1][:, g, :])
                    ins.then_inc(stat_sb[1], 1)
                    t.apart()
                    t.wait_ge(stat_sb[1], t.now(1))
                    for g in range(G):
                        ins = nc.vector.bn_aggr(MV[1][:, g, :], STAT[1][:, g, :])
                    ins.then_inc(mv_sb[1], 1)
                if t.has(-1):
                    t.wait_ge(q_hi[0], t.now(-1))
                    biased_lo(QT[0], 1, bq0s).then_inc(q_lo[0], 1)
                if t.has(3):
                    t.wait_ge(o3_ps, t.now(3))
                    t.wait_ge(rs3_sb, t.now(3))
                    t.wait_ge(out_stored, t.was(3), 16)
                    for g in range(G):
                        ins = nc.vector.scalar_tensor_tensor(out=OUT[:, g, :], in0=work[:, 2, g * D:(g + 1) * D],
                                                             scalar=RS3[:, g:g + 1], in1=X3[:, g, :],
                                                             op0=ALU.mult, op1=ALU.add)
                    ins.then_inc(out_sb, 1)
                if t.has(1):
                    t.wait_ge(rstd_sb[1], t.now(1))
                    for g in range(G):
                        ins = nc.vector.tensor_scalar(Y[1][:, g, :], Y[1][:, g, :], MV[1][:, g, 0:1], RSTD[1][:, g:g + 1],
                                                      ALU.subtract, ALU.mult)
                    ins.then_inc(z_sb[1], 1)
                if t.has(0):
                    t.wait_ge(x1_sb, t.now(0))
                    t.wait_ge(bias1_sb, t.was(0))
                    for g in range(G):
                        ins = nc.vector.tensor_tensor_reduce(
                            out=U1junk[:, g, :], in0=X1[:, g, :], in1=wu1[:], scale=1.0, scalar=0.0, op0=ALU.mult,
                            op1=ALU.add, accum_out=U1[:, g:g + 1])
                    ins.then_inc(u1_sb, 1)
                if t.has(2):
                    t.wait_ge(o2_ps, t.now(2))
                    t.wait_ge(out_sb, t.was(2))
                    nc.vector.tensor_tensor(X3[:], by_graph(0), X2[:], ALU.add).then_inc(x3_sb, 1)
                if t.has(-1):
                    t.wait_ge(v0_ps, t.now(-1))
                    t.wait_ge(ot_ps[0][1], t.was(-1))
                    nc.vector.tensor_tensor(V[0][:], by_graph(3), both(row["bv0"]), ALU.add).then_inc(v0_sb, 1)
                    t.apart()
                    t.wait_ge(s_ps[0][0], t.now(-1))
                    t.wait_ge(bias0_sb, t.now(-1))
                    shifted(0, 0, BIAS0)
                if t.has(2):
                    t.wait_ge(xt_hi[3], t.now(2))
                    nc.vector.tensor_tensor(XT[3].lo[:], by_chunk(0), XT[3].hi[:].bitcast(F32),
                                            ALU.subtract).then_inc(xt_lo[3], 1)
                if t.has(1):
                    t.wait_ge(xt_hi[2], t.now(1))
                    t.wait_ge(q_ps[2], t.was(1))
                    nc.vector.tensor_tensor(XT[2].lo[:], by_chunk(1), XT[2].hi[:].bitcast(F32),
                                            ALU.subtract).then_inc(xt_lo[2], 1)
                if t.has(0):
                    t.wait_ge(x1t_sb, t.now(0))
                    t.wait_ge(g1_ps, t.was(0))
                    nc.vector.tensor_copy(XT[1].hi[:], X1T[:]).then_inc(xt_hi[1], 1)
                if t.has(-1):
                    t.apart()
                    t.wait_ge(s_ps[0][1], t.now(-1))
                    t.wait_ge(t_all[0][0], t.now(-1))
                    shifted(0, 1, BIAS0)
                if t.has(2):
                    t.wait_ge(f3_ps[0], t.now(2))
                    nc.vector.tensor_tensor(QK3[:, 0, :], work[:, 2, D:D + 2], add3[:], ALU.add)
                    nc.vector.tensor_tensor(F3[:, 0, :], work[:, 2, 0:D], row["bf3"][:], ALU.add).then_inc(f3_sb[0], 1)
                if t.has(1):
                    t.wait_ge(v2_ps[0], t.now(1))
                    t.wait_ge(ot_ps[2][0], t.was(1))
                    nc.vector.tensor_tensor(AC2[:, 0, :], work[:, 1, D:D + 2], bg2[:], ALU.add)
                    nc.vector.tensor_tensor(V[2][:, 0, :], work[:, 1, 0:D], row["bv2"][:], ALU.add).then_inc(v2_sb[0], 1)
                if t.has(0):
                    t.wait_ge(adj_in, t.now(0), 16)
                    t.wait_ge(t1_all, t.was(0))
                    nc.vector.tensor_scalar(BIAS1[:], t.slot(0), 0.0, MASKED, ALU.is_equal, ALU.mult).then_inc(nbias1_sb, 1)
                if t.has(-1):
                    t.wait_ge(exp_all[0][0], t.now(-1))
                    inverse(0, 0)
                if t.has(1):
                    t.wait_ge(k_hi[2], t.now(1))
                    biased_lo(KT, 0, bk2).then_inc(k_lo[2], 1)
                if t.has(2):
                    t.wait_ge(f3_ps[1], t.now(2))
                    nc.vector.tensor_tensor(QK3[:, 1, :], work[:, 2, D:D + 2], add3[:], ALU.add)
                    nc.vector.tensor_tensor(F3[:, 1, :], work[:, 2, 0:D], row["bf3"][:], ALU.add).then_inc(f3_sb[1], 1)
                if t.has(0):
                    t.wait_ge(nbias1_sb, t.now(0))
                    for g in range(G):
                        ins = nc.vector.tensor_scalar(BIAS1[:, g * P:(g + 1) * P], BIAS1[:, g * P:(g + 1) * P],
                                                      U1[:, g:g + 1], c0[:, 0:1], ALU.add, ALU.add)
                    ins.then_inc(bias1_sb, 1)
                if t.has(1):
                    t.wait_ge(v2_ps[1], t.now(1))
                    t.wait_ge(ot_ps[2][1], t.was(1))
                    nc.vector.tensor_tensor(AC2[:, 1, :], work[:, 3, D:D + 2], bg2[:], ALU.add)
                    nc.vector.tensor_tensor(V[2][:, 1, :], work[:, 3, 0:D], row["bv2"][:], ALU.add).then_inc(v2_sb[1], 1)
                if t.has(2):
                    t.wait_ge(k3_ps, t.now(2))
                    t.wait_ge(m3_sb, t.now(2))
                    for g in range(G):
                        ins = nc.vector.scalar_tensor_tensor(
                            out=U3[:, g * P:(g + 1) * P], in0=work[:, 2, g * P:(g + 1) * P], scalar=QK3[:, g, 0:1],
                            in1=M3[:, g * P:(g + 1) * P], op0=ALU.add, op1=ALU.add)
                    ins.then_inc(u3_sb, 1)
                if t.has(-1):
                    t.wait_ge(exp_all[0][1], t.now(-1))
                    inverse(0, 1)
                if t.has(0):
                    t.wait_ge(adj_in, t.now(0), 16)
                    t.wait_ge(a1_sb, t.was(0))
                    nc.vector.tensor_scalar(MASK1[:], t.slot(0), 0.0, None, ALU.not_equal).then_inc(mask1_sb, 1)
                if t.has(1):
                    t.wait_ge(c2_ps, t.now(1))
                    t.wait_ge(lnadj2_sb, t.now(1))
                    for g in range(G):
                        ins = nc.vector.scalar_tensor_tensor(
                            out=BIAS2[:, g * P:(g + 1) * P], in0=work[:, 2, g * P:(g + 1) * P], scalar=AC2[:, g, 0:1],
                            in1=LNADJ2[:, g * P:(g + 1) * P], op0=ALU.add, op1=ALU.add)
                    ins.then_inc(bias2_sb, 1)
                    t.apart()
                    t.wait_ge(adj_in, t.now(1), 16)
                    t.wait_ge(u3_sb, t.was(1))
                    nc.vector.tensor_scalar(M3[:], t.slot(1), 1.0, 1.0e9, ALU.subtract, ALU.mult).then_inc(m3_sb, 1)
                    t.wait_ge(q_hi[2], t.now(1))
                    biased_lo(QT[2], 0, bq2s).then_inc(q_lo[2], 1)

            run(dve, turn, multiples=((-3, 16), (0, 16), (1, 16), (2, 16),))

        @block.gpsimd
        def _(pool):
            nc.gpsimd.memset(ident[:], 0.0).then_inc(pool_const, 1)
            pool.wait_ge(pool_const, 1)
            nc.gpsimd.affine_select(out=ident[:], in_=ident[:], compare_op=ALU.not_equal, fill=1.0, base=0,
                                    pattern=[[-1, P]], channel_multiplier=1).then_inc(const_ready, 1)
            nc.gpsimd.memset(half[:], -0.5)
            for n in ROWS:
                pool.dma_start(row[n][:], w[n].rearrange("(a d) -> a d", a=1).to_broadcast([P, D])).then_inc(rows_in, 16)
            pool.dma_start(bg2[:, 0:1], w["b_g"].to_broadcast([P, 1])).then_inc(rows_in, 16)
            for n, j in (("q_b", 0), ("k_b", 1)):
                pool.dma_start(bqk3[:, j:j + 1], w[n].to_broadcast([P, 1])).then_inc(rows_in, 16)
            pool.wait_ge(rows_in, 16 * N_ROWS)

            def both(r_):
                return r_[:].unsqueeze(1).to_broadcast([P, G, D])

            def probs(l, g):
                nc.gpsimd.tensor_tensor(E[l][:, g], E[l][:, g],
                                        RS[l][:, g * H:(g + 1) * H].unsqueeze(2).to_broadcast([P, H, P]),
                                        ALU.mult).then_inc(prob[l][g], 1)

            def turn(t):
                if t.has(0):
                    t.wait_ge(z_sb[0], t.now(0))
                    nc.gpsimd.tensor_tensor(Y[0][:], Y[0][:], both(row["gamma0"]), ALU.mult).then_inc(zg_sb[0], 1)
                if t.has(1):
                    t.apart()
                    t.wait_ge(mv_sb[1], t.now(1))
                    t.wait_ge(z_sb[1], t.was(1))
                    nc.gpsimd.tensor_scalar(VE[1][:], MV[1][:, :, 1], LN_EPS, None, ALU.add).then_inc(ve_sb[1], 1)
                    t.wait_ge(ve_sb[1], t.now(1))
                    nc.gpsimd.tensor_tensor(RSTD[1][:], VE[1][:], half[:], ALU.pow).then_inc(rstd_sb[1], 1)
                if t.has(0):
                    t.wait_ge(zg_sb[0], t.now(0))
                    t.wait_ge(y_sb[1], t.was(0))
                    nc.gpsimd.tensor_tensor(X1[:], Y[0][:], both(row["beta0"]), ALU.add).then_inc(x1_sb, 1)
                if t.has(1):
                    t.wait_ge(z_sb[1], t.now(1))
                    nc.gpsimd.tensor_tensor(Y[1][:], Y[1][:], both(row["gamma1"]), ALU.mult).then_inc(zg_sb[1], 1)
                    t.wait_ge(zg_sb[1], t.now(1))
                    t.wait_ge(x3_sb, t.was(1))
                    nc.gpsimd.tensor_tensor(X2[:], Y[1][:], both(row["beta1"]), ALU.add).then_inc(x2_sb, 1)
                if t.has(0):
                    t.wait_ge(xt_hi[1], t.now(0))
                    nc.gpsimd.tensor_tensor(XT[1].lo[:], X1T[:], XT[1].hi[:].bitcast(F32), ALU.subtract).then_inc(xt_lo[1], 1)
                if t.has(-1):
                    t.wait_ge(x_in, t.now(-1), 16)
                    t.wait_ge(y_sb[0], t.was(-1))
                    nc.gpsimd.tensor_tensor(X0b[:], X0[:], both(row["bo0"]), ALU.add).then_inc(x0b_sb, 1)
                    t.wait_ge(rs_sb[0][0], t.now(-1))
                    probs(0, 0)
                    t.wait_ge(rs_sb[0][1], t.now(-1))
                    probs(0, 1)
                if t.has(1):
                    t.wait_ge(rs_sb[2][0], t.now(1))
                    probs(2, 0)
                if t.has(-1):
                    t.apart()
                    t.wait_ge(mv_sb[0], t.now(-1))
                    t.wait_ge(z_sb[0], t.was(-1))
                    nc.gpsimd.tensor_scalar(VE[0][:], MV[0][:, :, 1], LN_EPS, None, ALU.add).then_inc(ve_sb[0], 1)
                    t.wait_ge(ve_sb[0], t.now(-1))
                    nc.gpsimd.tensor_tensor(RSTD[0][:], VE[0][:], half[:], ALU.pow).then_inc(rstd_sb[0], 1)
                if t.has(1):
                    t.wait_ge(rs_sb[2][1], t.now(1))
                    probs(2, 1)

            run(pool, turn, multiples=((2, 16),))


_INS = {
    "x": "x", "adj": "adj",
    "Wq0": "L0_gnn_Wq", "bq0": "L0_gnn_bq", "Wk0": "L0_gnn_Wk", "bk0": "L0_gnn_bk", "Wv0": "L0_gnn_Wv",
    "bv0": "L0_gnn_bv", "Wo0": "L0_gnn_Wo", "bo0": "L0_gnn_bo", "gamma0": "L0_gnn_gamma", "beta0": "L0_gnn_beta",
    "Wq1": "L1_gnn_Wq", "bq1": "L1_gnn_bq", "Wk1": "L1_gnn_Wk", "bk1": "L1_gnn_bk", "Wc1": "L1_gnn_Wc",
    "gamma1": "L1_gnn_gamma", "beta1": "L1_gnn_beta",
    "Wq2": "L2_gnn_W_q", "bq2": "L2_gnn_b_q", "Wk2": "L2_gnn_W_k", "bk2": "L2_gnn_b_k", "Wv2": "L2_gnn_W_v",
    "bv2": "L2_gnn_b_v", "w_g": "L2_gnn_w_g", "b_g": "L2_gnn_b_g",
    "fc3": "L3_gnn_fc_w", "bf3": "L3_gnn_fc_b", "q_w": "L3_gnn_q_w", "q_b": "L3_gnn_q_b",
    "k_w": "L3_gnn_k_w", "k_b": "L3_gnn_k_b",
}


def kernel(**inputs):
    import numpy as np
    import concourse.bacc as bacc
    from concourse.bass_utils import run_bass_kernel_spmd

    nc = bacc.Bacc("TRN2", target_bir_lowering=False, num_devices=1)
    arrays, aps = {}, {}
    for short, name in _INS.items():
        a = np.ascontiguousarray(inputs[name])
        if a.ndim == 0:
            a = a.reshape(1)
        arrays[f"in_{short}"] = a
        aps[short] = nc.dram_tensor(f"in_{short}", a.shape, mybir.dt.from_np(a.dtype), kind="ExternalInput").ap()
    out = nc.dram_tensor("out_0", aps["x"].shape, F32, kind="ExternalOutput").ap()
    build(nc, aps["x"], aps["adj"], aps, out)
    r = run_bass_kernel_spmd(nc, [arrays], core_ids=[0])
    return r.results[0]["out_0"]
```
